# Optimizing a Trainium2 kernel written in Bass

```python
import numpy as np
import jax
import jax.numpy as jnp

def _softmax(x, axis=-1):
    return jax.nn.softmax(x, axis=axis)

def _gelu(x):
    return jax.nn.gelu(x, approximate=True)

def _silu(x):
    return jax.nn.silu(x)

def _sigmoid(x):
    return jax.nn.sigmoid(x)

def _layernorm(x, axis=-1, eps=1e-05):
    m = jnp.mean(x, axis=axis, keepdims=True)
    v = jnp.var(x, axis=axis, keepdims=True)
    return (x - m) / jnp.sqrt(v + eps)

def _scatter_add(tgt, idx, src, axis=0):
    return tgt.at[idx].add(src)

def _segment_sum(src, seg, n):
    return jax.ops.segment_sum(src, seg, n)
kernel_name = 'mk_seq_preln_d4_jaxref_r8_d32b67'

def setup_inputs(seed: int=0):
    np.random.seed(seed)
    _w = jnp.asarray

    def _L0_attn_setup():
        import jax, jax.numpy as jnp
        import numpy as np
        EMBED_DIM = 128
        NUM_HEADS = 16
        HEAD_DIM = EMBED_DIM // NUM_HEADS
        ALPHA = 1.0

        def _power_law_mask(seq_len, dtype):
            pos = jnp.arange(seq_len)
            delta = pos[None, :] - pos[:, None]
            log_d = jnp.log(jnp.maximum(delta, 0).astype(jnp.float32) + 1.0)
            mask = jnp.where(delta > 0, (-ALPHA * log_d).astype(dtype), jnp.zeros((), dtype))
            mask = jnp.where(delta < 0, jnp.asarray(-jnp.inf, dtype), mask)
            return mask
        key = jax.random.key(seed)
        k1, k2, k3 = jax.random.split(key, 3)
        B, S, D = (2, 256, EMBED_DIM)
        hidden_states = jax.random.normal(k1, (B, S, D), dtype=jnp.float32)
        w_attn = jax.random.normal(k2, (D, 3 * D), dtype=jnp.float32) * D ** (-0.5)
        b_attn = jnp.zeros((3 * D,), dtype=jnp.float32)
        w_proj = jax.random.normal(k3, (D, D), dtype=jnp.float32) * D ** (-0.5)
        b_proj = jnp.zeros((D,), dtype=jnp.float32)
        return {'hidden_states': hidden_states, 'w_attn': w_attn, 'b_attn': b_attn, 'w_proj': w_proj, 'b_proj': b_proj}
    _L0_attn_in = _L0_attn_setup()

    def _L0_ffn_setup():
        import jax, jax.numpy as jnp
        import numpy as np
        DIM = 128
        HIDDEN = 384
        SCALE = 1.0 / 127.0

        def _dequant(w_int, dtype):
            return w_int.astype(dtype) * jnp.asarray(SCALE, dtype)
        key = jax.random.key(seed)
        k_x, k_g, k_u, k_d = jax.random.split(key, 4)
        x = jax.random.normal(k_x, (4, 256, DIM), dtype=jnp.float32)
        w_gate = jax.random.randint(k_g, (HIDDEN, DIM), -127, 128, dtype=jnp.int32)
        w_up = jax.random.randint(k_u, (HIDDEN, DIM), -127, 128, dtype=jnp.int32)
        w_down = jax.random.randint(k_d, (DIM, HIDDEN), -127, 128, dtype=jnp.int32)
        return {'x': x, 'w_gate': w_gate, 'w_up': w_up, 'w_down': w_down}
    _L0_ffn_in = _L0_ffn_setup()

    def _L1_attn_setup():
        import jax, jax.numpy as jnp
        import numpy as np
        HEADS = 16
        D_MODEL = 128
        D_K = D_MODEL // HEADS
        SEQ = 256
        BSZ = 2
        BASE = 10000.0

        def _rope(x):
            s = x.shape[0]
            d = x.shape[-1]
            ar = jnp.arange(0, d, 2, dtype=jnp.float32)
            theta = 1.0 / (jnp.power(BASE, ar) / d)
            pos = jnp.arange(s, dtype=jnp.float32)
            idx_theta = pos[:, None] * theta[None, :]
            idx2 = jnp.concatenate([idx_theta, idx_theta], -1)
            cos = jnp.cos(idx2)[:, None, None, :]
            sin = jnp.sin(idx2)[:, None, None, :]
            neg_x = jnp.concatenate([-x[..., d // 2:], x[..., :d // 2]], axis=-1)
            return x * cos + neg_x * sin

        def _softmax_one(x, axis):
            x = x - jnp.max(x, axis=axis, keepdims=True)
            e = jnp.exp(x)
            return e / (1.0 + jnp.sum(e, axis=axis, keepdims=True))
        key = jax.random.key(seed)
        ks = jax.random.split(key, 7)
        sc = 1.0 / np.sqrt(D_MODEL)
        return {'x': jax.random.normal(ks[0], (SEQ, BSZ, D_MODEL), jnp.float32), 'Wq': jax.random.normal(ks[1], (D_MODEL, D_MODEL), jnp.float32) * sc, 'bq': jnp.zeros((D_MODEL,), jnp.float32), 'Wk': jax.random.normal(ks[2], (D_MODEL, D_MODEL), jnp.float32) * sc, 'bk': jnp.zeros((D_MODEL,), jnp.float32), 'Wv': jax.random.normal(ks[3], (D_MODEL, D_MODEL), jnp.float32) * sc, 'bv': jnp.zeros((D_MODEL,), jnp.float32)}
    _L1_attn_in = _L1_attn_setup()

    def _L1_ffn_setup():
        import jax, jax.numpy as jnp
        import numpy as np
        B, S, D = (8, 512, 128)
        E, R, K = (6, 16, 2)
        key = jax.random.key(seed)
        ks = jax.random.split(key, 9)
        sc = 0.02
        return {'x': jax.random.normal(ks[0], (B, S, D), jnp.float32), 'base_W': jax.random.normal(ks[1], (D, D), jnp.float32) * sc, 'base_b': jax.random.normal(ks[2], (D,), jnp.float32) * sc, 'shared_A': jax.random.normal(ks[3], (R, D), jnp.float32) * sc, 'shared_B': jax.random.normal(ks[4], (D, R), jnp.float32) * sc, 'routed_A': jax.random.normal(ks[5], (E, R, D), jnp.float32) * sc, 'routed_B': jax.random.normal(ks[6], (E, D, R), jnp.float32) * sc, 'router_W': jax.random.normal(ks[7], (E, D), jnp.float32) * sc, 'router_b': jax.random.normal(ks[8], (E,), jnp.float32) * sc}
    _L1_ffn_in = _L1_ffn_setup()

    def _L2_attn_setup():
        import jax, jax.numpy as jnp
        import numpy as np
        EPS = 1e-06
        NUM_HEADS = 16

        def _phi(x):
            return jax.nn.elu(x) + 1.0
        key = jax.random.key(seed)
        ks = jax.random.split(key, 5)
        B, S, D = (2, 256, 128)
        scale = 1.0 / np.sqrt(D)
        return {'x': jax.random.normal(ks[0], (B, S, D), dtype=jnp.float32), 'Wq': jax.random.normal(ks[1], (D, D), dtype=jnp.float32) * scale, 'bq': jnp.zeros((D,), dtype=jnp.float32), 'Wk': jax.random.normal(ks[2], (D, D), dtype=jnp.float32) * scale, 'bk': jnp.zeros((D,), dtype=jnp.float32), 'Wv': jax.random.normal(ks[3], (D, D), dtype=jnp.float32) * scale, 'bv': jnp.zeros((D,), dtype=jnp.float32), 'Wo': jax.random.normal(ks[4], (D, D), dtype=jnp.float32) * scale, 'bo': jnp.zeros((D,), dtype=jnp.float32)}
    _L2_attn_in = _L2_attn_setup()

    def _L2_ffn_setup():
        import jax, jax.numpy as jnp
        import numpy as np
        E, K, D = (8, 2, 128)
        B, S = (2, 512)

        def _layernorm(x, g, b, eps=1e-06):
            m = jnp.mean(x, axis=-1, keepdims=True)
            v = jnp.var(x, axis=-1, keepdims=True)
            return (x - m) * jax.lax.rsqrt(v + eps) * g + b
        key = jax.random.key(seed)
        ks = jax.random.split(key, 6)
        n = lambda k, shape, scale: jax.random.normal(k, shape, jnp.float32) * scale
        return {'x': n(ks[0], (B, S, D), 1.0), 'gate_w': n(ks[1], (D, E), 0.02), 'w1': n(ks[2], (E, D, 2 * D), 0.02), 'b1': jnp.zeros((E, 2 * D), jnp.float32), 'w2': n(ks[3], (E, 2 * D, D), 0.02), 'b2': jnp.zeros((E, D), jnp.float32), 'ln_g': jnp.ones((E, D), jnp.float32), 'ln_b': jnp.zeros((E, D), jnp.float32)}
    _L2_ffn_in = _L2_ffn_setup()

    def _L3_attn_setup():
        import jax, jax.numpy as jnp
        import numpy as np
        import math
        B, N, DIM = (4, 512, 128)
        HEADS, DHEAD, NRF = (16, 64, 64)
        STAB = 1e-06

        def _phi(t, RF):
            return jax.nn.relu(jnp.einsum('bhnd,hdr->bhnr', t, RF))
        key = jax.random.key(seed)
        k1, k2, k3, k4 = jax.random.split(key, 4)
        x = jax.random.normal(k1, (B, N, DIM), dtype=jnp.float32)
        W_qkv = jax.random.normal(k2, (DIM, 3 * HEADS * DHEAD), dtype=jnp.float32) * (1.0 / math.sqrt(DIM))
        RF = jax.random.normal(k3, (HEADS, DHEAD, NRF), dtype=jnp.float32) / math.sqrt(NRF)
        W_out = jax.random.normal(k4, (HEADS * DHEAD, DIM), dtype=jnp.float32) * (1.0 / math.sqrt(HEADS * DHEAD))
        b_out = jnp.zeros((DIM,), dtype=jnp.float32)
        return {'x': x, 'W_qkv': W_qkv, 'RF': RF, 'W_out': W_out, 'b_out': b_out}
    _L3_attn_in = _L3_attn_setup()

    def _L3_ffn_setup():
        import jax, jax.numpy as jnp
        import numpy as np
        JITTER_EPS = 0.01

        def phi_routing(logits, jitter_eps=JITTER_EPS):
            m, sel = jax.lax.top_k(logits, 2)
            T, E = logits.shape
            m1 = m[:, :1]
            factor1 = jnp.maximum(jnp.abs(logits), m1)
            mask1 = (m1 - logits) / factor1 > 2.0 * jitter_eps
            p1 = jax.nn.softmax(jnp.where(mask1, -jnp.inf, logits), axis=-1)
            mult1 = jnp.take_along_axis(p1, sel[:, :1], axis=-1)
            m2 = m[:, 1:2]
            factor2 = jnp.maximum(jnp.abs(logits), m2)
            mask2 = (m2 - logits) / factor2 > 2.0 * jitter_eps
            drop_top1 = jnp.arange(E)[None, :] == sel[:, :1]
            p2 = jax.nn.softmax(jnp.where(mask2 | drop_top1, -jnp.inf, logits), axis=-1)
            mult2 = jnp.take_along_axis(p2, sel[:, 1:2], axis=-1)
            return (jnp.concatenate([mult1, mult2], axis=-1), sel)
        key = jax.random.key(seed)
        k = jax.random.split(key, 5)
        B, S, H, F, E = (1, 64, 128, 512, 8)
        return {'hidden_states': jax.random.normal(k[0], (B, S, H), jnp.float32), 'gate_w': jax.random.normal(k[1], (E, H), jnp.float32) * 0.02, 'w1': jax.random.normal(k[2], (E, F, H), jnp.float32) * 0.02, 'w2': jax.random.normal(k[3], (E, H, F), jnp.float32) * 0.02, 'w3': jax.random.normal(k[4], (E, F, H), jnp.float32) * 0.02}
    _L3_ffn_in = _L3_ffn_setup()
    _d = {'L0_attn_hidden_states': _L0_attn_in['hidden_states'], 'L0_attn_w_attn': _L0_attn_in['w_attn'], 'L0_attn_b_attn': _L0_attn_in['b_attn'], 'L0_attn_w_proj': _L0_attn_in['w_proj'], 'L0_attn_b_proj': _L0_attn_in['b_proj'], 'L0_ffn_w_gate': _L0_ffn_in['w_gate'], 'L0_ffn_w_up': _L0_ffn_in['w_up'], 'L0_ffn_w_down': _L0_ffn_in['w_down'], 'L1_attn_Wq': _L1_attn_in['Wq'], 'L1_attn_bq': _L1_attn_in['bq'], 'L1_attn_Wk': _L1_attn_in['Wk'], 'L1_attn_bk': _L1_attn_in['bk'], 'L1_attn_Wv': _L1_attn_in['Wv'], 'L1_attn_bv': _L1_attn_in['bv'], 'L1_ffn_base_W': _L1_ffn_in['base_W'], 'L1_ffn_base_b': _L1_ffn_in['base_b'], 'L1_ffn_shared_A': _L1_ffn_in['shared_A'], 'L1_ffn_shared_B': _L1_ffn_in['shared_B'], 'L1_ffn_routed_A': _L1_ffn_in['routed_A'], 'L1_ffn_routed_B': _L1_ffn_in['routed_B'], 'L1_ffn_router_W': _L1_ffn_in['router_W'], 'L1_ffn_router_b': _L1_ffn_in['router_b'], 'L2_attn_Wq': _L2_attn_in['Wq'], 'L2_attn_bq': _L2_attn_in['bq'], 'L2_attn_Wk': _L2_attn_in['Wk'], 'L2_attn_bk': _L2_attn_in['bk'], 'L2_attn_Wv': _L2_attn_in['Wv'], 'L2_attn_bv': _L2_attn_in['bv'], 'L2_attn_Wo': _L2_attn_in['Wo'], 'L2_attn_bo': _L2_attn_in['bo'], 'L2_ffn_gate_w': _L2_ffn_in['gate_w'], 'L2_ffn_w1': _L2_ffn_in['w1'], 'L2_ffn_b1': _L2_ffn_in['b1'], 'L2_ffn_w2': _L2_ffn_in['w2'], 'L2_ffn_b2': _L2_ffn_in['b2'], 'L2_ffn_ln_g': _L2_ffn_in['ln_g'], 'L2_ffn_ln_b': _L2_ffn_in['ln_b'], 'L3_attn_W_qkv': _L3_attn_in['W_qkv'], 'L3_attn_RF': _L3_attn_in['RF'], 'L3_attn_W_out': _L3_attn_in['W_out'], 'L3_attn_b_out': _L3_attn_in['b_out'], 'L3_ffn_gate_w': _L3_ffn_in['gate_w'], 'L3_ffn_w1': _L3_ffn_in['w1'], 'L3_ffn_w2': _L3_ffn_in['w2'], 'L3_ffn_w3': _L3_ffn_in['w3']}
    _x0 = _d['L0_attn_hidden_states']
    _d['L0_attn_hidden_states'] = jax.random.normal(jax.random.fold_in(jax.random.key(seed), 1), (2, 1024, 128), dtype=_x0.dtype)
    del _x0
    return _d

def reference(L0_attn_hidden_states, L0_attn_w_attn, L0_attn_b_attn, L0_attn_w_proj, L0_attn_b_proj, L0_ffn_w_gate, L0_ffn_w_up, L0_ffn_w_down, L1_attn_Wq, L1_attn_bq, L1_attn_Wk, L1_attn_bk, L1_attn_Wv, L1_attn_bv, L1_ffn_base_W, L1_ffn_base_b, L1_ffn_shared_A, L1_ffn_shared_B, L1_ffn_routed_A, L1_ffn_routed_B, L1_ffn_router_W, L1_ffn_router_b, L2_attn_Wq, L2_attn_bq, L2_attn_Wk, L2_attn_bk, L2_attn_Wv, L2_attn_bv, L2_attn_Wo, L2_attn_bo, L2_ffn_gate_w, L2_ffn_w1, L2_ffn_b1, L2_ffn_w2, L2_ffn_b2, L2_ffn_ln_g, L2_ffn_ln_b, L3_attn_W_qkv, L3_attn_RF, L3_attn_W_out, L3_attn_b_out, L3_ffn_gate_w, L3_ffn_w1, L3_ffn_w2, L3_ffn_w3):

    def _L0_attn_ref(hidden_states, w_attn, b_attn, w_proj, b_proj):
        import jax, jax.numpy as jnp
        import numpy as np
        EMBED_DIM = 128
        NUM_HEADS = 16
        HEAD_DIM = EMBED_DIM // NUM_HEADS
        ALPHA = 1.0

        def _power_law_mask(seq_len, dtype):
            pos = jnp.arange(seq_len)
            delta = pos[None, :] - pos[:, None]
            log_d = jnp.log(jnp.maximum(delta, 0).astype(jnp.float32) + 1.0)
            mask = jnp.where(delta > 0, (-ALPHA * log_d).astype(dtype), jnp.zeros((), dtype))
            mask = jnp.where(delta < 0, jnp.asarray(-jnp.inf, dtype), mask)
            return mask
        B, S, D = hidden_states.shape
        H, hd = (NUM_HEADS, HEAD_DIM)
        scaling = hd ** (-0.5)
        qkv = hidden_states @ w_attn + b_attn
        q, k, v = jnp.split(qkv, 3, axis=-1)
        q = q.reshape(B, S, H, hd).transpose(0, 2, 1, 3)
        k = k.reshape(B, S, H, hd).transpose(0, 2, 1, 3)
        v = v.reshape(B, S, H, hd).transpose(0, 2, 1, 3)
        scores = jnp.einsum('bhqd,bhkd->bhqk', q, k) * scaling
        scores = scores + _power_law_mask(S, scores.dtype)[None, None]
        attn = jax.nn.softmax(scores, axis=-1)
        out = jnp.einsum('bhqk,bhkd->bhqd', attn, v)
        out = out.transpose(0, 2, 1, 3).reshape(B, S, D)
        out = out @ w_proj + b_proj
        return out

    def _L0_ffn_ref(x, w_gate, w_up, w_down):
        import jax, jax.numpy as jnp
        import numpy as np
        DIM = 128
        HIDDEN = 384
        SCALE = 1.0 / 127.0

        def _dequant(w_int, dtype):
            return w_int.astype(dtype) * jnp.asarray(SCALE, dtype)
        wg = _dequant(w_gate, x.dtype)
        wu = _dequant(w_up, x.dtype)
        wd = _dequant(w_down, x.dtype)
        gate = jnp.einsum('bsd,hd->bsh', x, wg)
        up = jnp.einsum('bsd,hd->bsh', x, wu)
        h = jax.nn.silu(gate) * up
        return jnp.einsum('bsh,dh->bsd', h, wd)

    def _L1_attn_ref(x, Wq, bq, Wk, bk, Wv, bv):
        import jax, jax.numpy as jnp
        import numpy as np
        HEADS = 16
        D_MODEL = 128
        D_K = D_MODEL // HEADS
        SEQ = 256
        BSZ = 2
        BASE = 10000.0

        def _rope(x):
            s = x.shape[0]
            d = x.shape[-1]
            ar = jnp.arange(0, d, 2, dtype=jnp.float32)
            theta = 1.0 / (jnp.power(BASE, ar) / d)
            pos = jnp.arange(s, dtype=jnp.float32)
            idx_theta = pos[:, None] * theta[None, :]
            idx2 = jnp.concatenate([idx_theta, idx_theta], -1)
            cos = jnp.cos(idx2)[:, None, None, :]
            sin = jnp.sin(idx2)[:, None, None, :]
            neg_x = jnp.concatenate([-x[..., d // 2:], x[..., :d // 2]], axis=-1)
            return x * cos + neg_x * sin

        def _softmax_one(x, axis):
            x = x - jnp.max(x, axis=axis, keepdims=True)
            e = jnp.exp(x)
            return e / (1.0 + jnp.sum(e, axis=axis, keepdims=True))
        s, b, dm = x.shape
        q = (x @ Wq.T + bq).reshape(s, b, HEADS, D_K)
        k = (x @ Wk.T + bk).reshape(s, b, HEADS, D_K)
        v = (x @ Wv.T + bv).reshape(s, b, HEADS, D_K)
        q = _rope(q)
        k = _rope(k)
        scores = jnp.einsum('ibhd,jbhd->ijbh', q, k) / np.sqrt(D_K)
        mask = jnp.tril(jnp.ones((s, s), dtype=bool))[:, :, None, None]
        scores = jnp.where(mask, scores, -jnp.inf)
        attn = _softmax_one(scores, axis=1)
        out = jnp.einsum('ijbh,jbhd->ibhd', attn, v)
        return out.reshape(s, b, dm)

    def _L1_ffn_ref(x, base_W, base_b, shared_A, shared_B, routed_A, routed_B, router_W, router_b):
        import jax, jax.numpy as jnp
        import numpy as np
        B, S, D = (8, 512, 128)
        E, R, K = (6, 16, 2)
        base_out = jax.lax.stop_gradient(jnp.einsum('bsi,oi->bso', x, base_W) + base_b)
        shared_out = jnp.einsum('bsr,or->bso', jnp.einsum('bsi,ri->bsr', x, shared_A), shared_B)
        logits = jnp.einsum('bsi,ei->bse', x, router_W) + router_b
        gate = jax.nn.softmax(logits, axis=-1)
        topk_w, topk_i = jax.lax.top_k(gate, K)
        sparse_w = jnp.sum(jax.nn.one_hot(topk_i, E, dtype=gate.dtype) * topk_w[..., None], axis=-2)
        sparse_w = sparse_w / (jnp.sum(sparse_w, axis=-1, keepdims=True) + 1e-06)
        h = jnp.einsum('bsi,eri->bser', x, routed_A)
        routed_outs = jnp.einsum('bser,eor->bseo', h, routed_B)
        routed_out = jnp.einsum('bseo,bse->bso', routed_outs, sparse_w)
        return base_out + shared_out + routed_out

    def _L2_attn_ref(x, Wq, bq, Wk, bk, Wv, bv, Wo, bo):
        import jax, jax.numpy as jnp
        import numpy as np
        EPS = 1e-06
        NUM_HEADS = 16

        def _phi(x):
            return jax.nn.elu(x) + 1.0
        B, S, D = x.shape
        H = NUM_HEADS
        hd = D // H
        q = (x @ Wq.T + bq).reshape(B, S, H, hd).transpose(0, 2, 1, 3)
        k = (x @ Wk.T + bk).reshape(B, S, H, hd).transpose(0, 2, 1, 3)
        v = (x @ Wv.T + bv).reshape(B, S, H, hd).transpose(0, 2, 1, 3)
        q = _phi(q)
        k = _phi(k)
        kv_cum = jnp.cumsum(k[..., :, None] * v[..., None, :], axis=2)
        k_cum = jnp.cumsum(k, axis=2)
        num = jnp.einsum('bhsd,bhsde->bhse', q, kv_cum)
        den = jnp.einsum('bhsd,bhsd->bhs', q, k_cum)
        out = num / (den[..., None] + EPS)
        out = out.transpose(0, 2, 1, 3).reshape(B, S, D)
        return out @ Wo.T + bo

    def _L2_ffn_ref(x, gate_w, w1, b1, w2, b2, ln_g, ln_b):
        import jax, jax.numpy as jnp
        import numpy as np
        E, K, D = (8, 2, 128)
        B, S = (2, 512)

        def _layernorm(x, g, b, eps=1e-06):
            m = jnp.mean(x, axis=-1, keepdims=True)
            v = jnp.var(x, axis=-1, keepdims=True)
            return (x - m) * jax.lax.rsqrt(v + eps) * g + b
        orig_shape = x.shape
        xt = x.reshape(-1, orig_shape[-1])
        scores = xt @ gate_w
        ew, ei = jax.lax.top_k(scores, K)
        ew = jax.nn.softmax(ew, axis=-1)
        mask = ei[None, :, :] == jnp.arange(E)[:, None, None]
        wE = jnp.sum(ew[None, :, :] * mask, axis=-1)
        h = jax.nn.gelu(jnp.einsum('td,edf->etf', xt, w1) + b1[:, None, :], approximate=False)
        o = jnp.einsum('etf,efd->etd', h, w2) + b2[:, None, :]
        y = _layernorm(xt[None, :, :] + o, ln_g[:, None, :], ln_b[:, None, :])
        out = jnp.einsum('et,etd->td', wE, y)
        return out.reshape(orig_shape)

    def _L3_attn_ref(x, W_qkv, RF, W_out, b_out):
        import jax, jax.numpy as jnp
        import numpy as np
        import math
        B, N, DIM = (4, 512, 128)
        HEADS, DHEAD, NRF = (16, 64, 64)
        STAB = 1e-06

        def _phi(t, RF):
            return jax.nn.relu(jnp.einsum('bhnd,hdr->bhnr', t, RF))
        b, n, _ = x.shape
        qkv = x @ W_qkv
        q, k, v = jnp.split(qkv, 3, axis=-1)

        def to_heads(t):
            return t.reshape(b, n, HEADS, DHEAD).transpose(0, 2, 1, 3)
        q, k, v = (to_heads(q), to_heads(k), to_heads(v))
        phi_q = _phi(q, RF)
        phi_k = _phi(k, RF)
        kv = jnp.einsum('bhnr,bhnd->bhrd', phi_k, v)
        out = jnp.einsum('bhnr,bhrd->bhnd', phi_q, kv)
        k_sum = phi_k.sum(axis=2)
        normalizer = jnp.einsum('bhnr,bhr->bhn', phi_q, k_sum)[..., None] + STAB
        out = out / normalizer
        out = out.transpose(0, 2, 1, 3).reshape(b, n, HEADS * DHEAD)
        out = out @ W_out + b_out
        return out

    def _L3_ffn_ref(hidden_states, gate_w, w1, w2, w3):
        import jax, jax.numpy as jnp
        import numpy as np
        JITTER_EPS = 0.01

        def phi_routing(logits, jitter_eps=JITTER_EPS):
            m, sel = jax.lax.top_k(logits, 2)
            T, E = logits.shape
            m1 = m[:, :1]
            factor1 = jnp.maximum(jnp.abs(logits), m1)
            mask1 = (m1 - logits) / factor1 > 2.0 * jitter_eps
            p1 = jax.nn.softmax(jnp.where(mask1, -jnp.inf, logits), axis=-1)
            mult1 = jnp.take_along_axis(p1, sel[:, :1], axis=-1)
            m2 = m[:, 1:2]
            factor2 = jnp.maximum(jnp.abs(logits), m2)
            mask2 = (m2 - logits) / factor2 > 2.0 * jitter_eps
            drop_top1 = jnp.arange(E)[None, :] == sel[:, :1]
            p2 = jax.nn.softmax(jnp.where(mask2 | drop_top1, -jnp.inf, logits), axis=-1)
            mult2 = jnp.take_along_axis(p2, sel[:, 1:2], axis=-1)
            return (jnp.concatenate([mult1, mult2], axis=-1), sel)
        B, S, H = hidden_states.shape
        E = w1.shape[0]
        x = hidden_states.reshape(-1, H)
        logits = x @ gate_w.T
        routing_weights, selected = phi_routing(logits)
        T = x.shape[0]
        wte = jnp.zeros((T, E), x.dtype).at[jnp.arange(T)[:, None], selected].add(routing_weights)
        out = jnp.zeros_like(x)
        for e in range(E):
            h = jax.nn.silu(x @ w1[e].T) * (x @ w3[e].T)
            out = out + wte[:, e:e + 1] * (h @ w2[e].T)
        return out.reshape(B, S, H)
    x = L0_attn_hidden_states
    x = x + _L0_attn_ref(_layernorm(x, axis=-1), L0_attn_w_attn, L0_attn_b_attn, L0_attn_w_proj, L0_attn_b_proj)
    x = x + _L0_ffn_ref(_layernorm(x, axis=-1), L0_ffn_w_gate, L0_ffn_w_up, L0_ffn_w_down)
    x = x + _L1_attn_ref(_layernorm(x, axis=-1), L1_attn_Wq, L1_attn_bq, L1_attn_Wk, L1_attn_bk, L1_attn_Wv, L1_attn_bv)
    x = x + _L1_ffn_ref(_layernorm(x, axis=-1), L1_ffn_base_W, L1_ffn_base_b, L1_ffn_shared_A, L1_ffn_shared_B, L1_ffn_routed_A, L1_ffn_routed_B, L1_ffn_router_W, L1_ffn_router_b)
    x = x + _L2_attn_ref(_layernorm(x, axis=-1), L2_attn_Wq, L2_attn_bq, L2_attn_Wk, L2_attn_bk, L2_attn_Wv, L2_attn_bv, L2_attn_Wo, L2_attn_bo)
    x = x + _L2_ffn_ref(_layernorm(x, axis=-1), L2_ffn_gate_w, L2_ffn_w1, L2_ffn_b1, L2_ffn_w2, L2_ffn_b2, L2_ffn_ln_g, L2_ffn_ln_b)
    x = x + _L3_attn_ref(_layernorm(x, axis=-1), L3_attn_W_qkv, L3_attn_RF, L3_attn_W_out, L3_attn_b_out)
    x = x + _L3_ffn_ref(_layernorm(x, axis=-1), L3_ffn_gate_w, L3_ffn_w1, L3_ffn_w2, L3_ffn_w3)
    return x

_drawn_inputs = setup_inputs


def setup_inputs(seed=0):
    import zlib

    import numpy as np

    out = dict(_drawn_inputs(seed))
    spreads = {'L0_attn_b_attn': (0.0, 0.1),
     'L0_attn_b_proj': (0.0, 0.1),
     'L1_attn_bq': (0.0, 2.0),
     'L1_attn_bk': (0.0, 2.0),
     'L1_attn_bv': (0.0, 2.0),
     'L2_attn_bq': (0.0, 2.0),
     'L2_attn_bk': (0.0, 2.0),
     'L2_attn_bv': (0.0, 2.0),
     'L2_attn_bo': (0.0, 2.0),
     'L2_ffn_b1': (0.0, 2.0),
     'L2_ffn_b2': (0.0, 2.0),
     'L2_ffn_ln_g': (1.0, 0.6),
     'L2_ffn_ln_b': (0.0, 2.0),
     'L3_attn_b_out': (0.0, 2.0)}
    factors = {'L1_attn_Wq': 64.0,
     'L1_attn_Wk': 64.0,
     'L1_attn_Wv': 37.086,
     'L1_ffn_base_W': 64.0,
     'L1_ffn_base_b': 64.0,
     'L1_ffn_shared_A': 64.0,
     'L1_ffn_shared_B': 64.0,
     'L1_ffn_routed_A': 64.0,
     'L1_ffn_routed_B': 64.0,
     'L1_ffn_router_W': 64.0,
     'L1_ffn_router_b': 64.0,
     'L2_attn_Wq': 30.844,
     'L2_attn_Wk': 24.758,
     'L2_attn_Wv': 8.0,
     'L2_attn_Wo': 8.0,
     'L2_ffn_gate_w': 64.0,
     'L2_ffn_w1': 64.0,
     'L2_ffn_w2': 64.0,
     'L3_attn_W_qkv': 8.0,
     'L3_attn_RF': 64.0,
     'L3_attn_W_out': 8.0,
     'L3_ffn_gate_w': 8.0,
     'L3_ffn_w1': 8.0,
     'L3_ffn_w2': 8.0,
     'L3_ffn_w3': 8.0}
    for name, (base, spread) in spreads.items():
        noise = np.random.default_rng([zlib.crc32(name.encode()), seed]).standard_normal(out[name].shape)
        drawn = base * np.exp(spread * noise) if base else spread * noise
        out[name] = jnp.asarray(drawn.astype(out[name].dtype))
    for name, factor in factors.items():
        out[name] = (out[name] * factor).astype(out[name].dtype)
    return out
```

```python
from contextlib import ExitStack

import numpy as np

import concourse.bass as bass
from concourse import mybir

F32 = mybir.dt.float32
BF16 = mybir.dt.bfloat16
I32 = mybir.dt.int32
ALU = mybir.AluOpType
ACT = mybir.ActivationFunctionType
AX = mybir.AxisListType

P = 128
B, S, D = 2, 1024, 128
T = B * S
NT = T // P
CH = 512
NC = T // CH
TPC = CH // P
LN_EPS = 1e-5


class Part:

    def __init__(self, ready, tensor=None, vector=None, scalar=None, gpsimd=None, sync=None,
                 before_norm=None, bias=None):
        self.ready, self.before_norm, self.bias = ready, before_norm or {}, bias
        self.tensor, self.vector, self.scalar, self.gpsimd, self.sync = tensor, vector, scalar, gpsimd, sync


class Norm:

    def __init__(self, nc, m, k, before, biased, counted):
        self.nc, self.m, self.k, self.before, self.biased, self.counted = nc, m, k, before, biased, counted

    def value(self, c):
        return NC * self.k + c + 1

    def biased_value(self, c):
        return NC * self.biased + c + 1

    def done(self, c):
        return NC * self.counted + c + 1

    def vector(self, dve):
        nc, m = self.nc, self.m

        def statistics(c):
            dve.wait_ge(*self.before.ready[c])
            for t in range(c * TPC, (c + 1) * TPC):
                last = nc.vector.bn_stats(m.stats[:, t, :], m.x[:, t, :])
            last.then_inc(m.ln_stats, 1)
            dve.wait_ge(m.ln_stats, self.value(c))
            for t in range(c * TPC, (c + 1) * TPC):
                last = nc.vector.bn_aggr(m.meanvar[:, t, :], m.stats[:, t, :])
            last.then_inc(m.ln_var, 1)

        def normalise(c):
            dve.wait_ge(m.ln_rstd, 2 * self.value(c))
            for t in range(c * TPC, (c + 1) * TPC):
                last = nc.vector.tensor_scalar(m.xn[:, t, :], m.x[:, t, :], m.meanvar[:, t, 0:1],
                                               m.rstd[:, t:t + 1], ALU.subtract, ALU.mult)
            last.then_inc(m.ln_xn, 1)

        statistics(0)
        for c in range(NC):
            if c + 1 < NC:
                statistics(c + 1)
            normalise(c)

    def gpsimd(self, pool, bias):
        nc, m = self.nc, self.m
        if self.k == 0:
            pool.wait_ge(m.set_up, 2)
        for c in range(NC):
            ts = slice(c * TPC, (c + 1) * TPC)
            pool.wait_ge(m.ln_var, self.value(c))
            nc.gpsimd.tensor_scalar(m.vareps[:, ts], m.meanvar[:, ts, 1], LN_EPS, None, ALU.add).then_inc(m.ln_rstd, 1)
            pool.wait_ge(m.ln_rstd, 2 * self.value(c) - 1)
            nc.gpsimd.tensor_tensor(m.rstd[:, ts], m.vareps[:, ts], m.power[:, ts], ALU.pow).then_inc(m.ln_rstd, 1)
        if bias is not None:
            for c in range(NC):
                xs = m.x[:, c * TPC:(c + 1) * TPC, :]
                pool.wait_ge(m.ln_xn, self.value(c))
                nc.gpsimd.tensor_tensor(xs, xs, bias.unsqueeze(1).broadcast_to([P, TPC, D]), ALU.add).then_inc(m.biased, 1)

    def tensor(self, pe):
        nc, m = self.nc, self.m
        if self.k == 0:
            pe.wait_ge(m.set_up, 2)
            pe.wait_ge(m.consts_in, 16 * (2 + len(BIASES)))
        for c in range(NC):
            pe.wait_ge(m.ln_xn, self.value(c))
            if c >= 2:
                pe.wait_ge(m.ln_xnT, self.value(c - 2))
            for j in range(TPC):
                last = nc.tensor.transpose(m.ps[:, 6 + c % 2, j * P:(j + 1) * P], m.xn[:, c * TPC + j, :], m.ident[:, :])
            last.then_inc(m.ln_turned, 1)

    def scalar(self, act):
        nc, m = self.nc, self.m
        for c in range(NC):
            act.wait_ge(m.ln_turned, self.value(c))
            nc.scalar.activation(m.xnT[:, c * CH:(c + 1) * CH], m.ps[:, 6 + c % 2, :], ACT.Copy).then_inc(m.ln_xnT, 1)


def l0_attn(nc, m, A, sem, sb, norm):
    H, HD, PAD, GH = 16, 8, 32, 4
    G = H // GH
    UNITS = B * G
    TB = S // P
    QC = S // CH
    SLOTS_Q, SLOTS_K = (0, 0, 1, 1, 0, 2), (0, 1, 0, 1, 2, 0)
    ROWS = 16 * len(SLOTS_Q)
    SCALE = HD ** -0.5
    BUFS, RING, LAG, SETTLE = 3, 6, 4, 8
    w = sb("l0a_w", [P, 3, D])
    wo = sb("l0a_wo", [P, D])
    bqk = sb("l0a_bqk", [P, 2])
    bv = sb("l0a_bv", [P, D])
    weight = sb("l0a_weight", [P, S])
    identb = sb("l0a_identb", [P, P], BF16)
    before = sb("l0a_before", [P, 2, P], BF16)
    rest = sb("l0a_rest", [P, 2, CH])
    parts = sb("l0a_parts", [P, 3, 2, T], BF16)
    vpad = sb("l0a_vpad", [P, NT, H, PAD])
    qs = sb("l0a_qs", [P, BUFS, 2, S], BF16)
    ks = sb("l0a_ks", [P, BUFS, GH, S], BF16)
    negmax = sb("l0a_negmax", [P, 2, GH, TB])
    nrest = sb("l0a_nrest", [P, GH, TB])
    nparts = sb("l0a_nparts", [P, 2, TB, GH * 3], BF16)
    mrows = sb("l0a_mrows", [GH * 3, 2, S], BF16)
    pe_ = sb("l0a_probs", [P, RING, CH])
    numT = sb("l0a_numT", [P, 2, CH])
    rec = sb("l0a_rec", [P, 2, TPC * GH])
    o = m.xn
    oT = numT[:, 0, :]

    w_in, zeroed, tails_in = sem("l0a_w_in"), sem("l0a_zeroed"), sem("l0a_tails_in")
    p_mm, high_set, rest_set, mid_set, low_set = (sem(f"l0a_{n}") for n in ("p_mm", "high_set", "rest_set", "mid_set", "low_set"))
    v_mm, v_set = sem("l0a_v_mm"), sem("l0a_v_set")
    stack_in = [sem(f"l0a_stack_in{n}") for n in range(BUFS)]
    mrows_in = [sem(f"l0a_mrows_in{n}") for n in range(BUFS)]
    a_mm, max_set, nsplit, nparts_set, n_turned, mrows_set = (sem(f"l0a_{n}") for n in ("a_mm", "max_set", "nsplit", "nparts_set", "n_turned", "mrows_set"))
    s_mm, exps, weighed_v, weighed_p = (sem(f"l0a_{n}") for n in ("s_mm", "exps", "weighed_v", "weighed_p"))
    pv_mm, num_out, num_turned, rec_set, o_set = (sem(f"l0a_{n}") for n in ("pv_mm", "num_out", "num_turned", "rec_set", "o_set"))
    o_turned, oT_set, y_mm = (sem(f"l0a_{n}") for n in ("o_turned", "oT_set", "y_mm"))
    x_done = m.x_done

    TILES = [(h, i) for i in range(TB) for h in range(GH)]
    STEPS = [(qc, kt, h) for qc in range(QC) for kt in range(TB - 1, TPC * qc - 1, -1) for h in range(GH)]
    NS = len(STEPS)
    LAST = [max(n for n, s in enumerate(STEPS) if s[0] == qc) for qc in range(QC)]

    def width(qc, kt):
        return min(CH, P * (kt + 1) - CH * qc)

    def by_pool(n):
        return n % 3 != 0

    def count_v(u, n):
        return u * sum(not by_pool(x) for x in range(NS)) + sum(not by_pool(x) for x in range(n + 1))

    def count_p(u, n):
        return u * NS + n + 1 - count_v(u, n)

    def wait_weighed(eng, u, n):
        if by_pool(n):
            eng.wait_ge(weighed_p, count_p(u, n))
        else:
            eng.wait_ge(weighed_v, count_v(u, n))

    def schedule():
        yield from (("max", 0, n) for n in range(len(TILES)))
        yield from ((what, 0, 0) for what in ("split", "turn_max", "take_max"))
        due = {}
        for u in range(UNITS):
            for n in range(NS):
                at = u * NS + n
                due.setdefault(at, []).insert(0, ("exp", u, n))
                if u + 1 < UNITS:
                    share = [min(len(TILES), len(TILES) * x // (NS - SETTLE)) for x in (n, n + 1)]
                    due[at] += [("max", u + 1, x) for x in range(*share)]
                    due[at] += [(what, u + 1, 0) for late, what in enumerate(("split", "turn_max", "take_max")) if n == NS - SETTLE + late]
                for what, late in (("weigh", 1), ("times_v", LAG)):
                    due.setdefault(at + late, []).append((what, u, n))
                if n in LAST:
                    for what, late in (("take_num", LAG), ("turn_num", LAG + 3), ("divide", LAG + 4)):
                        due.setdefault(at + late, []).append((what, u, LAST.index(n)))
        for at in sorted(due):
            yield from due[at]

    def sync(sp):
        sp.dma_start(w[:, :, :], A["L0_attn_w"]).then_inc(w_in, 16)
        sp.dma_start(wo[:, :], A["L0_attn_wo"]).then_inc(w_in, 16)
        sp.dma_start(bqk[:, :], A["L0_attn_bqk"]).then_inc(w_in, 16)
        sp.dma_start(bv[:, :], A["L0_attn_bv"].broadcast_to([P, D])).then_inc(w_in, 16)
        sp.dma_start(weight[:, :], A["L0_attn_weight"]).then_inc(w_in, 16)
        sp.dma_start(identb[:, :], A["L0_attn_ident"]).then_inc(w_in, 16)
        sp.dma_start(before[:, :, :], A["L0_attn_before"]).then_inc(w_in, 16)
        sp.wait_ge(zeroed, 3)
        for buf in range(BUFS):
            for h in range(GH):
                sp.dma_start(ks[ROWS:P, buf, h, :], A["L0_attn_ones"][h % 2]).then_inc(tails_in, 16)

        def stack(u):
            b, g = divmod(u, G)
            if u < BUFS:
                for c in range(QC * b, QC * (b + 1)):
                    sp.wait_ge(low_set, 2 * (c + 1))
            if u == BUFS or u == G:
                sp.wait_ge(low_set, 2 * NC)
            if u >= BUFS:
                sp.wait_ge(s_mm, NS * (u - BUFS + 1))
            ts = slice(b * S, (b + 1) * S)
            for pair in range(2):
                row = 16 * (2 * g + pair)
                for slot in range(len(SLOTS_Q)):
                    sp.dma_start(qs[16 * slot:16 * slot + 16, u % BUFS, pair, :], parts[row:row + 16, SLOTS_Q[slot], 0, ts]).then_inc(stack_in[u % BUFS], 16)
                    for h in range(2):
                        at = 16 * slot + HD * h
                        sp.dma_start(ks[at:at + HD, u % BUFS, 2 * pair + h, :], parts[row + HD * h:row + HD * (h + 1), SLOTS_K[slot], 1, ts]).then_inc(stack_in[u % BUFS], 16)

        def maxima(u):
            sp.wait_ge(mrows_set, u + 1)
            for pair in range(2):
                sp.dma_start(qs[ROWS:ROWS + 6, u % BUFS, pair, :], mrows[6 * pair:6 * pair + 6, u % 2, :]).then_inc(mrows_in[u % BUFS], 16)

        stack(0)
        stack(1)
        for u in range(UNITS):
            maxima(u)
            if u + 2 < UNITS:
                stack(u + 2)

    STACK = 16 * 18 * 2

    def clear(pool):
        nc.gpsimd.memset(vpad[:, :, :, :], 0.0).then_inc(zeroed, 1)
        nc.gpsimd.memset(ks[:, :, :, :], 0.0).then_inc(zeroed, 1)
        nc.gpsimd.memset(qs[:, :, :, :], 0.0).then_inc(zeroed, 1)
        pool.wait_ge(zeroed, 3)
        nc.gpsimd.memset(vpad[:, :, :, HD:HD + 1], 1.0).then_inc(zeroed, 1)

    def weigh(eng, engine, u, n, done):
        qc, kt, h = STEPS[n]
        i = (u * NS + n) % RING
        k = width(qc, kt)
        at = CH * qc - P * kt + S - P
        eng.wait_ge(exps, u * NS + n + 1)
        engine.tensor_tensor(pe_[:, i, 0:k], pe_[:, i, 0:k], weight[:, at:at + k], ALU.mult).then_inc(done, 1)

    def gpsimd(pool):
        pool.wait_ge(w_in, 16 * 7)
        for u in range(UNITS):
            for n in range(NS):
                if by_pool(n):
                    weigh(pool, nc.gpsimd, u, n, weighed_p)

    def tensor(pe):
        pe.wait_ge(w_in, 16 * 7)
        for c in range(NC):
            pe.wait_ge(m.ln_xnT, norm.value(c))
            for j in range(2):
                n = 2 * c + j
                if n >= 4:
                    pe.wait_ge(rest_set, n - 3)
                nc.tensor.matmul(m.ps[:, n % 4, :], w[:, j, :], m.xnT[:, c * CH:(c + 1) * CH], start=True, stop=True).then_inc(p_mm, 1)
            if c:
                pe.wait_ge(v_set, c)
            for t in range(c * TPC, (c + 1) * TPC):
                mm = nc.tensor.matmul(m.ps[:, 4, t % TPC * P:(t % TPC + 1) * P], m.xnT[:, t * P:(t + 1) * P], w[:, 2, :], start=True, stop=True)
            mm.then_inc(v_mm, 1)
        pe.wait_ge(rest_set, 2 * NC)
        pe.wait_ge(v_set, NC)
        pe.wait_ge(tails_in, 16 * BUFS * GH)

        def scores_by_query(u, n):
            h, i = TILES[n]
            k = u * len(TILES) + n
            if n == 0:
                pe.wait_ge(stack_in[u % BUFS], STACK * (u // BUFS + 1))
            if k >= 2:
                pe.wait_ge(max_set, k - 1)
            bank = 2 * (k % 2)
            q = qs[0:ROWS, u % BUFS, h // 2, i * P:(i + 1) * P]
            for j in range(0, S - i * P, CH):
                width_ = min(CH, S - i * P - j)
                mm = nc.tensor.matmul(m.ps[:, bank + j // CH, 0:width_], q, ks[0:ROWS, u % BUFS, h, i * P + j:i * P + j + width_],
                                      start=True, stop=(j > 0), skip_group_check=True)
                if j == 0:
                    mm = nc.tensor.matmul(m.ps[:, bank, 0:P], identb[:, :], before[:, 0, :], start=False, stop=True, skip_group_check=True)
            mm.then_inc(a_mm, 1)

        def turn_maxima(u, _):
            pe.wait_ge(nparts_set, u + 1)
            if u:
                pe.wait_ge(o_set, 2 * u - 1)
            for i in range(TB):
                mm = nc.tensor.transpose(m.ps7b[0:GH * 3, i * P:(i + 1) * P], nparts[:, u % 2, i, :], identb[:, :])
            mm.then_inc(n_turned, 1)

        def scores_by_key(u, n):
            qc, kt, h = STEPS[n]
            k = u * NS + n
            if n == 0:
                pe.wait_ge(mrows_in[u % BUFS], 32 * (u // BUFS + 1))
            if k >= 2:
                pe.wait_ge(exps, k - 1)
            wd = width(qc, kt)
            diagonal = kt // TPC == qc
            out = m.ps[:, 4 + k % 2, 0:wd]
            mm = nc.tensor.matmul(out, ks[:, u % BUFS, h, kt * P:(kt + 1) * P], qs[:, u % BUFS, h // 2, CH * qc:CH * qc + wd],
                                  start=True, stop=not diagonal, skip_group_check=True)
            if diagonal:
                mm = nc.tensor.matmul(m.ps[:, 4 + k % 2, wd - P:wd], identb[:, :], before[:, 1, :], start=False, stop=True, skip_group_check=True)
            mm.then_inc(s_mm, 1)

        def times_v(u, n):
            b = u // G
            qc, kt, h = STEPS[n]
            i = (u * NS + n) % RING
            wd = width(qc, kt)
            wait_weighed(pe, u, n)
            if kt == TB - 1 and h == 0 and u * QC + qc:
                pe.wait_ge(num_out, u * QC + qc)
            mm = nc.tensor.matmul(m.ps[PAD * h:PAD * (h + 1), 6, 0:wd], vpad[:, b * TB + kt, u % G * GH + h, :], pe_[:, i, 0:wd],
                                  start=(kt == TB - 1), stop=(n >= LAST[qc] - GH + 1), skip_group_check=True)
            mm.then_inc(pv_mm, 1)

        def turn_numerators(u, qc):
            k = u * QC + qc
            pe.wait_ge(num_out, k + 1)
            if k:
                pe.wait_ge(o_set, k)
            pe.wait_ge(mrows_set, min(UNITS, u + 1 + qc))
            for j in range(TPC):
                mm = nc.tensor.transpose(m.ps[:, 7, j * P:(j + 1) * P], numT[:, k % 2, j * P:(j + 1) * P], m.ident[:, :])
            mm.then_inc(num_turned, 1)

        do = {"max": scores_by_query, "turn_max": turn_maxima, "exp": scores_by_key, "times_v": times_v, "turn_num": turn_numerators}
        for what, u, n in schedule():
            if what in do:
                do[what](u, n)
        pe.wait_ge(max_set, len(TILES) * UNITS)
        for c in range(NC):
            pe.wait_ge(o_set, min(UNITS * QC, (c // QC + 1) * G * QC))
            for j in range(TPC):
                mm = nc.tensor.transpose(m.ps[:, c, j * P:(j + 1) * P], o[:, c * TPC + j, :], m.ident[:, :])
            mm.then_inc(o_turned, 1)
        for c in range(NC):
            pe.wait_ge(oT_set, c + 1)
            for j in range(TPC):
                mm = nc.tensor.matmul(m.ps[:, c, j * P:(j + 1) * P], oT[:, j * P:(j + 1) * P], wo[:, :], start=True, stop=True)
            mm.then_inc(y_mm, 1)

    def scalar(act):
        for n in range(2 * NC):
            cs = slice(n // 2 * CH, (n // 2 + 1) * CH)
            act.wait_ge(p_mm, n + 1)
            nc.scalar.activation(parts[:, 0, n % 2, cs], m.ps[:, n % 4, :], ACT.Identity, bias=bqk[:, n % 2:n % 2 + 1]).then_inc(high_set, 1)
            act.wait_ge(rest_set, n + 1)
            nc.scalar.activation(parts[:, 1, n % 2, cs], rest[:, n % 2, :], ACT.Copy).then_inc(mid_set, 1)

        def exp(u, n):
            qc, kt, h = STEPS[n]
            k = u * NS + n
            wd = width(qc, kt)
            act.wait_ge(s_mm, k + 1)
            if k >= RING:
                act.wait_ge(pv_mm, k - RING + 1)
            nc.scalar.activation(pe_[:, k % RING, 0:wd], m.ps[:, 4 + k % 2, 0:wd], ACT.Exp, scale=SCALE).then_inc(exps, 1)

        def take_numerators(u, qc):
            k = u * QC + qc
            act.wait_ge(pv_mm, u * NS + LAST[qc] + 1)
            if k >= 2:
                act.wait_ge(num_turned, k - 1)
            nc.scalar.activation(numT[:, k % 2, :], m.ps[:, 6, :], ACT.Copy).then_inc(num_out, 1)

        def take_maxima(u, _):
            act.wait_ge(n_turned, u + 1)
            nc.scalar.activation(mrows[:, u % 2, :], m.ps7b[0:GH * 3, :], ACT.Copy).then_inc(mrows_set, 1)

        do = {"exp": exp, "take_num": take_numerators, "take_max": take_maxima}
        for what, u, n in schedule():
            if what in do:
                do[what](u, n)
        for c in range(NC):
            act.wait_ge(o_turned, c + 1)
            if c:
                act.wait_ge(y_mm, c)
            nc.scalar.activation(oT, m.ps[:, c, :], ACT.Copy).then_inc(oT_set, 1)

    def vector(dve):
        for n in range(2 * NC):
            c = n // 2
            cs = slice(c * CH, (c + 1) * CH)
            dve.wait_ge(high_set, n + 1)
            if n >= 2:
                dve.wait_ge(low_set, n - 1)
            nc.vector.scalar_tensor_tensor(out=rest[:, n % 2, :], in0=m.ps[:, n % 4, :], scalar=bqk[:, n % 2:n % 2 + 1],
                                           in1=parts[:, 0, n % 2, cs], op0=ALU.add, op1=ALU.subtract).then_inc(rest_set, 1)
            if n % 2:
                dve.wait_ge(v_mm, c + 1)
                dve.wait_ge(zeroed, 4)
                nc.vector.tensor_tensor(vpad[:, c * TPC:(c + 1) * TPC, :, 0:HD], m.ps[:, 4, :].rearrange("p (t h e) -> p t h e", h=H, e=HD),
                                        bv[:, :].rearrange("p (h e) -> p h e", e=HD).unsqueeze(1).broadcast_to([P, TPC, H, HD]), ALU.add).then_inc(v_set, 1)
            dve.wait_ge(mid_set, n + 1)
            nc.vector.tensor_tensor(parts[:, 2, n % 2, cs], rest[:, n % 2, :], parts[:, 1, n % 2, cs], ALU.subtract).then_inc(low_set, 1)

        def maximum(u, n):
            h, i = TILES[n]
            k = u * len(TILES) + n
            dve.wait_ge(a_mm, k + 1)
            bank = 2 * (k % 2)
            nc.vector.tensor_reduce(negmax[:, u % 2, h, i:i + 1], m.psf[:, bank * CH:bank * CH + S - i * P], AX.X, ALU.max,
                                    negate=True).then_inc(max_set, 1)

        def split_maxima(u, _):
            dve.wait_ge(max_set, len(TILES) * (u + 1))
            mine = negmax[:, u % 2, :, :]
            part = lambda p: nparts[:, u % 2, :, :].rearrange("q i (h p) -> q h i p", p=3)[:, :, :, p]
            if u >= 2:
                dve.wait_ge(n_turned, u - 1)
            nc.vector.tensor_copy(part(0), mine).then_inc(nsplit, 1)
            dve.wait_ge(nsplit, 3 * u + 1)
            nc.vector.tensor_tensor(nrest[:, :, :], mine, part(0), ALU.subtract).then_inc(nsplit, 1)
            dve.wait_ge(nsplit, 3 * u + 2)
            nc.vector.tensor_copy(part(1), nrest[:, :, :]).then_inc(nsplit, 1)
            dve.wait_ge(nsplit, 3 * u + 3)
            nc.vector.tensor_tensor(part(2), nrest[:, :, :], part(1), ALU.subtract).then_inc(nparts_set, 1)

        def divide(u, qc):
            k = u * QC + qc
            b, g = divmod(u, G)
            dve.wait_ge(num_turned, k + 1)
            turned = m.ps[:, 7, :].rearrange("p (t h e) -> p t h e", h=GH, e=PAD)
            r = rec[:, k % 2, :].rearrange("p (t h) -> p t h", h=GH)
            nc.vector.reciprocal(r, turned[:, :, :, HD]).then_inc(rec_set, 1)
            dve.wait_ge(rec_set, k + 1)
            t0 = b * TB + qc * TPC
            nc.vector.tensor_tensor(o[:, t0:t0 + TPC, g * GH * HD:(g + 1) * GH * HD].rearrange("p t (h e) -> p t h e", e=HD),
                                    turned[:, :, :, 0:HD], r.unsqueeze(3).broadcast_to([P, TPC, GH, HD]), ALU.mult).then_inc(o_set, 1)

        def weigh_mine(u, n):
            if not by_pool(n):
                weigh(dve, nc.vector, u, n, weighed_v)

        do = {"max": maximum, "split": split_maxima, "weigh": weigh_mine, "divide": divide}
        for what, u, n in schedule():
            if what in do:
                do[what](u, n)
        for c in range(NC):
            dve.wait_ge(y_mm, c + 1)
            dve.wait_ge(m.biased, norm.biased_value(c))
            xs = m.x[:, c * TPC:(c + 1) * TPC, :]
            nc.vector.tensor_tensor(xs, m.ps[:, c, :].rearrange("p (j d) -> p j d", d=D), xs, ALU.add).then_inc(x_done, 1)

    return Part([(x_done, norm.done(c)) for c in range(NC)], tensor=tensor, vector=vector, scalar=scalar, gpsimd=gpsimd, sync=sync,
                before_norm={"gpsimd": clear}, bias="L0_attn_b_proj")


def l0_ffn(nc, m, A, sem, sb, norm):
    F = 384
    FT = F // P
    SCALE = 1.0 / 127.0
    wi = sb("l0f_wi", [P, 3, F], I32)
    w = sb("l0f_w", [P, 3, F])
    sg = sb("l0f_sg", [P, 2, CH])
    hT = sb("l0f_hT", [P, 2, FT, CH])
    w_in = sem("l0f_w_in")
    w_scaled = sem("l0f_w_scaled")
    gate_done, up_done = sem("l0f_gate_done"), sem("l0f_up_done")
    sg_done, h_done = sem("l0f_sg_done"), sem("l0f_h_done")
    down_done, x_done = sem("l0f_down_done"), m.x_done

    def sync(sp):
        sp.dma_start(wi[:, :, :], A["L0_ffn_w"]).then_inc(w_in, 16)

    def dequantise(dve):
        dve.wait_ge(w_in, 16)
        nc.vector.tensor_scalar(w[:, :, :], wi[:, :, :], SCALE, None, ALU.mult).then_inc(w_scaled, 1)

    def tensor(pe):
        def gates(c):
            pe.wait_ge(m.ln_xnT, norm.value(c))
            for f in range(FT):
                s = c * FT + f
                if s >= 2:
                    pe.wait_ge(h_done, s - 1)
                for half, done in ((0, gate_done), (1, up_done)):
                    nc.tensor.matmul(m.ps[:, 2 * (s % 2) + half, :], w[:, half, f * P:(f + 1) * P], m.xnT[:, c * CH:(c + 1) * CH],
                                     start=True, stop=True).then_inc(done, 1)

        def down(c):
            if c >= 2:
                pe.wait_ge(x_done, norm.done(c - 2))
            for f in range(FT):
                pe.wait_ge(h_done, c * FT + f + 1)
                for j in range(TPC):
                    mm = nc.tensor.matmul(m.ps[:, 4 + c % 2, j * P:(j + 1) * P], hT[:, c % 2, f, j * P:(j + 1) * P],
                                          w[:, 2, f * P:(f + 1) * P], start=(f == 0 and j == 0), stop=(f == FT - 1), skip_group_check=True)
            mm.then_inc(down_done, 1)

        pe.wait_ge(w_scaled, 1)
        for c in range(NC):
            gates(c)
            if c:
                down(c - 1)
        down(NC - 1)

    def scalar(act):
        for s in range(NC * FT):
            act.wait_ge(gate_done, s + 1)
            nc.scalar.activation(sg[:, s % 2, :], m.ps[:, 2 * (s % 2), :], ACT.Silu).then_inc(sg_done, 1)

    def vector(dve):
        def add(c):
            dve.wait_ge(down_done, c + 1)
            xs = m.x[:, c * TPC:(c + 1) * TPC, :]
            nc.vector.tensor_tensor(xs, m.ps[:, 4 + c % 2, :].rearrange("p (j d) -> p j d", d=D), xs, ALU.add).then_inc(x_done, 1)

        for c in range(NC):
            for f in range(FT):
                s = c * FT + f
                dve.wait_ge(up_done, s + 1)
                dve.wait_ge(sg_done, s + 1)
                nc.vector.tensor_tensor(hT[:, c % 2, f, :], m.ps[:, 2 * (s % 2) + 1, :], sg[:, s % 2, :], ALU.mult).then_inc(h_done, 1)
            if c:
                add(c - 1)
        add(NC - 1)

    return Part([(x_done, norm.done(c)) for c in range(NC)], tensor=tensor, vector=vector, scalar=scalar, sync=sync,
                before_norm={"vector": dequantise})


def l1_attn(nc, m, A, sem, sb, norm):
    H, HD = 16, 8
    HB = NT // 2
    SCALE = HD ** -0.5
    wqk = sb("l1a_wqk", [P, 2, D])
    rope = sb("l1a_rope", [P, P])
    w = sb("l1a_w", [P, 5, D])
    bcol = sb("l1a_bcol", [P, 2])
    bwide = sb("l1a_bwide", [P, 2, P])
    bias = sb("l1a_bias", [P, 5, D])
    kv0 = sb("l1a_kv0", [P, HB, 2, D])
    qkv1 = sb("l1a_qkv1", [P, HB, 3, D])
    prod = sb("l1a_prod", [P, 2, TPC * D])
    sc = sb("l1a_sc", [P, 2, TPC * H])
    mx, tot = sb("l1a_mx", [P, TPC * H]), sb("l1a_tot", [P, TPC * H])
    ex = sb("l1a_ex", [P, 2, TPC * H])

    w_in = sem("l1a_w_in")
    widened, rot_mm, rot_set = sem("l1a_widened"), sem("l1a_rot_mm"), sem("l1a_rot_set")
    mm_done = sem("l1a_mm_done")
    taken = sem("l1a_taken")
    step, exps, x_done = sem("l1a_step"), sem("l1a_exps"), sem("l1a_x_done")

    ORDER = [t for half in range(2) for pos in range(2) for t in range(pos * HB + half * TPC, pos * HB + half * TPC + TPC)]

    def sync(sp):
        sp.dma_start(wqk[:, :, :], A["L1_attn_wqk"]).then_inc(w_in, 16)
        sp.dma_start(rope[:, :], A["L1_attn_rope"]).then_inc(w_in, 16)
        sp.dma_start(w[:, 0:2, :], A["L1_attn_wkvT"]).then_inc(w_in, 16)
        sp.dma_start(w[:, 4, :], A["L1_attn_wkvT"][:, 1, :]).then_inc(w_in, 16)
        sp.dma_start(bcol[:, :], A["L1_attn_bcol"]).then_inc(w_in, 16)
        sp.dma_start(bias[:, 0, :], A["L1_attn_bkv"][0:1, :].broadcast_to([P, D])).then_inc(w_in, 16)
        sp.dma_start(bias[:, 1, :], A["L1_attn_bkv"][1:2, :].broadcast_to([P, D])).then_inc(w_in, 16)
        sp.dma_start(bias[:, 4, :], A["L1_attn_bkv"][1:2, :].broadcast_to([P, D])).then_inc(w_in, 16)

    def widen(dve):
        dve.wait_ge(w_in, 16 * 8)
        for j in range(2):
            ins = nc.vector.tensor_copy(bwide[:, j, :], bcol[:, j:j + 1].broadcast_to([P, P]))
        ins.then_inc(widened, 1)

    def rotate(pe):
        pe.wait_ge(w_in, 16 * 8)
        pe.wait_ge(widened, 1)
        for j in range(2):
            nc.tensor.matmul(m.ps[:, 0, j * P:(j + 1) * P], wqk[:, j, :], rope[:, :], start=True, stop=True)
            mm = nc.tensor.matmul(m.ps[:, 0, (2 + j) * P:(3 + j) * P], bwide[:, j, :], rope[:, :], start=True, stop=True)
        mm.then_inc(rot_mm, 1)

    def take_rotated(act):
        act.wait_ge(rot_mm, 1)
        nc.scalar.activation(w[:, 2:4, :].rearrange("p a b -> p (a b)"), m.ps[:, 0, 0:2 * P], ACT.Copy)
        nc.scalar.activation(bias[:, 2:4, :].rearrange("p a b -> p (a b)"), m.ps[:, 0, 2 * P:4 * P], ACT.Copy).then_inc(rot_set, 1)

    def tensor(pe):
        pe.wait_ge(rot_set, 1)
        for n, t in enumerate(ORDER):
            pe.wait_ge(m.ln_xnT, norm.value(t // TPC))
            if n >= 4:
                pe.wait_ge(taken, n - 3)
            cols = w[:, 0:2, :] if t < HB else w[:, 2:5, :]
            width = 2 * D if t < HB else 3 * D
            nc.tensor.matmul(m.ps[:, n % 4, 0:width], m.xnT[:, t * P:(t + 1) * P], cols, start=True, stop=True).then_inc(mm_done, 1)

    def scalar(act):
        for half in range(2):
            act.wait_ge(step, STEPS * half + 4)
            nc.scalar.activation(ex[:, :, :], sc[:, :, :], ACT.Exp, scale=SCALE).then_inc(exps, 1)

    STEPS = 11

    def vector(dve):
        count = [0]

        def then(ins):
            ins.then_inc(step, 1)
            count[0] += 1
            dve.wait_ge(step, count[0])

        for half in range(2):
            for n in range(8 * half, 8 * half + 8):
                t = ORDER[n]
                dve.wait_ge(mm_done, n + 1)
                dst, k, b0 = (kv0[:, t, :, :], 2, 0) if t < HB else (qkv1[:, t - HB, :, :], 3, 2)
                nc.vector.tensor_tensor(dst, m.ps[:, n % 4, 0:k * D].rearrange("p (a d) -> p a d", d=D), bias[:, b0:b0 + k, :],
                                        ALU.add).then_inc(taken, 1)
            dve.wait_ge(taken, 8 * half + 8)
            hs = slice(half * TPC, (half + 1) * TPC)
            q1, k1, v1 = (qkv1[:, hs, j, :] for j in range(3))
            k0, v0 = (kv0[:, hs, j, :] for j in range(2))
            tile = lambda a: a.rearrange("p (t d) -> p t d", d=D)
            heads = lambda a: a.rearrange("p (g e) -> p g e", e=HD)
            nc.vector.tensor_tensor(tile(prod[:, 0, :]), q1, k0, ALU.mult)
            then(nc.vector.tensor_tensor(tile(prod[:, 1, :]), q1, k1, ALU.mult))
            then(nc.vector.tensor_reduce(sc[:, :, :].rearrange("p a b -> p (a b)"),
                                         prod[:, :, :].rearrange("p a (g e) -> p (a g) e", e=HD), AX.X, ALU.add))
            then(nc.vector.tensor_tensor(mx[:, :], sc[:, 0, :], sc[:, 1, :], ALU.max))
            then(nc.vector.tensor_tensor(sc[:, :, :], sc[:, :, :], mx[:, :].unsqueeze(1).broadcast_to([P, 2, TPC * H]), ALU.subtract))
            x0 = m.x[:, hs, :]
            x1 = m.x[:, HB + half * TPC:HB + (half + 1) * TPC, :]
            nc.vector.scalar_tensor_tensor(out=x0, in0=v0, scalar=0.5, in1=x0, op0=ALU.mult, op1=ALU.add).then_inc(x_done, 1)
            dve.wait_ge(exps, half + 1)
            then(nc.vector.scalar_tensor_tensor(out=tot[:, :], in0=ex[:, 0, :], scalar=1.0, in1=ex[:, 1, :], op0=ALU.add, op1=ALU.add))
            then(nc.vector.reciprocal(tot[:, :], tot[:, :]))
            then(nc.vector.tensor_tensor(ex[:, :, :], ex[:, :, :], tot[:, :].unsqueeze(1).broadcast_to([P, 2, TPC * H]), ALU.mult))
            weight = lambda j: ex[:, j, :].rearrange("p (t h) -> p t h", h=H).unsqueeze(3).broadcast_to([P, TPC, H, HD])
            split = lambda a: a.rearrange("p t (h e) -> p t h e", e=HD)
            part = lambda j: prod[:, j, :].rearrange("p (t h e) -> p t h e", h=H, e=HD)
            then(nc.vector.tensor_tensor(part(0), split(v0), weight(0), ALU.mult))
            then(nc.vector.tensor_tensor(part(1), split(v1), weight(1), ALU.mult))
            then(nc.vector.tensor_tensor(prod[:, 0, :], prod[:, 0, :], prod[:, 1, :], ALU.add))
            then(nc.vector.tensor_tensor(x1, x1, tile(prod[:, 0, :]), ALU.add))
            assert count[0] == STEPS * (half + 1)

    return Part([(x_done, 1), (x_done, 2), (step, STEPS), (step, 2 * STEPS)], tensor=tensor, vector=vector, scalar=scalar, sync=sync,
                before_norm={"vector": widen, "tensor": rotate, "scalar": take_rotated})


def l1_ffn(nc, m, A, sem, sb, norm):
    E, R = 6, 16
    EP = 8
    HID = (E + 1) * R
    W = HID + E
    wa = sb("l1f_wa", [P, W])
    wb = sb("l1f_wb", [HID, D])
    base = sb("l1f_base", [P, D])
    rb = sb("l1f_rb", [P, E])
    r = router_buffers(sb, "l1f", EP)
    e_, sel_, wte = (sb(f"l1f_{n}", [P, NT, EP]) for n in ("e", "sel", "wte"))
    z, tot, f1 = (sb(f"l1f_{n}", [P, NT]) for n in ("z", "tot", "f1"))
    h = sb("l1f_h", [P, NT, HID])
    hT = sb("l1f_hT", [HID, 2, CH])

    w_in, filled = sem("l1f_w_in"), sem("l1f_filled")
    h_mm, step, exps = sem("l1f_h_mm"), sem("l1f_step"), sem("l1f_exps")
    h_set, turned, hT_set = sem("l1f_h_set"), sem("l1f_turned"), sem("l1f_hT_set")
    y_mm, x_done = sem("l1f_y_mm"), m.x_done

    def sync(sp):
        for dst, name in ((wa, "L1_ffn_wa"), (wb, "L1_ffn_wb"), (base, "L1_ffn_base")):
            sp.dma_start(dst[:, :], A[name]).then_inc(w_in, 16)
        sp.dma_start(rb[:, :], A["L1_ffn_rb"].broadcast_to([P, E])).then_inc(w_in, 16)

    def tensor(pe):
        pe.wait_ge(w_in, 64)
        for c in range(NC):
            pe.wait_ge(m.ln_xnT, norm.value(c))
            for j in range(TPC):
                t = c * TPC + j
                mm = nc.tensor.matmul(m.ps[:, c, j * W:(j + 1) * W], m.xnT[:, t * P:(t + 1) * P], wa[:, :], start=True, stop=True)
            mm.then_inc(h_mm, 1)
        pe.wait_ge(m.ln_xnT, norm.value(NC - 1))
        for c in range(NC + 1):
            if c < NC:
                pe.wait_ge(h_set, c + 1)
                if c >= 2:
                    pe.wait_ge(hT_set, c - 1)
                for j in range(TPC):
                    mm = nc.tensor.transpose(m.ps[0:HID, 4 + c % 2, j * P:(j + 1) * P], h[:, c * TPC + j, :], m.ident[:, :])
                mm.then_inc(turned, 1)
            if c:
                b = c - 1
                pe.wait_ge(hT_set, b + 1)
                if b >= 2:
                    pe.wait_ge(x_done, norm.done(b - 2))
                for j in range(TPC):
                    t = b * TPC + j
                    y = m.ps[:, 6 + b % 2, j * P:(j + 1) * P]
                    nc.tensor.matmul(y, m.xnT[:, t * P:(t + 1) * P], base[:, :], start=(j == 0), stop=False, skip_group_check=True)
                    mm = nc.tensor.matmul(y, hT[:, b % 2, j * P:(j + 1) * P], wb[:, :], start=False, stop=True, skip_group_check=True)
                mm.then_inc(y_mm, 1)

    def scalar(act):
        act.wait_ge(step, STEP_D)
        nc.scalar.activation(e_[:, :, :], e_[:, :, :], ACT.Exp).then_inc(exps, 1)
        for c in range(NC):
            act.wait_ge(turned, c + 1)
            if c >= 2:
                act.wait_ge(y_mm, c - 1)
            nc.scalar.activation(hT[:, c % 2, :], m.ps[0:HID, 4 + c % 2, :], ACT.Copy).then_inc(hT_set, 1)

    STEP_D = 10

    def vector(dve):
        count = [0]

        def then(ins):
            ins.then_inc(step, 1)
            count[0] += 1
            dve.wait_ge(step, count[0])

        L = r.logits
        then(nc.vector.memset(L[:, :, E:EP], -3e38))
        dve.wait_ge(w_in, 64)
        hview = lambda c: m.ps[:, c, 0:TPC * W].rearrange("p (j w) -> p j w", w=W)
        for c in range(NC):
            dve.wait_ge(h_mm, c + 1)
            ts = slice(c * TPC, (c + 1) * TPC)
            nc.vector.tensor_copy(h[:, ts, E * R:HID], hview(c)[:, :, E * R:HID])
            ins = nc.vector.tensor_tensor(L[:, ts, 0:E], hview(c)[:, :, HID:W], rb[:, :].unsqueeze(1).broadcast_to([P, TPC, E]), ALU.add)
            if c == NC - 1:
                then(ins)
        ranks(nc, then, m, r, EP)
        bc = lambda a: a.unsqueeze(2).broadcast_to([P, NT, EP])
        then(nc.vector.tensor_tensor(e_[:, :, :], L[:, :, :], bc(r.first[:, :]), ALU.subtract))
        then(nc.vector.tensor_tensor(sel_[:, :, :], r.is_first[:, :, :], r.is_second[:, :, :], ALU.add))
        assert STEP_D <= count[0], count[0]
        dve.wait_ge(exps, 1)
        then(nc.vector.tensor_reduce(z[:, :], e_[:, :, :], AX.X, ALU.add))
        then(nc.vector.reciprocal(z[:, :], z[:, :]))
        then(nc.vector.tensor_tensor(sel_[:, :, :], sel_[:, :, :], e_[:, :, :], ALU.mult))
        then(nc.vector.tensor_tensor(sel_[:, :, :], sel_[:, :, :], bc(z[:, :]), ALU.mult))
        then(nc.vector.tensor_reduce(tot[:, :], sel_[:, :, :], AX.X, ALU.add))
        then(nc.vector.tensor_scalar(tot[:, :], tot[:, :], 1e-6, None, ALU.add))
        then(nc.vector.reciprocal(tot[:, :], tot[:, :]))
        then(nc.vector.tensor_tensor(wte[:, :, :], sel_[:, :, :], bc(tot[:, :]), ALU.mult))
        for c in range(NC):
            ts = slice(c * TPC, (c + 1) * TPC)
            for j in range(TPC):
                t = c * TPC + j
                ins = nc.vector.tensor_tensor(h[:, t, 0:E * R].rearrange("p (e r) -> p e r", r=R),
                                              hview(c)[:, j, 0:E * R].rearrange("p (e r) -> p e r", r=R),
                                              wte[:, t, 0:E].unsqueeze(2).broadcast_to([P, E, R]), ALU.mult)
            ins.then_inc(h_set, 1)
        for c in range(NC):
            dve.wait_ge(y_mm, c + 1)
            dve.wait_ge(m.biased, norm.biased_value(c))
            xs = m.x[:, c * TPC:(c + 1) * TPC, :]
            nc.vector.tensor_tensor(xs, m.ps[:, 6 + c % 2, :].rearrange("p (j d) -> p j d", d=D), xs, ALU.add).then_inc(x_done, 1)

    return Part([(x_done, norm.done(c)) for c in range(NC)], tensor=tensor, vector=vector, scalar=scalar, sync=sync, bias="L1_ffn_base_b")


def l2_attn(nc, m, A, sem, sb, norm):
    H, HD = 16, 8
    G = H // 4
    PAD = 32
    TB = S // P
    VW = HD + 1
    w = sb("l2a_w", [P, 3, D])
    wo = sb("l2a_wo", [P, D])
    bqk = sb("l2a_bqk", [P, 2])
    bv = sb("l2a_bv", [P, D])
    causal = sb("l2a_causal", [P, P])
    hmask = sb("l2a_hmask", [P, H])
    early = sb("l2a_early", [P, NT * D])
    low, expd = (early[:, n * 2 * CH:(n + 1) * 2 * CH].rearrange("p (a b) -> p a b", a=2) for n in range(2))
    pos = sb("l2a_pos", [P, 2, CH])
    phi = sb("l2a_phi", [P, 2, T])
    ktok = sb("l2a_ktok", [P, NT, D])
    vpad = sb("l2a_vpad", [P, NT, H, PAD])
    qm = sb("l2a_qm", [P, 2, H, P])
    at = sb("l2a_at", [P, 2, G, 4 * P])
    state = sb("l2a_state", [P, 2, H, PAD])
    numT = sb("l2a_numT", [P, 2, G * P])
    den, rec = sb("l2a_den", [P, 2, H]), sb("l2a_rec", [P, 2, H])
    o = early.rearrange("p (t d) -> p t d", d=D)
    oT = sb("l2a_oT", [P, CH])

    w_in = sem("l2a_w_in")
    zeroed = sem("l2a_zeroed")
    p_mm, lowered, expd_set, elu_set, phi_set = (sem(f"l2a_{n}") for n in ("p_mm", "lowered", "expd_set", "elu_set", "phi_set"))
    v_mm, v_set, k_turned, ktok_set = (sem(f"l2a_{n}") for n in ("v_mm", "v_set", "k_turned", "ktok_set"))
    qm_set, a_mm, a_set, s_mm, s_set = (sem(f"l2a_{n}") for n in ("qm_set", "a_mm", "a_set", "s_mm", "s_set"))
    n_mm, n_out, n_turned, den_set, rec_set, o_set = (sem(f"l2a_{n}") for n in ("n_mm", "n_out", "n_turned", "den_set", "rec_set", "o_set"))
    o_turned, oT_set, y_mm = (sem(f"l2a_{n}") for n in ("o_turned", "oT_set", "y_mm"))
    x_done = m.x_done

    def sync(sp):
        sp.dma_start(w[:, :, :], A["L2_attn_w"]).then_inc(w_in, 16)
        sp.dma_start(wo[:, :], A["L2_attn_wo"]).then_inc(w_in, 16)
        sp.dma_start(bqk[:, :], A["L2_attn_bqk"]).then_inc(w_in, 16)
        sp.dma_start(bv[:, :], A["L2_attn_bv"].broadcast_to([P, D])).then_inc(w_in, 16)
        sp.dma_start(causal[:, :], A["causal"]).then_inc(w_in, 16)
        sp.dma_start(hmask[:, :], A["hmask"]).then_inc(w_in, 16)

    def clear(pool):
        pool.wait_ge(w_in, 16 * 6)
        nc.gpsimd.memset(vpad[:, :, :, :], 0.0).then_inc(zeroed, 1)
        nc.gpsimd.memset(state[:, :, :, :], 0.0).then_inc(zeroed, 1)
        pool.wait_ge(zeroed, 2)
        nc.gpsimd.memset(vpad[:, :, :, HD:VW], 1.0).then_inc(zeroed, 1)

    def gpsimd(pool):
        for t in range(NT):
            c = t // TPC
            pool.wait_ge(phi_set, 2 * c + 1)
            if t >= 2:
                pool.wait_ge(n_mm, t - 1)
            nc.gpsimd.tensor_tensor(qm[:, t % 2, :, :], phi[:, 0, t * P:(t + 1) * P].unsqueeze(1).broadcast_to([P, H, P]),
                                    hmask[:, :].unsqueeze(2).broadcast_to([P, H, P]), ALU.mult).then_inc(qm_set, 1)

    def tensor(pe):
        pe.wait_ge(w_in, 16 * 6)
        for c in range(NC):
            pe.wait_ge(m.ln_xnT, norm.value(c))
            cs = slice(c * CH, (c + 1) * CH)
            for j in range(2):
                n = 2 * c + j
                if n >= 4:
                    pe.wait_ge(phi_set, n - 3)
                nc.tensor.matmul(m.ps[:, n % 4, :], w[:, j, :], m.xnT[:, cs], start=True, stop=True).then_inc(p_mm, 1)
            if c:
                pe.wait_ge(v_set, c)
            for t in range(c * TPC, (c + 1) * TPC):
                mm = nc.tensor.matmul(m.ps[:, 4, t % TPC * P:(t % TPC + 1) * P], m.xnT[:, t * P:(t + 1) * P], w[:, 2, :], start=True, stop=True)
            mm.then_inc(v_mm, 1)
        for c in range(NC):
            pe.wait_ge(phi_set, 2 * c + 2)
            if c:
                pe.wait_ge(ktok_set, c)
            for t in range(c * TPC, (c + 1) * TPC):
                mm = nc.tensor.transpose(m.ps[:, 5, t % TPC * P:(t % TPC + 1) * P], phi[:, 1, t * P:(t + 1) * P], m.ident[:, :])
            mm.then_inc(k_turned, 1)
        pe.wait_ge(zeroed, 3)
        pe.wait_ge(v_set, NC)
        pe.wait_ge(ktok_set, NC)

        def scores(t):
            pe.wait_ge(qm_set, t + 1)
            for g in range(G):
                if t:
                    pe.wait_ge(a_set, G * (t - 1) + g + 1)
                nc.tensor.matmul(m.ps[:, g, :], phi[:, 1, t * P:(t + 1) * P], qm[:, t % 2, 4 * g:4 * g + 4, :], start=True, stop=True).then_inc(a_mm, 1)

        def add_state(t):
            if t:
                pe.wait_ge(s_set, t)
            nc.tensor.matmul(m.ps[:, 7, 0:H * VW], ktok[:, t, :], vpad[:, t, :, 0:VW], start=(t % TB == 0), stop=True,
                             skip_group_check=True).then_inc(s_mm, 1)

        def numerators(t):
            if t:
                pe.wait_ge(n_out, t)
            if t % TB:
                pe.wait_ge(s_set, t)
                for g in range(G):
                    nc.tensor.matmul(m.ps[:, 4, g * P:(g + 1) * P], state[:, t % 2, 4 * g:4 * g + 4, :], phi[:, 0, t * P:(t + 1) * P],
                                     start=(g == 0), stop=False, skip_group_check=True)
            for g in range(G):
                pe.wait_ge(a_set, G * t + g + 1)
                for j in range(4):
                    mm = nc.tensor.matmul(m.ps[PAD * j:PAD * (j + 1), 4, g * P:(g + 1) * P], vpad[:, t, 4 * g + j, :],
                                          at[:, t % 2, g, j * P:(j + 1) * P], start=(t % TB == 0 and g == 0), stop=(g == G - 1),
                                          skip_group_check=True)
            mm.then_inc(n_mm, 1)

        def turn_numerators(t):
            pe.wait_ge(n_out, t + 1)
            if t:
                pe.wait_ge(o_set, t)
            for g in range(G):
                mm = nc.tensor.transpose(m.ps[:, 5, g * P:(g + 1) * P], numT[:, t % 2, g * P:(g + 1) * P], m.ident[:, :])
            mm.then_inc(n_turned, 1)

        def project(c):
            pe.wait_ge(o_set, (c + 1) * TPC)
            if c:
                pe.wait_ge(x_done, norm.done(c - 1))
            for j in range(TPC):
                mm = nc.tensor.transpose(m.ps[:, 6, j * P:(j + 1) * P], o[:, c * TPC + j, :], m.ident[:, :])
            mm.then_inc(o_turned, 1)
            pe.wait_ge(oT_set, c + 1)
            for j in range(TPC):
                mm = nc.tensor.matmul(m.ps[:, 6, j * P:(j + 1) * P], oT[:, j * P:(j + 1) * P], wo[:, :], start=True, stop=True)
            mm.then_inc(y_mm, 1)

        for t in range(NT + 2):
            if t < NT:
                scores(t)
            if 1 <= t <= NT:
                numerators(t - 1)
            if t < NT:
                add_state(t)
            if t >= 2:
                turn_numerators(t - 2)
            if t >= 3 and (t - 3) % TPC == TPC - 1:
                project((t - 3) // TPC)
        project(NC - 1)

    def scalar(act):
        for n in range(2 * NC):
            act.wait_ge(lowered, n + 1)
            if n >= 2:
                act.wait_ge(phi_set, n - 1)
            nc.scalar.activation(expd[:, n % 2, :], low[:, n % 2, :], ACT.Exp)
            nc.scalar.activation(pos[:, n % 2, :], m.ps[:, n % 4, :], ACT.Relu, bias=bqk[:, n % 2:n % 2 + 1]).then_inc(expd_set, 1)
        for c in range(NC):
            act.wait_ge(k_turned, c + 1)
            nc.scalar.activation(ktok[:, c * TPC:(c + 1) * TPC, :].rearrange("p t d -> p (t d)"), m.ps[:, 5, :], ACT.Copy).then_inc(ktok_set, 1)

        def oT_copy(c):
            act.wait_ge(o_turned, c + 1)
            nc.scalar.activation(oT[:, :], m.ps[:, 6, :], ACT.Copy).then_inc(oT_set, 1)

        for t in range(NT):
            act.wait_ge(n_mm, t + 1)
            if t >= 2:
                act.wait_ge(n_turned, t - 1)
            nc.scalar.activation(numT[:, t % 2, :], m.ps[:, 4, :], ACT.Copy).then_inc(n_out, 1)
            if t >= TPC + 1 and (t - 1) % TPC == 0:
                oT_copy((t - 1) // TPC - 1)
        oT_copy(NC - 1)

    def vector(dve):
        for n in range(2 * NC):
            dve.wait_ge(p_mm, n + 1)
            if n >= 2:
                dve.wait_ge(expd_set, n - 1)
            nc.vector.tensor_scalar(low[:, n % 2, :], m.ps[:, n % 4, :], bqk[:, n % 2:n % 2 + 1], 0.0, ALU.add, ALU.min).then_inc(lowered, 1)
            if n % 2:
                c = n // 2
                dve.wait_ge(v_mm, c + 1)
                dve.wait_ge(zeroed, 3)
                ts = slice(c * TPC, (c + 1) * TPC)
                nc.vector.tensor_tensor(vpad[:, ts, :, 0:HD], m.ps[:, 4, :].rearrange("p (t h e) -> p t h e", h=H, e=HD),
                                        bv[:, :].rearrange("p (h e) -> p h e", e=HD).unsqueeze(1).broadcast_to([P, TPC, H, HD]), ALU.add).then_inc(v_set, 1)
            dve.wait_ge(expd_set, n + 1)
            c = n // 2
            ph = phi[:, n % 2, c * CH:(c + 1) * CH]
            nc.vector.scalar_tensor_tensor(out=ph, in0=expd[:, n % 2, :], scalar=-1.0, in1=pos[:, n % 2, :],
                                           op0=ALU.add, op1=ALU.add).then_inc(elu_set, 1)
            dve.wait_ge(elu_set, n + 1)
            nc.vector.tensor_scalar(ph, ph, 1.0, None, ALU.add).then_inc(phi_set, 1)

        def mask_scores(t):
            if t >= 2:
                dve.wait_ge(n_mm, t - 1)
            for g in range(G):
                dve.wait_ge(a_mm, G * t + g + 1)
                nc.vector.tensor_tensor(at[:, t % 2, g, :].rearrange("p (j q) -> p j q", q=P), m.ps[:, g, :].rearrange("p (j q) -> p j q", q=P),
                                        causal[:, :].unsqueeze(1).broadcast_to([P, 4, P]), ALU.mult).then_inc(a_set, 1)

        def mask_state(t):
            dve.wait_ge(s_mm, t + 1)
            nc.vector.tensor_tensor(state[:, (t + 1) % 2, :, 0:VW], m.ps[:, 7, 0:H * VW].rearrange("p (h e) -> p h e", e=VW),
                                    hmask[:, :].unsqueeze(2).broadcast_to([P, H, VW]), ALU.mult).then_inc(s_set, 1)

        def divide(t):
            dve.wait_ge(n_turned, t + 1)
            turned = m.ps[:, 5, :].rearrange("p (h e) -> p h e", e=PAD)
            nc.vector.tensor_scalar(den[:, t % 2, :], turned[:, :, HD], 1e-6, None, ALU.add).then_inc(den_set, 1)
            dve.wait_ge(den_set, t + 1)
            nc.vector.reciprocal(rec[:, t % 2, :], den[:, t % 2, :]).then_inc(rec_set, 1)
            dve.wait_ge(rec_set, t + 1)
            nc.vector.tensor_tensor(o[:, t, :].rearrange("p (h e) -> p h e", e=HD), turned[:, :, 0:HD],
                                    rec[:, t % 2, :].unsqueeze(2).broadcast_to([P, H, HD]), ALU.mult).then_inc(o_set, 1)

        def add(c):
            dve.wait_ge(y_mm, c + 1)
            dve.wait_ge(m.biased, norm.biased_value(c))
            xs = m.x[:, c * TPC:(c + 1) * TPC, :]
            nc.vector.tensor_tensor(xs, m.ps[:, 6, :].rearrange("p (j d) -> p j d", d=D), xs, ALU.add).then_inc(x_done, 1)

        for t in range(NT + 2):
            if t < NT:
                mask_scores(t)
            if t < NT:
                mask_state(t)
            if t >= 2:
                divide(t - 2)
            if t >= TPC + 3 and (t - 3) % TPC == 0:
                add((t - 3) // TPC - 1)
        add(NC - 1)

    return Part([(x_done, norm.done(c)) for c in range(NC)], tensor=tensor, vector=vector, scalar=scalar, gpsimd=gpsimd, sync=sync,
                before_norm={"gpsimd": clear}, bias="L2_attn_bo")


def l2_ffn(nc, m, A, sem, sb, norm):
    E, F = 8, 256
    FT = F // P
    W1, W2, B1, WN = 0, F, 2 * F, 2 * F + 2
    EPS = 1e-6
    UNROLL = 2 * NC
    w = sb("l2f_w", [P, 2, WN])
    gate = sb("l2f_gate", [P, E])
    lnb = sb("l2f_lnb", [E, D])
    b2 = sb("l2f_b2", [P, E, D])
    lng = sb("l2f_lng", [P, E, D])
    hT = sb("l2f_hT", [P, 2, FT, CH])
    xb = sb("l2f_xb", [P, 2, TPC, D])
    z = sb("l2f_z", [P, 4, TPC, D])
    st, mv = sb("l2f_st", [P, 4, TPC, 6]), sb("l2f_mv", [P, 4, TPC, 2])
    ve, rs, nb = (sb(f"l2f_{n}", [P, 4, TPC]) for n in ("ve", "rs", "nb"))
    r = router_buffers(sb, "l2f", E)
    wte, w2nd = sb("l2f_wte", [P, NT, E]), sb("l2f_w2nd", [P, NT, E])
    wteT = sb("l2f_wteT", [E, T])
    gap, z12 = sb("l2f_gap", [P, NT]), sb("l2f_z12", [P, NT])
    eps = sb("l2f_eps", [P, TPC])

    small_in, eps_set = sem("l2f_small_in"), sem("l2f_eps_set")
    w_in = [sem(f"l2f_w_in{u}") for u in range(2)]
    logits, step, exps = sem("l2f_logits"), sem("l2f_step"), sem("l2f_exps")
    wte_set, turned, wteT_set, lnb_mm, lnb_added = (sem(f"l2f_{n}") for n in ("wte_set", "turned", "wteT_set", "lnb_mm", "lnb_added"))
    up_done, h_done, o_done = sem("l2f_up_done"), sem("l2f_h_done"), sem("l2f_o_done")
    xb_done, z_done, stats, var, vareps = (sem(f"l2f_{n}") for n in ("xb_done", "z_done", "stats", "var", "vareps"))
    rstd, nb_done, zn_done, zg_done, y_done = (sem(f"l2f_{n}") for n in ("rstd", "nb_done", "zn_done", "zg_done", "y_done"))

    def load(sp, slot, e):
        return sp.dma_start(w[:, slot, :], A["L2_ffn_w"][bass.ds(e, 1), :, :].rearrange("e p n -> p (e n)")).then_inc(w_in[slot], 16)

    def sync(sp):
        sp.dma_start(gate[:, :], A["L2_ffn_gate_w"]).then_inc(small_in, 16)
        sp.dma_start(lnb[:, :], A["L2_ffn_ln_b"]).then_inc(small_in, 16)
        sp.dma_start(b2[:, :, :].rearrange("p e d -> p (e d)"), A["L2_ffn_b2"].broadcast_to([P, E * D])).then_inc(small_in, 16)
        sp.dma_start(lng[:, :, :].rearrange("p e d -> p (e d)"), A["L2_ffn_ln_g"].broadcast_to([P, E * D])).then_inc(small_in, 16)
        load(sp, 0, 0)
        load(sp, 1, 1)
        with sp.Fori(1, E // 2) as i:
            for u in range(2):
                sp.wait_ge(o_done, i * UNROLL + NC * (u - 1))
                load(sp, u, i * 2 + u)

    def pipelined(eng, body, tail):
        for k in range(UNROLL):
            body(0, k, k)
        with eng.Fori(1, E // 2) as i:
            for k in range(UNROLL):
                body(i, k, None)
        tail()

    def tensor(pe):
        pe.wait_ge(small_in, 64)
        for t in range(NT):
            if t % TPC == 0:
                pe.wait_ge(m.ln_xnT, norm.value(t // TPC))
            mm = nc.tensor.matmul(m.ps[:, 5, t * E:(t + 1) * E], m.xnT[:, t * P:(t + 1) * P], gate[:, :], start=True, stop=True)
        mm.then_inc(logits, 1)

        def up(i, k, n):
            u, c = k // NC % 2, k % NC
            if c == 0:
                pe.wait_ge(w_in[u], (i + 1) * 16)
            if n is None or n >= 2:
                pe.wait_ge(h_done, i * (FT * UNROLL) + FT * (k - 1))
            for f in range(FT):
                mm = nc.tensor.matmul(m.ps[:, 2 * (k % 2) + f, :], w[:, u, W1 + f * P:W1 + (f + 1) * P], m.xnT[:, c * CH:(c + 1) * CH],
                                      start=True, stop=True)
                mm.then_inc(up_done, 1)

        def down(i, k, n):
            u = k // NC % 2
            if n is None or n >= 2:
                pe.wait_ge(z_done, i * UNROLL + (k - 1))
            pe.wait_ge(h_done, i * (FT * UNROLL) + FT * (k + 1))
            for f in range(FT):
                for j in range(TPC):
                    mm = nc.tensor.matmul(m.ps[:, 4 + k % 2, j * P:(j + 1) * P], hT[:, k % 2, f, j * P:(j + 1) * P],
                                          w[:, u, W2 + f * P:W2 + (f + 1) * P], start=(f == 0 and j == 0),
                                          stop=(f == FT - 1), skip_group_check=True)
            mm.then_inc(o_done, 1)

        def norm_biases():
            pe.wait_ge(wte_set, 1)
            for c in range(NC):
                if c >= 2:
                    pe.wait_ge(wteT_set, c - 1)
                for j in range(TPC):
                    mm = nc.tensor.transpose(m.ps[0:E, 6 + c % 2, j * P:(j + 1) * P], wte[:, c * TPC + j, :], m.ident[:, :])
                mm.then_inc(turned, 1)
            for c in range(NC):
                pe.wait_ge(wteT_set, NC)
                if c >= 2:
                    pe.wait_ge(lnb_added, c - 1)
                for j in range(TPC):
                    t = c * TPC + j
                    mm = nc.tensor.matmul(m.ps[:, 6 + c % 2, j * P:(j + 1) * P], wteT[:, t * P:(t + 1) * P], lnb[:, :], start=True, stop=True)
                mm.then_inc(lnb_mm, 1)

        pe.wait_ge(step, 1)

        def body(i, k, n):
            up(i, k, n)
            if n is None or n >= 1:
                down(i, k - 1, None if n is None else n - 1)
            if n == 1:
                norm_biases()

        pipelined(pe, body, lambda: down(E // 2 - 1, UNROLL - 1, None))

    def scalar(act):
        act.wait_ge(step, 9)
        nc.scalar.activation(gap[:, :], gap[:, :], ACT.Exp).then_inc(exps, 1)
        def turn(c):
            act.wait_ge(turned, c + 1)
            nc.scalar.activation(wteT[:, c * CH:(c + 1) * CH], m.ps[0:E, 6 + c % 2, :], ACT.Copy).then_inc(wteT_set, 1)

        def zn(i, k):
            act.wait_ge(nb_done, i * UNROLL + (k + 1))
            for j in range(TPC):
                ins = nc.scalar.activation(z[:, k % 4, j, :], z[:, k % 4, j, :], ACT.Identity, bias=nb[:, k % 4, j:j + 1],
                                           scale=rs[:, k % 4, j:j + 1])
            ins.then_inc(zn_done, 1)

        def body(i, k, n):
            u = k // NC % 2
            for f in range(FT):
                act.wait_ge(up_done, i * (FT * UNROLL) + (FT * k + f + 1))
                nc.scalar.activation(hT[:, k % 2, f, :], m.ps[:, 2 * (k % 2) + f, :], ACT.Gelu,
                                     bias=w[:, u, B1 + f:B1 + f + 1]).then_inc(h_done, 1)
            if n == 1:
                for c in range(NC):
                    turn(c)
            if n is None or n >= 3:
                zn(i, k - 3)

        def tail():
            for k in range(UNROLL - 3, UNROLL):
                zn(E // 2 - 1, k)

        pipelined(act, body, tail)

    def gpsimd(pool):
        pool.wait_ge(small_in, 64)

        def expert(i, k):
            return bass.ds(i * 2 + k // NC, 1)

        def add_b2(i, k):
            c = k % NC
            nc.gpsimd.tensor_tensor(xb[:, k % 2, :, :], m.xn[:, c * TPC:(c + 1) * TPC, :],
                                    b2[:, expert(i, k), :].broadcast_to([P, TPC, D]), ALU.add).then_inc(xb_done, 1)

        def times_g(i, k):
            nc.gpsimd.tensor_tensor(z[:, k % 4, :, :], z[:, k % 4, :, :], lng[:, expert(i, k), :].broadcast_to([P, TPC, D]),
                                    ALU.mult).then_inc(zg_done, 1)

        def body(i, k, n, last=False):
            pool.wait_ge(var, i * UNROLL + (k + 1))
            nc.gpsimd.tensor_tensor(ve[:, k % 4, :], mv[:, k % 4, :, 1], eps[:, :], ALU.add).then_inc(vareps, 1)
            if n is None or n >= 2:
                pool.wait_ge(zn_done, i * UNROLL + (k - 1))
            pool.wait_ge(vareps, i * UNROLL + (k + 1))
            nc.gpsimd.tensor_tensor(rs[:, k % 4, :], ve[:, k % 4, :], m.power[:, 0:TPC], ALU.pow).then_inc(rstd, 1)
            if not last:
                add_b2(i, k + 1)
            if n is None or n >= 2:
                times_g(i, k - 2)

        nc.gpsimd.memset(eps[:, :], EPS).then_inc(eps_set, 1)
        pool.wait_ge(eps_set, 1)
        pool.wait_ge(m.ln_xn, norm.value(NC - 1))
        add_b2(0, 0)
        for k in range(UNROLL):
            body(0, k, k)
        with pool.Fori(1, E // 2 - 1) as i:
            for k in range(UNROLL):
                body(i, k, None)
        last = E // 2 - 1
        for k in range(UNROLL):
            body(last, k, None, last=(k == UNROLL - 1))
        for k in (UNROLL - 2, UNROLL - 1):
            pool.wait_ge(zn_done, last * UNROLL + (k + 1))
            times_g(last, k)

    def vector(dve):
        count = [0]

        def then(ins):
            ins.then_inc(step, 1)
            count[0] += 1
            dve.wait_ge(step, count[0])

        L = r.logits
        dve.wait_ge(logits, 1)
        then(nc.vector.tensor_copy(L[:, :, :].rearrange("p t e -> p (t e)"), m.ps[:, 5, 0:NT * E]))
        ranks(nc, then, m, r, E)
        bc = lambda a: a.unsqueeze(2).broadcast_to([P, NT, E])
        then(nc.vector.tensor_tensor(gap[:, :], r.second[:, :], r.first[:, :], ALU.subtract))
        assert count[0] == 9
        dve.wait_ge(exps, 1)
        then(nc.vector.tensor_scalar(z12[:, :], gap[:, :], 1.0, None, ALU.add))
        then(nc.vector.reciprocal(z12[:, :], z12[:, :]))
        then(nc.vector.tensor_tensor(gap[:, :], gap[:, :], z12[:, :], ALU.mult))
        then(nc.vector.tensor_tensor(w2nd[:, :, :], r.is_second[:, :, :], bc(gap[:, :]), ALU.mult))
        then(nc.vector.tensor_tensor(wte[:, :, :], r.is_first[:, :, :], bc(z12[:, :]), ALU.mult))
        nc.vector.tensor_tensor(wte[:, :, :], wte[:, :, :], w2nd[:, :, :], ALU.add).then_inc(wte_set, 1)
        dve.wait_ge(wte_set, 1)

        def sums(i, k, n):
            if n is None or n >= 4:
                dve.wait_ge(y_done, i * UNROLL + (k - 3))
            dve.wait_ge(o_done, i * UNROLL + (k + 1))
            dve.wait_ge(xb_done, i * UNROLL + (k + 1))
            nc.vector.tensor_tensor(z[:, k % 4, :, :], m.ps[:, 4 + k % 2, :].rearrange("p (j d) -> p j d", d=D), xb[:, k % 2, :, :],
                                    ALU.add).then_inc(z_done, 1)
            dve.wait_ge(z_done, i * UNROLL + (k + 1))
            for j in range(TPC):
                ins = nc.vector.bn_stats(st[:, k % 4, j, :], z[:, k % 4, j, :])
            ins.then_inc(stats, 1)

        def variance(i, k):
            if isinstance(i, int) and i * UNROLL + k == 0:
                dve.wait_ge(stats, 1)
            for j in range(TPC):
                ins = nc.vector.bn_aggr(mv[:, k % 4, j, :], st[:, k % 4, j, :])
            ins.then_inc(var, 1)

        def shift(i, k, last=False):
            if not last:
                dve.wait_ge(stats, i * UNROLL + (k + 2))
            dve.wait_ge(rstd, i * UNROLL + (k + 1))
            nc.vector.scalar_tensor_tensor(out=nb[:, k % 4, :], in0=mv[:, k % 4, :, 0], scalar=-1.0, in1=rs[:, k % 4, :],
                                           op0=ALU.mult, op1=ALU.mult).then_inc(nb_done, 1)

        def add(i, k, n):
            c = k % NC
            dve.wait_ge(zg_done, i * UNROLL + (k + 1))
            if n is None or n >= NC:
                dve.wait_ge(y_done, i * UNROLL + (k - NC + 1))
            for j in range(TPC):
                t = c * TPC + j
                ins = nc.vector.scalar_tensor_tensor(out=m.x[:, t, :], in0=z[:, k % 4, j, :], scalar=wte[:, t, bass.ds(i * 2 + k // NC, 1)],
                                                     in1=m.x[:, t, :], op0=ALU.mult, op1=ALU.add)
            ins.then_inc(y_done, 1)

        def add_biases(c):
            dve.wait_ge(lnb_mm, c + 1)
            xs = m.x[:, c * TPC:(c + 1) * TPC, :]
            nc.vector.tensor_tensor(xs, m.ps[:, 6 + c % 2, :].rearrange("p (j d) -> p j d", d=D), xs, ALU.add).then_inc(lnb_added, 1)

        def body(i, k, n):
            sums(i, k, n)
            if n == 0:
                for c in range(NC):
                    add_biases(c)
                dve.wait_ge(lnb_added, NC)
            if n is None or n >= 1:
                shift(i, k - 1)
            variance(i, k)
            if n is None or n >= 3:
                add(i, k - 3, None if n is None else n - 3)

        def tail():
            shift(E // 2 - 1, UNROLL - 1, last=True)
            for k in range(UNROLL - 3, UNROLL):
                add(E // 2 - 1, k, None)

        pipelined(dve, body, tail)

    total = E * NC
    return Part([(y_done, total - NC + c + 1) for c in range(NC)], tensor=tensor, vector=vector, scalar=scalar, gpsimd=gpsimd, sync=sync)


def l3_attn(nc, m, A, sem, sb, norm):
    HEADS, DH, R = 16, 64, 64
    RT = HEADS * R // P
    TB = S // P
    SW = D + 1
    wqk = sb("l3a_wqk", [P, 2 * RT, D])
    rf = sb("l3a_rf", [P, RT, P])
    wv = sb("l3a_wv", [P, RT, P])
    wout = sb("l3a_wout", [P, RT, D])
    sel = sb("l3a_sel", [P, RT, P])
    kmask = sb("l3a_kmask", [P, RT, 32])
    blocks = sb("l3a_blocks", [P, P])
    wrf = sb("l3a_wrf", [P, 2 * RT, P])
    phik = sb("l3a_phik", [P, 2, RT * P])
    s_sb = sb("l3a_s", [P, B, RT, SW])
    sT = sb("l3a_sT", [P, RT, P])
    kv = sb("l3a_kv", [P, RT, P])
    mix = sb("l3a_mix", [P, B, RT, D])
    knorm = sb("l3a_knorm", [P, B, RT, 32])
    phiq = sb("l3a_phiq", [P, 2, RT, CH])
    rn = sb("l3a_rn", [P, 2, CH])

    w_in = sem("l3a_w_in")
    prod = sem("l3a_prod")
    prod_out = sem("l3a_prod_out")
    k_mm = sem("l3a_k_mm")
    k_relu = sem("l3a_k_relu")
    s_mm = sem("l3a_s_mm")
    s_out = sem("l3a_s_out")
    knorm_set = sem("l3a_knorm_set")
    tail_mm = sem("l3a_tail_mm")
    tail_act, tail_dve = sem("l3a_tail_act"), sem("l3a_tail_dve")
    q_mm = sem("l3a_q_mm")
    q_relu = sem("l3a_q_relu")
    n_mm = sem("l3a_n_mm")
    n_eps = sem("l3a_n_eps")
    n_rec = sem("l3a_n_rec")
    b_mm = sem("l3a_b_mm")
    scaled = sem("l3a_scaled")
    o_mm = sem("l3a_o_mm")
    x_done = m.x_done

    def sync(sp):
        for dst, name in ((wqk, "L3_attn_wqkT"), (rf, "L3_attn_rf"), (wv, "L3_attn_wv"), (wout, "L3_attn_wout"),
                          (sel, "L3_attn_sel"), (kmask, "L3_attn_kmask")):
            sp.dma_start(dst[:, :, :], A[name]).then_inc(w_in, 16)
        sp.dma_start(blocks[:, :], A["L3_attn_blocks"]).then_inc(w_in, 16)

    def before_norm(pe):
        pe.wait_ge(w_in, 16 * 7)
        for t in range(2 * RT):
            if t % 4 == 0 and t >= 8:
                pe.wait_ge(prod_out, t // 4 - 1)
            mm = nc.tensor.matmul(m.ps[:, t // 4 % 2, t % 4 * P:(t % 4 + 1) * P], wqk[:, t, :], rf[:, t % RT, :],
                                  start=True, stop=True)
            if t % 4 == 3:
                mm.then_inc(prod, 1)

    def tensor(pe):
        def phi_k(n):
            b, t = divmod(n, TB)
            pe.wait_ge(m.ln_xnT, norm.value(n // TPC))
            pe.wait_ge(prod_out, 4)
            if n >= 2:
                pe.wait_ge(k_relu, n - 1)
            for h in range(2):
                mm = nc.tensor.matmul(m.ps[:, 2 * (n % 2) + h, :], m.xnT[:, n * P:(n + 1) * P],
                                      wrf[:, RT + 4 * h:RT + 4 * h + 4, :], start=True, stop=True)
            mm.then_inc(k_mm, 1)

        def phi_k_xn(n):
            b, t = divmod(n, TB)
            pe.wait_ge(k_relu, n + 1)
            if n == 0:
                pe.wait_ge(m.ln_xnT, norm.value(NC - 1))
            if t == 0 and b:
                pe.wait_ge(s_out, b)
            for r in range(RT):
                mm = nc.tensor.matmul(m.ps[:, 4 + r // 3, r % 3 * SW:(r % 3 + 1) * SW], phik[:, n % 2, r * P:(r + 1) * P],
                                      m.xn1[:, n, :], start=(t == 0 and r % 3 == 0), stop=(t == TB - 1), skip_group_check=True)
            if t == TB - 1:
                mm.then_inc(s_mm, 1)

        for n in range(NT):
            phi_k(n)
            if n:
                phi_k_xn(n - 1)
        phi_k_xn(NT - 1)

        def turn_s(b):
            pe.wait_ge(s_out, B)
            if b:
                pe.wait_ge(tail_act, 2 * b)
            for r in range(RT):
                mm = nc.tensor.transpose(m.ps[:, 6 + r // 4, r % 4 * P:(r % 4 + 1) * P], s_sb[:, b, r, 0:D], m.ident[:, :])
            mm.then_inc(tail_mm, 1)

        def s_wv(b):
            pe.wait_ge(tail_act, 2 * b + 1)
            for r in range(RT):
                mm = nc.tensor.matmul(m.ps[:, 6 + r // 4, r % 4 * P:(r % 4 + 1) * P], wv[:, r, :], sT[:, r, :], start=True, stop=True)
            mm.then_inc(tail_mm, 1)

        def kv_wout(b):
            pe.wait_ge(tail_dve, b + 1)
            for r in range(RT):
                mm = nc.tensor.matmul(m.ps[:, 6 + r // 4, r % 4 * P:(r % 4 + 1) * P], kv[:, r, :], wout[:, r, :], start=True, stop=True)
            mm.then_inc(tail_mm, 1)

        def phi_q(c, rs):
            for r in rs:
                n = c * RT + r
                if n >= 2:
                    pe.wait_ge(q_relu, n - 1)
                nc.tensor.matmul(m.ps[:, n % 2, :], wrf[:, r, :], m.xnT[:, c * CH:(c + 1) * CH], start=True, stop=True).then_inc(q_mm, 1)

        def normaliser(c):
            b = c // (NC // B)
            pe.wait_ge(knorm_set, b + 1)
            pe.wait_ge(q_relu, c * RT + RT)
            if c:
                pe.wait_ge(n_eps, c)
            for r in range(RT):
                g = 32 * (r % 4)
                mm = nc.tensor.matmul(m.ps[g:g + 32, 2, :], knorm[:, b, r, :], phiq[:, c % 2, r, :], start=(r < 4), stop=(r >= 4),
                                      skip_group_check=True)
            mm.then_inc(n_mm, 1)

        def spread(c):
            pe.wait_ge(n_rec, c + 1)
            for r in range(RT):
                n = c * RT + r
                if n >= 2:
                    pe.wait_ge(scaled, n - 1)
                nc.tensor.matmul(m.ps[:, 3 + n % 2, :], sel[:, r, :], rn[:, c % 2, :], start=True, stop=True).then_inc(b_mm, 1)

        def outputs(c):
            b = c // (NC // B)
            pe.wait_ge(tail_act, 2 * b + 2)
            if c:
                pe.wait_ge(x_done, norm.done(c - 1))
            for r in range(RT):
                pe.wait_ge(scaled, c * RT + r + 1)
                for j in range(TPC):
                    mm = nc.tensor.matmul(m.ps[:, 5, j * P:(j + 1) * P], phiq[:, c % 2, r, j * P:(j + 1) * P], mix[:, b, r, :],
                                          start=(r == 0 and j == 0), stop=(r == RT - 1), skip_group_check=True)
            mm.then_inc(o_mm, 1)

        for c in range(NC + 1):
            tail = c < NC and c % (NC // B) == 0
            b = c // (NC // B)
            if c < NC:
                phi_q(c, range(0, 2))
                if c == 0:
                    turn_s(0)
                if tail:
                    s_wv(b)
                phi_q(c, range(2, 4))
                if tail:
                    kv_wout(b)
                phi_q(c, range(4, RT))
                normaliser(c)
            if c == 1:
                turn_s(1)
            if c:
                spread(c - 1)
                outputs(c - 1)

    def scalar(act):
        for n in range(4):
            act.wait_ge(prod, n + 1)
            nc.scalar.activation(wrf[:, 4 * n:4 * n + 4, :].rearrange("p a b -> p (a b)"), m.ps[:, n % 2, :], ACT.Copy).then_inc(prod_out, 1)

    def scalar_main(act):
        def s_copy(b):
            act.wait_ge(s_mm, b + 1)
            for q in range(3):
                k = min(3, RT - 3 * q)
                cp = nc.scalar.activation(s_sb[:, b, 3 * q:3 * q + k, :].rearrange("p a b -> p (a b)"), m.ps[:, 4 + q, 0:k * SW], ACT.Copy)
            cp.then_inc(s_out, 1)

        for n in range(NT):
            act.wait_ge(k_mm, n + 1)
            nc.scalar.activation(phik[:, n % 2, :].rearrange("p (a b) -> p a b", a=2), m.ps[:, 2 * (n % 2):2 * (n % 2) + 2, :],
                                 ACT.Relu).then_inc(k_relu, 1)
            if n == TB:
                s_copy(0)
        s_copy(1)

        def relu_q(c, rs):
            for r in rs:
                n = c * RT + r
                act.wait_ge(q_mm, n + 1)
                nc.scalar.activation(phiq[:, c % 2, r, :], m.ps[:, n % 2, :], ACT.Relu).then_inc(q_relu, 1)

        def tail_copy(b, dst, n):
            act.wait_ge(tail_mm, n)
            nc.scalar.activation(dst.rearrange("p (a b) c -> p a (b c)", a=2), m.ps[:, 6:8, :], ACT.Copy).then_inc(tail_act, 1)

        for c in range(NC):
            b = c // (NC // B)
            relu_q(c, range(0, 2))
            if c == 0:
                tail_copy(0, sT[:, :, :], 1)
            relu_q(c, range(2, 4))
            relu_q(c, range(4, RT))
            if c % (NC // B) == 0:
                tail_copy(b, mix[:, b, :, :], 3 * b + 3)
            if c == 1:
                tail_copy(1, sT[:, :, :], 4)

    def vector(dve):
        def knorms(b):
            dve.wait_ge(s_out, b + 1)
            nc.vector.tensor_tensor(knorm[:, b, :, :], kmask[:, :, :], s_sb[:, b, :, D:SW].broadcast_to([P, RT, 32]), ALU.mult).then_inc(knorm_set, 1)

        def mask_kv(b):
            dve.wait_ge(tail_mm, 3 * b + 2)
            nc.vector.tensor_tensor(kv[:, :, :], m.ps[:, 6:8, :].rearrange("p a (b c) -> p (a b) c", c=P),
                                    blocks[:, :].unsqueeze(1).broadcast_to([P, RT, P]), ALU.mult).then_inc(tail_dve, 1)

        def reciprocals(c):
            dve.wait_ge(n_mm, c + 1)
            if c >= 2:
                dve.wait_ge(b_mm, (c - 1) * RT)
            nc.vector.tensor_scalar(rn[:, c % 2, :], m.ps[:, 2, :], 1e-6, None, ALU.add).then_inc(n_eps, 1)
            dve.wait_ge(n_eps, c + 1)
            nc.vector.reciprocal(rn[:, c % 2, :], rn[:, c % 2, :]).then_inc(n_rec, 1)

        def scale(c):
            for r in range(RT):
                n = c * RT + r
                dve.wait_ge(b_mm, n + 1)
                nc.vector.tensor_tensor(phiq[:, c % 2, r, :], m.ps[:, 3 + n % 2, :], phiq[:, c % 2, r, :], ALU.mult).then_inc(scaled, 1)

        def add(c):
            dve.wait_ge(o_mm, c + 1)
            dve.wait_ge(m.biased, norm.biased_value(c))
            xs = m.x[:, c * TPC:(c + 1) * TPC, :]
            nc.vector.tensor_tensor(xs, m.ps[:, 5, :].rearrange("p (j d) -> p j d", d=D), xs, ALU.add).then_inc(x_done, 1)

        knorms(0)
        knorms(1)
        for c in range(NC + 1):
            if c < NC and c % (NC // B) == 0:
                mask_kv(c // (NC // B))
            if c < NC:
                reciprocals(c)
            if c:
                scale(c - 1)
                add(c - 1)

    return Part([(x_done, norm.done(c)) for c in range(NC)], tensor=tensor, vector=vector, scalar=scalar_main, sync=sync,
                before_norm={"tensor": before_norm, "scalar": scalar}, bias="L3_attn_b_out")


def l3_ffn(nc, m, w_dram, gate_dram, sem, sb, norm):
    E, F = 8, 512
    FT = F // P
    W1, W3, W2 = 0, F, 2 * F
    w = sb("l3f_w", [P, 2, 3 * F])
    gate = sb("l3f_gate", [P, E])
    sg = sb("l3f_sg", [P, 2, CH])
    hT = sb("l3f_hT", [P, 2, FT, CH])
    r = router_buffers(sb, "l3f", E)
    keep1, keep2, e1, e2, wte = (sb(f"l3f_{n}", [P, NT, E]) for n in ("keep1", "keep2", "e1", "e2", "wte"))
    d1, d2, fac = (sb(f"l3f_{n}", [P, NT, E]) for n in ("d1", "d2", "fac"))
    z1, z2 = sb("l3f_z1", [P, NT]), sb("l3f_z2", [P, NT])

    gate_in = sem("l3f_gate_in")
    w_in = [sem(f"l3f_w_in{u}") for u in range(2)]
    logits = sem("l3f_logits")
    step = sem("l3f_step")
    shifted = sem("l3f_shifted")
    exps = sem("l3f_exps")
    gate_done = sem("l3f_gate_done")
    up_done = sem("l3f_up_done")
    sg_done = sem("l3f_sg_done")
    h_done = sem("l3f_h_done")
    down_done = sem("l3f_down_done")
    y_done = sem("l3f_y_done")

    def load(sp, slot, e):
        return sp.dma_start(w[:, slot, :], w_dram[bass.ds(e, 1), :, :].rearrange("e p n -> p (e n)")).then_inc(w_in[slot], 16)

    def sync(sp):
        sp.dma_start(gate[:, :], gate_dram).then_inc(gate_in, 16)
        load(sp, 0, 0)
        load(sp, 1, 1)
        with sp.Fori(1, E // 2) as i:
            for u in range(2):
                sp.wait_ge(down_done, i * (2 * NC) + NC * (u - 1))
                load(sp, u, i * 2 + u)

    def tensor(pe):
        pe.wait_ge(gate_in, 16)
        for t in range(NT):
            if t % TPC == 0:
                pe.wait_ge(m.ln_xnT, norm.value(t // TPC))
            last = nc.tensor.matmul(m.ps[:, 5, t * E:(t + 1) * E], m.xnT[:, t * P:(t + 1) * P], gate[:, :], start=True, stop=True)
        last.then_inc(logits, 1)

        def gates(i, k):
            u, c = divmod(k, NC)
            if c == 0:
                pe.wait_ge(w_in[u], (i + 1) * 16)
            for f in range(FT):
                s = k * FT + f
                pair = 2 * (s % 2)
                cs = slice(c * CH, (c + 1) * CH)
                pe.wait_ge(h_done, i * (2 * NC * FT) + (s + 1))
                nc.tensor.matmul(m.ps[:, pair, :], w[:, u, W1 + f * P:W1 + (f + 1) * P], m.xnT[:, cs],
                                 start=True, stop=True).then_inc(gate_done, 1)
                nc.tensor.matmul(m.ps[:, pair + 1, :], w[:, u, W3 + f * P:W3 + (f + 1) * P], m.xnT[:, cs],
                                 start=True, stop=True).then_inc(up_done, 1)

        def down(i, k):
            u, c = divmod(k, NC)
            pe.wait_ge(y_done, i * (2 * NC) + (k + 1))
            for f in range(FT):
                pe.wait_ge(h_done, i * (2 * NC * FT) + (k * FT + f + 1 + 2))
                for j in range(TPC):
                    last = nc.tensor.matmul(m.ps[:, 4 + k % 2, j * P:(j + 1) * P], hT[:, k % 2, f, j * P:(j + 1) * P],
                                            w[:, u, W2 + f * P:W2 + (f + 1) * P], start=(f == 0 and j == 0),
                                            stop=(f == FT - 1), skip_group_check=True)
            last.then_inc(down_done, 1)

        pe.wait_ge(step, 1)
        with pe.Fori(0, E // 2) as i:
            for k in range(2 * NC):
                gates(i, k)
                if k:
                    down(i, k - 1)
            down(i, 2 * NC - 1)

    def scalar(act):
        act.wait_ge(shifted, 1)
        nc.scalar.activation(e1[:, :, :], d1[:, :, :], ACT.Exp, scale=-1.0).then_inc(exps, 1)
        act.wait_ge(shifted, 2)
        nc.scalar.activation(e2[:, :, :], d2[:, :, :], ACT.Exp, scale=-1.0).then_inc(exps, 1)
        with act.Fori(0, E // 2) as i:
            for s in range(2 * NC * FT):
                act.wait_ge(gate_done, i * (2 * NC * FT) + (s + 1))
                nc.scalar.activation(sg[:, s % 2, :], m.ps[:, 2 * (s % 2), :], ACT.Silu).then_inc(sg_done, 1)

    def vector(dve):
        dve.sem_inc(h_done, 2)
        dve.sem_inc(y_done, 2)
        dve.wait_ge(logits, 1)
        n = [0]

        def then(ins):
            ins.then_inc(step, 1)
            n[0] += 1
            dve.wait_ge(step, n[0])

        L = r.logits
        then(nc.vector.tensor_copy(L[:, :, :].rearrange("p t e -> p (t e)"), m.ps[:, 5, 0:NT * E]))
        ranks(nc, then, m, r, E)
        bc = lambda a: a.unsqueeze(2).broadcast_to([P, NT, E])
        nc.vector.tensor_tensor(d1[:, :, :], bc(r.first[:, :]), L[:, :, :], ALU.subtract).then_inc(shifted, 1)
        then(nc.vector.tensor_tensor(d2[:, :, :], bc(r.second[:, :]), L[:, :, :], ALU.subtract))
        nc.vector.tensor_scalar(d2[:, :, :], d2[:, :, :], 0.0, None, ALU.max).then_inc(shifted, 1)
        then(nc.vector.scalar_tensor_tensor(out=fac[:, :, :], in0=L[:, :, :], scalar=-1.0, in1=L[:, :, :], op0=ALU.mult, op1=ALU.max))
        then(nc.vector.tensor_tensor(keep1[:, :, :], fac[:, :, :], bc(r.first[:, :]), ALU.max))
        then(nc.vector.tensor_tensor(keep2[:, :, :], fac[:, :, :], bc(r.second[:, :]), ALU.max))
        then(nc.vector.scalar_tensor_tensor(out=keep1[:, :, :], in0=keep1[:, :, :], scalar=0.02, in1=d1[:, :, :], op0=ALU.mult, op1=ALU.is_ge))
        then(nc.vector.scalar_tensor_tensor(out=keep2[:, :, :], in0=keep2[:, :, :], scalar=0.02, in1=d2[:, :, :], op0=ALU.mult, op1=ALU.is_ge))
        then(nc.vector.tensor_tensor(keep2[:, :, :], keep2[:, :, :], r.is_first[:, :, :], ALU.is_gt))
        dve.wait_ge(exps, 2)
        then(nc.vector.tensor_tensor(keep1[:, :, :], keep1[:, :, :], e1[:, :, :], ALU.mult))
        then(nc.vector.tensor_tensor(keep2[:, :, :], keep2[:, :, :], e2[:, :, :], ALU.mult))
        then(nc.vector.tensor_reduce(z1[:, :], keep1[:, :, :], AX.X, ALU.add))
        then(nc.vector.tensor_reduce(z2[:, :], keep2[:, :, :], AX.X, ALU.add))
        then(nc.vector.reciprocal(z1[:, :], z1[:, :]))
        then(nc.vector.reciprocal(z2[:, :], z2[:, :]))
        then(nc.vector.tensor_tensor(wte[:, :, :], r.is_first[:, :, :], bc(z1[:, :]), ALU.mult))
        then(nc.vector.tensor_tensor(e2[:, :, :], r.is_second[:, :, :], bc(z2[:, :]), ALU.mult))
        then(nc.vector.tensor_tensor(wte[:, :, :], wte[:, :, :], e2[:, :, :], ALU.add))

        def outputs(i, k):
            u, c = divmod(k, NC)
            dve.wait_ge(down_done, i * (2 * NC) + (k + 1))
            dve.wait_ge(y_done, i * (2 * NC) + (k + 1))
            for j in range(TPC):
                t = c * TPC + j
                last = nc.vector.scalar_tensor_tensor(out=m.x[:, t, :], in0=m.ps[:, 4 + k % 2, j * P:(j + 1) * P],
                                                      scalar=wte[:, t, bass.ds(i * 2 + u, 1)], in1=m.x[:, t, :],
                                                      op0=ALU.mult, op1=ALU.add)
            last.then_inc(y_done, 1)

        with dve.Fori(0, E // 2) as i:
            for k in range(2 * NC):
                for f in range(FT):
                    s = k * FT + f
                    dve.wait_ge(up_done, i * (2 * NC * FT) + (s + 1))
                    dve.wait_ge(sg_done, i * (2 * NC * FT) + (s + 1))
                    nc.vector.tensor_tensor(hT[:, k % 2, f, :], m.ps[:, 2 * (s % 2) + 1, :], sg[:, s % 2, :],
                                            ALU.mult).then_inc(h_done, 1)
                if k:
                    outputs(i, k - 1)
            outputs(i, 2 * NC - 1)

    total = E * NC
    return Part([(y_done, total - NC + c + 1 + 2) for c in range(NC)], tensor=tensor, vector=vector, scalar=scalar, sync=sync)


class Router:
    pass


def router_buffers(sb, name, E):
    r = Router()
    r.logits, r.rank, r.is_first, r.is_second, r.tmp = (
        sb(f"{name}_{n}", [P, NT, E]) for n in ("logits", "rank", "is_first", "is_second", "tmp"))
    r.greater = sb(f"{name}_greater", [P, NT * E, E])
    r.equal = sb(f"{name}_equal", [P, NT * E, E])
    r.first, r.second = sb(f"{name}_first", [P, NT]), sb(f"{name}_second", [P, NT])
    return r


def ranks(nc, then, m, r, E):
    L = r.logits
    flat = L[:, :, :].rearrange("p t e -> p (t e)")
    own = flat.unsqueeze(2).broadcast_to([P, NT * E, E])
    other = L[:, :, :].unsqueeze(2).broadcast_to([P, NT, E, E])
    grid = lambda a: a[:, :, :].rearrange("p (t i) j -> p t i j", i=E)
    own4 = L[:, :, :].unsqueeze(3).broadcast_to([P, NT, E, E])
    lower = m.lower[:, 0:E, 0:E].unsqueeze(1).broadcast_to([P, NT, E, E])
    nc.vector.tensor_tensor(grid(r.greater), other, own4, ALU.is_gt)
    then(nc.vector.tensor_tensor(grid(r.equal), other, own4, ALU.is_equal))
    then(nc.vector.tensor_tensor(grid(r.equal), grid(r.equal), lower, ALU.mult))
    then(nc.vector.tensor_tensor(r.greater[:, :, :], r.greater[:, :, :], r.equal[:, :, :], ALU.add))
    then(nc.vector.tensor_reduce(r.rank[:, :, :].rearrange("p t e -> p (t e)"), r.greater[:, :, :], AX.X, ALU.add))
    nc.vector.tensor_scalar(r.is_first[:, :, :], r.rank[:, :, :], 0.0, None, ALU.is_equal)
    then(nc.vector.tensor_scalar(r.is_second[:, :, :], r.rank[:, :, :], 1.0, None, ALU.is_equal))
    nc.vector.tensor_reduce(r.first[:, :], L[:, :, :], AX.X, ALU.max)
    then(nc.vector.tensor_tensor(r.tmp[:, :, :], r.is_second[:, :, :], L[:, :, :], ALU.mult))
    then(nc.vector.tensor_reduce(r.second[:, :], r.tmp[:, :, :], AX.X, ALU.add))


BIASES = ["L0_attn_b_proj", "L1_ffn_base_b", "L2_attn_bo", "L3_attn_b_out"]


ARENAS = [31900, 14200]


class Memory:
    pass


class Arena:

    def __init__(self, area):
        self.area, self.used = area, 0

    def fresh(self):
        self.used = 0
        return self.take

    def take(self, name, shape, dt=F32):
        size = {F32: 4, I32: 4, BF16: 2}[dt]
        words = (int(np.prod(shape[1:])) * size + 31) // 32 * 8
        assert self.used + words <= self.area.shape[1], (name, self.used, words)
        flat = self.area[0:shape[0], self.used:self.used + words]
        self.used += words
        flat = (flat if dt == F32 else flat.bitcast(dt))[:, 0:int(np.prod(shape[1:]))]
        if len(shape) == 2:
            return flat
        names = "abcd"[:len(shape) - 1]
        return flat.rearrange(f"p ({' '.join(names)}) -> p {' '.join(names)}", **{n: k for n, k in zip(names[1:], shape[2:])})


def program(nc, A, out, parts):
    with ExitStack() as ctx:
        def sb(name, shape, dt=F32):
            return ctx.enter_context(nc.sbuf_tensor(name, shape, dt))

        def sem(name):
            return ctx.enter_context(nc.semaphore(name))

        m = Memory()
        m.ps = ctx.enter_context(nc.psum_tensor("ps", [P, 8, 512], F32))
        m.psf = m.ps[:, :, :].rearrange("p b n -> p (b n)")
        m.ps7b = m.ps[:, 7, :].bitcast(BF16)
        m.x = sb("x", [P, NT, D])
        m.xn1 = sb("xn1", [P, NT, D + 1])
        m.xn = m.xn1[:, :, 0:D]
        m.xnT = sb("xnT", [P, T])
        m.ident = sb("ident", [P, P])
        m.lower = sb("lower", [P, 8, 8])
        m.stats = sb("stats", [P, NT, 6])
        m.meanvar = sb("meanvar", [P, NT, 2])
        m.vareps = sb("vareps", [P, NT])
        m.rstd = sb("rstd", [P, NT])
        m.power = sb("power", [P, NT])
        m.bias = sb("bias", [P, len(BIASES), D])
        m.consts_in, m.x_in, m.set_up, m.out_written = sem("consts_in"), [sem(f"x_in{c}") for c in range(NC)], sem("set_up"), sem("out_written")
        m.ln_stats, m.ln_var, m.ln_rstd = sem("ln_stats"), sem("ln_var"), sem("ln_rstd")
        m.biased, m.x_done = sem("biased"), sem("x_done")
        m.ln_xn, m.ln_turned, m.ln_xnT = sem("ln_xn"), sem("ln_turned"), sem("ln_xnT")

        m.bias_of = {name: m.bias[:, n, :] for n, name in enumerate(BIASES)}
        arenas = [Arena(sb("arena0", [P, ARENAS[0]])), Arena(sb("arena1", [P, ARENAS[1]]))]
        start = Part([(m.x_in[c], 16) for c in range(NC)])
        built = []
        for k, name in enumerate(parts):
            sb = arenas[k % 2].fresh()
            norm = Norm(nc, m, k, built[-1][1] if built else start, sum(p.bias is not None for _, p in built),
                        sum(p.ready[0][0] is m.x_done for _, p in built))
            if name == "l0_attn":
                part = l0_attn(nc, m, A, sem, sb, norm)
            if name == "l0_ffn":
                part = l0_ffn(nc, m, A, sem, sb, norm)
            if name == "l1_attn":
                part = l1_attn(nc, m, A, sem, sb, norm)
            if name == "l1_ffn":
                part = l1_ffn(nc, m, A, sem, sb, norm)
            if name == "l2_attn":
                part = l2_attn(nc, m, A, sem, sb, norm)
            if name == "l2_ffn":
                part = l2_ffn(nc, m, A, sem, sb, norm)
            if name == "l3_attn":
                part = l3_attn(nc, m, A, sem, sb, norm)
            if name == "l3_ffn":
                part = l3_ffn(nc, m, A["L3_ffn_w"], A["L3_ffn_gate_w"], sem, sb, norm)
            built.append((norm, part))
        last = built[-1][1]
        block = ctx.enter_context(nc.Block())

        @block.sync
        def _(sp):
            x_view = A["x"].rearrange("(t p) d -> p t d", p=P)
            for c in range(NC):
                sp.dma_start(m.x[:, c * TPC:(c + 1) * TPC, :], x_view[:, c * TPC:(c + 1) * TPC, :]).then_inc(m.x_in[c], 16)
            sp.dma_start(m.ident[:, :], A["ident"]).then_inc(m.consts_in, 16)
            sp.dma_start(m.lower[:, :, :].rearrange("p i j -> p (i j)"), A["lower"]).then_inc(m.consts_in, 16)
            for n, name in enumerate(BIASES):
                m_bias = m.bias[:, n, :]
                sp.dma_start(m_bias, A[name].broadcast_to([P, D])).then_inc(m.consts_in, 16)
            for k, (norm, part) in enumerate(built):
                if k >= 2:
                    for c in range(NC):
                        sp.wait_ge(*built[k - 2][1].ready[c])
                if part.sync:
                    part.sync(sp)
            out_view = out.rearrange("(t p) d -> p t d", p=P)
            for c in range(NC):
                sp.wait_ge(*last.ready[c])
                sp.dma_start(out_view[:, c * TPC:(c + 1) * TPC, :], m.x[:, c * TPC:(c + 1) * TPC, :]).then_inc(m.out_written, 16)
            sp.wait_ge(m.out_written, 16 * NC)

        @block.tensor
        def _(pe):
            for norm, part in built:
                if "tensor" in part.before_norm:
                    part.before_norm["tensor"](pe)
                norm.tensor(pe)
                if part.tensor:
                    part.tensor(pe)

        @block.vector
        def _(dve):
            for norm, part in built:
                if "vector" in part.before_norm:
                    part.before_norm["vector"](dve)
                norm.vector(dve)
                if part.vector:
                    part.vector(dve)

        @block.scalar
        def _(act):
            for norm, part in built:
                if "scalar" in part.before_norm:
                    part.before_norm["scalar"](act)
                norm.scalar(act)
                if part.scalar:
                    part.scalar(act)

        @block.gpsimd
        def _(pool):
            nc.gpsimd.memset(m.xn1[:, :, D:D + 1], 1.0).then_inc(m.set_up, 1)
            nc.gpsimd.memset(m.power[:, :], -0.5).then_inc(m.set_up, 1)
            pool.wait_ge(m.consts_in, 16 * (2 + len(BIASES)))
            for norm, part in built:
                if "gpsimd" in part.before_norm:
                    part.before_norm["gpsimd"](pool)
                norm.gpsimd(pool, m.bias_of.get(part.bias))
                if part.gpsimd:
                    part.gpsimd(pool)


ALL_PARTS = ["l0_attn", "l0_ffn", "l1_attn", "l1_ffn", "l2_attn", "l2_ffn", "l3_attn", "l3_ffn"]


def layouts(a):
    c = np.ascontiguousarray
    f = {}
    f["x"] = c(a["L0_attn_hidden_states"]).reshape(T, D)
    f["ident"] = np.eye(P, dtype=np.float32)
    f["lower"] = c(np.broadcast_to(np.tril(np.ones((8, 8), np.float32), -1).reshape(1, 64), (P, 64)))
    up = lambda w: np.asarray(w).transpose(0, 2, 1)
    down = lambda w: np.asarray(w).transpose(0, 2, 1).reshape(w.shape[0], -1, P, D).transpose(0, 2, 1, 3).reshape(w.shape[0], P, -1)
    f["L3_ffn_w"] = c(np.concatenate([up(a["L3_ffn_w1"]), up(a["L3_ffn_w3"]), down(a["L3_ffn_w2"])], axis=2))
    f["L3_ffn_gate_w"] = c(np.asarray(a["L3_ffn_gate_w"]).T)
    w = np.asarray(a["L0_attn_w_attn"])
    f["L0_attn_w"] = c(w.reshape(D, 3, D))
    f["L0_attn_wo"] = c(a["L0_attn_w_proj"])
    f["L0_attn_bqk"] = c(np.asarray(a["L0_attn_b_attn"])[:256].reshape(2, D).T)
    f["L0_attn_bv"] = c(np.asarray(a["L0_attn_b_attn"])[256:]).reshape(1, D)
    away = np.arange(P)[:, None] - np.arange(S)[None, :] + S - P
    f["L0_attn_weight"] = np.where(away >= 0, 1 / (np.maximum(away, 0) + 1.0), 0).astype(np.float32)
    bf16 = np.dtype("bfloat16")
    f["L0_attn_ident"] = np.eye(P).astype(bf16)
    before = np.where(np.tril(np.ones((P, P)), -1) > 0, -1e30, 0)
    f["L0_attn_before"] = c(np.stack([before, before.T], axis=1)).astype(bf16)
    ones = np.zeros((2, 32, S))
    ones[0, 0:3], ones[1, 3:6] = 1, 1
    f["L0_attn_ones"] = ones.astype(bf16)
    f["L0_ffn_w"] = c(np.stack([np.asarray(a["L0_ffn_w_gate"]).T, np.asarray(a["L0_ffn_w_up"]).T,
                                np.asarray(a["L0_ffn_w_down"]).T.reshape(3, P, D).transpose(1, 0, 2).reshape(P, 384)], axis=1))
    f["L1_attn_wqk"] = c(np.stack([a["L1_attn_Wq"], a["L1_attn_Wk"]], axis=1))
    f["L1_attn_wkvT"] = c(np.stack([np.asarray(a["L1_attn_Wk"]).T, np.asarray(a["L1_attn_Wv"]).T], axis=1))
    f["L1_attn_bcol"] = c(np.stack([a["L1_attn_bq"], a["L1_attn_bk"]], axis=1))
    f["L1_attn_bkv"] = c(np.stack([a["L1_attn_bk"], a["L1_attn_bv"]], axis=0))
    theta = (np.float32(1) / (np.power(np.float32(10000.0), np.arange(0, 8, 2, dtype=np.float32)) / np.float32(8))).astype(np.float32)
    theta = np.concatenate([theta, theta])
    turn = np.zeros((8, 8), np.float32)
    for j in range(8):
        turn[j, j] += np.cos(theta[j])
        turn[(j + 4) % 8, j] += np.sin(theta[j]) * (-1 if j < 4 else 1)
    f["L1_attn_rope"] = np.kron(np.eye(16, dtype=np.float32), turn)
    ra, rbm = np.asarray(a["L1_ffn_routed_A"]), np.asarray(a["L1_ffn_routed_B"])
    f["L1_ffn_wa"] = c(np.concatenate([ra.reshape(96, D), a["L1_ffn_shared_A"], a["L1_ffn_router_W"]], axis=0).T)
    f["L1_ffn_wb"] = c(np.concatenate([rbm.transpose(0, 2, 1).reshape(96, D), np.asarray(a["L1_ffn_shared_B"]).T], axis=0))
    f["L1_ffn_base"] = c(np.asarray(a["L1_ffn_base_W"]).T)
    f["L1_ffn_rb"] = c(a["L1_ffn_router_b"]).reshape(1, 6)
    f["causal"] = np.triu(np.ones((P, P), np.float32))
    f["hmask"] = np.kron(np.eye(16, dtype=np.float32), np.ones((8, 1), np.float32))
    f["L2_attn_w"] = c(np.stack([np.asarray(a[f"L2_attn_W{n}"]).T for n in "qkv"], axis=1))
    f["L2_attn_wo"] = c(np.asarray(a["L2_attn_Wo"]).T)
    f["L2_attn_bqk"] = c(np.stack([a["L2_attn_bq"], a["L2_attn_bk"]], axis=1))
    f["L2_attn_bv"] = c(a["L2_attn_bv"]).reshape(1, D)
    b1 = np.asarray(a["L2_ffn_b1"]).reshape(8, 2, P).transpose(0, 2, 1)
    f["L2_ffn_w"] = c(np.concatenate([np.asarray(a["L2_ffn_w1"]), down(np.asarray(a["L2_ffn_w2"]).transpose(0, 2, 1)), b1], axis=2))
    f["L2_ffn_gate_w"] = c(a["L2_ffn_gate_w"])
    f["L2_ffn_ln_b"] = c(a["L2_ffn_ln_b"])
    f["L2_ffn_b2"] = c(a["L2_ffn_b2"]).reshape(1, -1)
    f["L2_ffn_ln_g"] = c(a["L2_ffn_ln_g"]).reshape(1, -1)
    w = np.asarray(a["L3_attn_W_qkv"])
    f["L3_attn_wqkT"] = c(w[:, :2048].T.reshape(16, P, D).transpose(1, 0, 2))
    rf = np.zeros((8, 2, 64, 2, 64), np.float32)
    for h in range(2):
        rf[:, h, :, h, :] = np.asarray(a["L3_attn_RF"])[h::2]
    f["L3_attn_rf"] = c(rf.reshape(8, P, P).transpose(1, 0, 2))
    f["L3_attn_wv"] = c(w[:, 2048:].reshape(D, 8, P))
    f["L3_attn_wout"] = c(np.asarray(a["L3_attn_W_out"]).reshape(8, P, D).transpose(1, 0, 2))
    sel, kmask = np.zeros((P, 8, P), np.float32), np.zeros((P, 8, 32), np.float32)
    for r in range(8):
        for h in range(2):
            sel[32 * (r % 4) + 2 * (r // 4) + h, r, 64 * h:64 * h + 64] = 1
            kmask[64 * h:64 * h + 64, r, 2 * (r // 4) + h] = 1
    f["L3_attn_sel"], f["L3_attn_kmask"] = sel, kmask
    f["L3_attn_blocks"] = np.kron(np.eye(2, dtype=np.float32), np.ones((64, 64), np.float32))
    for name in BIASES:
        f[name] = c(a[name]).reshape(1, D)
    return f


def kernel(**inputs):
    import concourse.bacc as bacc
    from concourse.bass_utils import run_bass_kernel_spmd

    nc = bacc.Bacc("TRN2", target_bir_lowering=False, num_devices=1)
    arrays = {f"in_{k}": v for k, v in layouts(inputs).items()}
    A = {k[3:]: nc.dram_tensor(k, v.shape, mybir.dt.from_np(v.dtype), kind="ExternalInput").ap() for k, v in arrays.items()}
    out = nc.dram_tensor("out", (T, D), F32, kind="ExternalOutput").ap()
    program(nc, A, out, ALL_PARTS)
    r = run_bass_kernel_spmd(nc, [arrays], core_ids=[0])
    return r.results[0]["out"].reshape(B, S, D)
```

```python
from contextlib import ExitStack

import numpy as np

import concourse.bass as bass
from concourse import mybir

F32 = mybir.dt.float32
BF16 = mybir.dt.bfloat16
F32R = mybir.dt.float32r
I32 = mybir.dt.int32
ALU = mybir.AluOpType
ACT = mybir.ActivationFunctionType
AX = mybir.AxisListType

P = 128
B, S, D = 2, 1024, 128
T = B * S
NT = T // P
CH = 512
NC = T // CH
TPC = CH // P
LN_EPS = 1e-5


class Part:

    def __init__(self, ready, tensor=None, vector=None, scalar=None, gpsimd=None, sync=None,
                 before_norm=None, bias=None, early=True):
        self.ready, self.before_norm, self.bias, self.early = ready, before_norm or {}, bias, early
        self.tensor, self.vector, self.scalar, self.gpsimd, self.sync = tensor, vector, scalar, gpsimd, sync


class Norm:

    def __init__(self, nc, m, k, before, biased, counted):
        self.nc, self.m, self.k, self.before, self.biased, self.counted = nc, m, k, before, biased, counted
        self.early = before.early
        self.banks, self.bias_late = (6, 7), False
        self.split, self.splits_before = None, m.splits
        self.counted_stats = self.counted_xn = self.turned = self.copied = 0

    def value(self, c):
        return NC * self.k + c + 1

    def biased_value(self, c):
        return NC * self.biased + c + 1

    def split_xnT(self):
        self.split = tuple(self.m.rounded.take(name, [P, T], F32R) for name in ("x_high", "x_low"))
        self.m.splits += 1
        return self.split

    def split_value(self, c):
        return NC * self.splits_before + c + 1

    def loads(self, n):
        area = self.k % 2
        self.m.loads[area] += n
        return self.m.loaded[area], 16 * self.m.loads[area]

    def done(self, c):
        return NC * self.counted + c + 1

    def after(self, dve, c):
        self.statistics(dve, c)
        if c and self.early:
            self.normalise(dve, c - 1)

    def vector(self, dve):
        while self.counted_stats < NC:
            self.statistics(dve, self.counted_stats)
        while self.counted_xn < NC:
            self.normalise(dve, self.counted_xn)

    def statistics(self, dve, c):
        nc, m = self.nc, self.m
        assert c == self.counted_stats
        self.counted_stats += 1
        dve.wait_ge(*self.before.ready[c])
        for t in range(c * TPC, (c + 1) * TPC):
            last = nc.vector.bn_stats(m.stats[:, t, :], m.x[:, t, :])
        last.then_inc(m.ln_var, 1)
        dve.wait_ge(m.ln_var, 2 * self.value(c) - 1)
        for t in range(c * TPC, (c + 1) * TPC):
            last = nc.vector.bn_aggr(m.meanvar[:, t, :], m.stats[:, t, :])
        last.then_inc(m.ln_var, 1)

    def normalise(self, dve, c):
        nc, m = self.nc, self.m
        self.counted_xn += 1
        dve.wait_ge(m.ln_rstd, 2 * self.value(c))
        for t in range(c * TPC, (c + 1) * TPC):
            last = nc.vector.tensor_scalar(m.xn[:, t, :], m.x[:, t, :], m.meanvar[:, t, 0:1],
                                           m.rstd[:, t:t + 1], ALU.subtract, ALU.mult)
        last.then_inc(m.ln_xn, 1)

    def gpsimd(self, pool, bias):
        nc, m = self.nc, self.m
        if self.k == 0:
            pool.wait_ge(m.set_up, 2)
        for c in range(NC):
            ts = slice(c * TPC, (c + 1) * TPC)
            pool.wait_ge(m.ln_var, 2 * self.value(c))
            nc.gpsimd.tensor_scalar(m.vareps[:, ts], m.meanvar[:, ts, 1], LN_EPS, None, ALU.add).then_inc(m.ln_rstd, 1)
            pool.wait_ge(m.ln_rstd, 2 * self.value(c) - 1)
            nc.gpsimd.tensor_tensor(m.rstd[:, ts], m.vareps[:, ts], m.power[:, ts], ALU.pow).then_inc(m.ln_rstd, 1)
        for c in range(NC):
            if self.split:
                cs = slice(c * CH, (c + 1) * CH)
                high, low = self.split
                pool.wait_ge(m.x_high_set, self.split_value(c))
                nc.gpsimd.tensor_tensor(low[:, cs], m.xnT[:, cs], high[:, cs].bitcast(F32), ALU.subtract).then_inc(m.x_low_set, 1)
            if bias is not None and not self.bias_late:
                self.add_bias(pool, bias, c)

    def add_bias(self, pool, bias, c):
        nc, m = self.nc, self.m
        if c == 0 and self.k == 0:
            pool.wait_ge(m.consts_in, 16 * (2 + len(BIASES)))
        xs = m.x[:, c * TPC:(c + 1) * TPC, :]
        pool.wait_ge(m.ln_xn, self.value(c))
        nc.gpsimd.tensor_tensor(xs, xs, bias.unsqueeze(1).broadcast_to([P, TPC, D]), ALU.add).then_inc(m.biased, 1)

    def wait_xnT(self, pe, c):
        nc, m = self.nc, self.m
        if self.turned == 0:
            pe.wait_ge(*self.before.ready[NC - 1])
            if self.k == 0:
                pe.wait_ge(m.set_up, 2)
                pe.wait_ge(m.consts_in, 16 * (2 + len(BIASES)))
        while self.turned < min(c + 2, NC):
            n = self.turned
            pe.wait_ge(m.ln_xn, self.value(n))
            if n >= len(self.banks):
                pe.wait_ge(m.ln_xnT, self.value(n - len(self.banks)))
            for j in range(TPC):
                last = nc.tensor.transpose(m.ps[:, self.banks[n % len(self.banks)], j * P:(j + 1) * P], m.xn[:, n * TPC + j, :], m.ident[:, :])
            last.then_inc(m.ln_turned, 1)
            self.turned += 1
        pe.wait_ge(m.ln_xnT, self.value(c))
        if self.split:
            pe.wait_ge(m.x_low_set, self.split_value(c))

    def copy_xnT(self, act, c):
        nc, m = self.nc, self.m
        while self.copied < min(c + 1, NC):
            n = self.copied
            act.wait_ge(m.ln_turned, self.value(n))
            nc.scalar.activation(m.xnT[:, n * CH:(n + 1) * CH], m.ps[:, self.banks[n % len(self.banks)], :], ACT.Copy).then_inc(m.ln_xnT, 1)
            if self.split:
                act.wait_ge(m.ln_xnT, self.value(n))
                nc.scalar.activation(self.split[0][:, n * CH:(n + 1) * CH], m.xnT[:, n * CH:(n + 1) * CH], ACT.Copy).then_inc(m.x_high_set, 1)
            self.copied += 1


def l0_attn(nc, m, A, sem, sb, norm):
    H, HD, PAD, GH = 16, 8, 32, 4
    G = H // GH
    UNITS = B * G
    TB = S // P
    QC = S // CH
    SLOTS_Q, SLOTS_K = (0, 0, 0, 1, 1, 2), (0, 1, 2, 1, 0, 0)
    RUNS = [[(0, 0, 1, 3), (1, 3, 1, 2), (2, 5, 1, 1)], [(0, 0, 1, 1), (0, 4, 1, 2), (1, 1, 2, 2), (2, 2, 1, 1)]]
    STACKED = HD * len(SLOTS_Q)
    ROWS = 96
    SCALE = HD ** -0.5
    BUFS, RING, LAG, SETTLE = 3, 10, 7, 11
    w = sb("l0a_w", [P, 3, D])
    wo = sb("l0a_wo", [P, D])
    bqk = sb("l0a_bqk", [P, 2])
    bv = sb("l0a_bv", [P, D])
    weight = sb("l0a_weight", [P, S])
    identb = sb("l0a_identb", [P, P], BF16)
    before = sb("l0a_before", [P, 2, P], BF16)
    parts = sb("l0a_parts", [P, 3, 2, 2 * CH], BF16)
    vpad = sb("l0a_vpad", [P, NT, H, PAD])
    qs = sb("l0a_qs", [P, BUFS, GH, S], BF16)
    ks = sb("l0a_ks", [P, BUFS, GH, S], BF16)
    negmax = sb("l0a_negmax", [P, 2, GH, TB])
    nrest = sb("l0a_nrest", [P, GH, TB])
    nparts = sb("l0a_nparts", [P, 2, TB, GH * 3], BF16)
    mrows = sb("l0a_mrows", [GH * 3, 2, S], BF16)
    ring = sb("l0a_ring", [P, RING - NC, CH])
    numT = sb("l0a_numT", [P, 2, CH])
    rest = numT
    rec = sb("l0a_rec", [P, 2, TPC * GH])
    o = m.xn
    oT = numT[:, 0, :]

    scratch = A["scratch"]
    parts_out = [sem(f"l0a_parts_out{b}") for b in range(B)]
    w_in, w_all = norm.loads(7)
    zeroed, v_zeroed, tails_in = sem("l0a_zeroed"), sem("l0a_v_zeroed"), sem("l0a_tails_in")
    p_mm, high_set, rest_set, mid_set, low_set = (sem(f"l0a_{n}") for n in ("p_mm", "high_set", "rest_set", "mid_set", "low_set"))
    v_mm, v_set = sem("l0a_v_mm"), sem("l0a_v_set")
    stack_in = [sem(f"l0a_stack_in{n}") for n in range(BUFS)]
    mrows_in = [sem(f"l0a_mrows_in{n}") for n in range(BUFS)]
    a_mm, max_set, nsplit, nparts_set, n_turned, mrows_set = (sem(f"l0a_{n}") for n in ("a_mm", "max_set", "nsplit", "nparts_set", "n_turned", "mrows_set"))
    s_mm, exps, weighed_v, weighed_p = (sem(f"l0a_{n}") for n in ("s_mm", "exps", "weighed_v", "weighed_p"))
    pv_mm, num_out, num_turned, rec_set, o_set = (sem(f"l0a_{n}") for n in ("pv_mm", "num_out", "num_turned", "rec_set", "o_set"))
    o_turned, oT_set, y_mm = (sem(f"l0a_{n}") for n in ("o_turned", "oT_set", "y_mm"))
    x_done = m.x_done

    TILES = [(h, i) for i in range(TB) for h in range(GH)]
    STEPS = [(qc, kt, h) for qc in range(QC) for kt in range(TB - 1, TPC * qc - 1, -1) for h in range(GH)]
    NS = len(STEPS)
    DVE_COST = 4.8
    LAST = [max(n for n, s in enumerate(STEPS) if s[0] == qc) for qc in range(QC)]

    A_BANKS, held, free = [], {}, 0
    for k in range(UNITS * len(TILES)):
        n = -(-(S - TILES[k % len(TILES)][1] * P) // CH)
        free = -(-free // n) * n % NC
        A_BANKS.append((free, max(held.get(free + j, -1) for j in range(n))))
        held.update({free + j: k for j in range(n)})
        free = (free + n) % NC

    def probs(k):
        i = k % RING
        return m.xnT[:, i * CH:(i + 1) * CH] if i < NC else ring[:, i - NC, :]

    def width(qc, kt):
        return min(CH, P * (kt + 1) - CH * qc)

    POOL_STEPS, free = set(), [0.0, 0.0]
    for n, (qc, kt, h) in enumerate(STEPS):
        pool_end, dve_end = free[0] + 90 + 2.4 * width(qc, kt), free[1] + 200 + DVE_COST * width(qc, kt)
        if pool_end <= dve_end:
            POOL_STEPS.add(n)
            free[0] = pool_end
        else:
            free[1] = dve_end

    def by_pool(n):
        return n in POOL_STEPS

    def count_v(u, n):
        return u * sum(not by_pool(x) for x in range(NS)) + sum(not by_pool(x) for x in range(n + 1))

    def count_p(u, n):
        return u * NS + n + 1 - count_v(u, n)

    def wait_weighed(eng, u, n):
        if by_pool(n):
            eng.wait_ge(weighed_p, count_p(u, n))
        else:
            eng.wait_ge(weighed_v, count_v(u, n))

    def schedule():
        yield from (("max", 0, n) for n in range(len(TILES)))
        yield from ((what, 0, 0) for what in ("split", "turn_max", "take_max"))
        due = {}
        for u in range(UNITS):
            for n in range(NS):
                at = u * NS + n
                due.setdefault(at, []).insert(0, ("exp", u, n))
                if u + 1 < UNITS:
                    share = [min(len(TILES), len(TILES) * x // (NS - SETTLE)) for x in (n, n + 1)]
                    due[at] += [("max", u + 1, x) for x in range(*share)]
                    due[at] += [(what, u + 1, 0) for late, what in enumerate(("split", "turn_max", "take_max")) if n == NS - SETTLE + late]
                for what, late in (("weigh", 3), ("times_v", LAG)):
                    due.setdefault(at + late, []).append((what, u, n))
                if n in LAST:
                    for what, late in (("take_num", LAG), ("turn_num", LAG + 3), ("divide", LAG + 4)):
                        due.setdefault(at + late, []).append((what, u, LAST.index(n)))
        for at in sorted(due):
            yield from due[at]

    def sync(sp):
        sp.dma_start(w[:, :, :], A["L0_attn_w"]).then_inc(w_in, 16)
        sp.dma_start(wo[:, :], A["L0_attn_wo"]).then_inc(w_in, 16)
        sp.dma_start(bqk[:, :], A["L0_attn_bqk"]).then_inc(w_in, 16)
        sp.dma_start(bv[:, :], A["L0_attn_bv"].broadcast_to([P, D])).then_inc(w_in, 16)
        sp.dma_start(weight[:, :], A["L0_attn_weight"]).then_inc(w_in, 16)
        sp.dma_start(identb[:, :], A["L0_attn_ident"]).then_inc(w_in, 16)
        sp.dma_start(before[:, :, :], A["L0_attn_before"]).then_inc(w_in, 16)
        for buf in range(BUFS):
            sp.dma_start(ks[STACKED:P, buf, :, :], A["L0_attn_tail"].unsqueeze(1).broadcast_to([P - STACKED, GH, S])).then_inc(tails_in, 16)
        for c in range(NC):
            for j in range(2):
                sp.wait_ge(low_set, 2 * c + j + 1)
                for part, slot, step, n in RUNS[j]:
                    dst = scratch[j, slot:slot + step * (n - 1) + 1:step, :, c * CH:(c + 1) * CH].rearrange("s f t -> f s t")
                    src = parts[:, part, j, c % 2 * CH:(c % 2 + 1) * CH].unsqueeze(1).broadcast_to([P, n, CH])
                    sp.dma_start(dst, src).then_inc(parts_out[c // QC], 16)
            if c % QC == QC - 1 and c // QC == 0:
                sp.wait_ge(zeroed, 3)
                stack(sp, 0)
                stack(sp, 1)
        for u in range(UNITS):
            sp.wait_ge(mrows_set, u + 1)
            for h in range(GH):
                sp.dma_start(qs[ROWS:ROWS + 3, u % BUFS, h, :], mrows[3 * h:3 * h + 3, u % 2, :]).then_inc(mrows_in[u % BUFS], 16)
            if u + 2 < UNITS:
                stack(sp, u + 2)

    def stack(sp, u):
        b, g = divmod(u, G)
        sp.wait_ge(parts_out[b], OUT)
        if u >= BUFS:
            sp.wait_ge(s_mm, NS * (u - BUFS + 1))
        for j, to in enumerate((qs, ks)):
            src = scratch[j].rearrange("s (r h) t -> (s r) h t", h=H)[:, g * GH:(g + 1) * GH, b * S:(b + 1) * S]
            sp.dma_start(to[0:STACKED, u % BUFS, :, :], src).then_inc(stack_in[u % BUFS], 16)

    STACK, OUT = 16 * 2, 16 * QC * (len(RUNS[0]) + len(RUNS[1]))

    def clear(act):
        act.wait_ge(m.set_up, 2)
        for buf in range(BUFS):
            nc.scalar.activation(qs[:, buf, :, :].rearrange("p h t -> p (h t)"), m.power[:, 0:1].broadcast_to([P, GH * S]), ACT.Copy,
                                 scale=0.0).then_inc(zeroed, 1)

    def weigh(eng, engine, u, n, done):
        qc, kt, h = STEPS[n]
        e = probs(u * NS + n)
        k = width(qc, kt)
        at = CH * qc - P * kt + S - P
        eng.wait_ge(exps, u * NS + n + 1)
        engine.tensor_tensor(e[:, 0:k], e[:, 0:k], weight[:, at:at + k], ALU.mult).then_inc(done, 1)

    def clear_v(pool):
        nc.gpsimd.memset(vpad[:, :, :, :], 0.0).then_inc(v_zeroed, 1)
        pool.wait_ge(v_zeroed, 1)
        nc.gpsimd.memset(vpad[:, :, :, HD:HD + 1], 1.0).then_inc(v_zeroed, 1)

    def gpsimd(pool):
        pool.wait_ge(w_in, w_all)
        for u in range(UNITS):
            for n in range(NS):
                if by_pool(n):
                    weigh(pool, nc.gpsimd, u, n, weighed_p)

    def tensor(pe):
        pe.wait_ge(w_in, w_all)
        for c in range(NC):
            norm.wait_xnT(pe, c)
            for j in range(2):
                n = 2 * c + j
                if n >= 4:
                    pe.wait_ge(rest_set, n - 3)
                nc.tensor.matmul(m.ps[:, n % 4, :], w[:, j, :], m.xnT[:, c * CH:(c + 1) * CH], start=True, stop=True).then_inc(p_mm, 1)
            if c:
                pe.wait_ge(v_set, c)
            for t in range(c * TPC, (c + 1) * TPC):
                mm = nc.tensor.matmul(m.ps[:, 4, t % TPC * P:(t % TPC + 1) * P], m.xnT[:, t * P:(t + 1) * P], w[:, 2, :], start=True, stop=True)
            mm.then_inc(v_mm, 1)
        pe.wait_ge(rest_set, 2 * NC)
        pe.wait_ge(v_set, NC)
        pe.wait_ge(tails_in, 16 * BUFS)

        def scores_by_query(u, n):
            h, i = TILES[n]
            k = u * len(TILES) + n
            if n == 0:
                pe.wait_ge(stack_in[u % BUFS], STACK * (u // BUFS + 1))
            bank, holder = A_BANKS[k]
            if holder >= 0:
                pe.wait_ge(max_set, holder + 1)
            q = qs[0:ROWS, u % BUFS, h, i * P:(i + 1) * P]
            for j in range(0, S - i * P, CH):
                width_ = min(CH, S - i * P - j)
                mm = nc.tensor.matmul(m.ps[:, bank + j // CH, 0:width_], q, ks[0:ROWS, u % BUFS, h, i * P + j:i * P + j + width_],
                                      start=True, stop=(j > 0), skip_group_check=True)
                if j == 0:
                    mm = nc.tensor.matmul(m.ps[:, bank, 0:P], identb[:, :], before[:, 0, :], start=False, stop=True, skip_group_check=True)
            mm.then_inc(a_mm, 1)

        in_bank7 = {"num": 0, "max": 0}

        def turn_maxima(u, _):
            pe.wait_ge(nparts_set, u + 1)
            if in_bank7["num"]:
                pe.wait_ge(o_set, in_bank7["num"])
            in_bank7["max"] += 1
            for i in range(TB):
                mm = nc.tensor.transpose(m.ps7b[0:GH * 3, i * P:(i + 1) * P], nparts[:, u % 2, i, :], identb[:, :])
            mm.then_inc(n_turned, 1)

        def scores_by_key(u, n):
            qc, kt, h = STEPS[n]
            k = u * NS + n
            if n == 0:
                pe.wait_ge(mrows_in[u % BUFS], 16 * GH * (u // BUFS + 1))
            if k >= 2:
                pe.wait_ge(exps, k - 1)
            wd = width(qc, kt)
            diagonal = kt // TPC == qc
            out = m.ps[:, 4 + k % 2, 0:wd]
            mm = nc.tensor.matmul(out, ks[:, u % BUFS, h, kt * P:(kt + 1) * P], qs[:, u % BUFS, h, CH * qc:CH * qc + wd],
                                  start=True, stop=not diagonal, skip_group_check=True)
            if diagonal:
                mm = nc.tensor.matmul(m.ps[:, 4 + k % 2, wd - P:wd], identb[:, :], before[:, 1, :], start=False, stop=True, skip_group_check=True)
            mm.then_inc(s_mm, 1)

        def times_v(u, n):
            b = u // G
            qc, kt, h = STEPS[n]
            wd = width(qc, kt)
            wait_weighed(pe, u, n)
            if kt == TB - 1 and h == 0 and u * QC + qc:
                pe.wait_ge(num_out, u * QC + qc)
            mm = nc.tensor.matmul(m.ps[PAD * h:PAD * (h + 1), 6, 0:wd], vpad[:, b * TB + kt, u % G * GH + h, :], probs(u * NS + n)[:, 0:wd],
                                  start=(kt == TB - 1), stop=(n >= LAST[qc] - GH + 1), skip_group_check=True)
            mm.then_inc(pv_mm, 1)

        def turn_numerators(u, qc):
            k = u * QC + qc
            pe.wait_ge(num_out, k + 1)
            if k:
                pe.wait_ge(o_set, k)
            pe.wait_ge(mrows_set, in_bank7["max"])
            in_bank7["num"] += 1
            for j in range(TPC):
                mm = nc.tensor.transpose(m.ps[:, 7, j * P:(j + 1) * P], numT[:, k % 2, j * P:(j + 1) * P], m.ident[:, :])
            mm.then_inc(num_turned, 1)

        do = {"max": scores_by_query, "turn_max": turn_maxima, "exp": scores_by_key, "times_v": times_v, "turn_num": turn_numerators}
        for what, u, n in schedule():
            if what in do:
                do[what](u, n)
        pe.wait_ge(max_set, len(TILES) * UNITS)
        for c in range(NC):
            pe.wait_ge(o_set, min(UNITS * QC, (c // QC + 1) * G * QC))
            for j in range(TPC):
                mm = nc.tensor.transpose(m.ps[:, c, j * P:(j + 1) * P], o[:, c * TPC + j, :], m.ident[:, :])
            mm.then_inc(o_turned, 1)
        for c in range(NC):
            pe.wait_ge(oT_set, c + 1)
            for j in range(TPC):
                mm = nc.tensor.matmul(m.ps[:, c, j * P:(j + 1) * P], oT[:, j * P:(j + 1) * P], wo[:, :], start=True, stop=True)
            mm.then_inc(y_mm, 1)

    def scalar(act):
        def high(n):
            cs = slice(n // 2 % 2 * CH, (n // 2 % 2 + 1) * CH)
            if n == 2 * QC:
                act.wait_ge(parts_out[0], OUT)
            norm.copy_xnT(act, n // 2 + 1)
            act.wait_ge(p_mm, n + 1)
            nc.scalar.activation(parts[:, 0, n % 2, cs], m.ps[:, n % 4, :], ACT.Identity, bias=bqk[:, n % 2:n % 2 + 1]).then_inc(high_set, 1)

        def mid(n):
            cs = slice(n // 2 % 2 * CH, (n // 2 % 2 + 1) * CH)
            act.wait_ge(rest_set, n + 1)
            nc.scalar.activation(parts[:, 1, n % 2, cs], rest[:, n % 2, :], ACT.Copy).then_inc(mid_set, 1)

        high(0)
        for n in range(2 * NC):
            if n + 1 < 2 * NC and n + 1 != 2 * QC:
                high(n + 1)
            mid(n)
            if n + 1 == 2 * QC:
                high(n + 1)

        def exp(u, n):
            qc, kt, h = STEPS[n]
            k = u * NS + n
            wd = width(qc, kt)
            act.wait_ge(s_mm, k + 1)
            if k >= RING:
                act.wait_ge(pv_mm, k - RING + 1)
            nc.scalar.activation(probs(k)[:, 0:wd], m.ps[:, 4 + k % 2, 0:wd], ACT.Exp, scale=SCALE).then_inc(exps, 1)

        def take_numerators(u, qc):
            k = u * QC + qc
            act.wait_ge(pv_mm, u * NS + LAST[qc] + 1)
            if k >= 2:
                act.wait_ge(num_turned, k - 1)
            nc.scalar.activation(numT[:, k % 2, :], m.ps[:, 6, :], ACT.Copy).then_inc(num_out, 1)

        def take_maxima(u, _):
            act.wait_ge(n_turned, u + 1)
            nc.scalar.activation(mrows[:, u % 2, :], m.ps7b[0:GH * 3, :], ACT.Copy).then_inc(mrows_set, 1)

        do = {"exp": exp, "take_num": take_numerators, "take_max": take_maxima}
        for what, u, n in schedule():
            if what in do:
                do[what](u, n)
        for c in range(NC):
            act.wait_ge(o_turned, c + 1)
            if c:
                act.wait_ge(y_mm, c)
            nc.scalar.activation(oT, m.ps[:, c, :], ACT.Copy).then_inc(oT_set, 1)

    def vector(dve, after):
        def left_of_high(n):
            c = n // 2
            cs = slice(c % 2 * CH, (c % 2 + 1) * CH)
            dve.wait_ge(high_set, n + 1)
            if n >= 2:
                dve.wait_ge(low_set, n - 1)
            nc.vector.scalar_tensor_tensor(out=rest[:, n % 2, :], in0=m.ps[:, n % 4, :], scalar=bqk[:, n % 2:n % 2 + 1],
                                           in1=parts[:, 0, n % 2, cs], op0=ALU.add, op1=ALU.subtract).then_inc(rest_set, 1)

        left_of_high(0)
        for n in range(2 * NC):
            c = n // 2
            cs = slice(c % 2 * CH, (c % 2 + 1) * CH)
            if n + 1 < 2 * NC and n + 1 != 2 * QC:
                left_of_high(n + 1)
            if n % 2:
                dve.wait_ge(v_mm, c + 1)
                dve.wait_ge(v_zeroed, 2)
                nc.vector.tensor_tensor(vpad[:, c * TPC:(c + 1) * TPC, :, 0:HD], m.ps[:, 4, :].rearrange("p (t h e) -> p t h e", h=H, e=HD),
                                        bv[:, :].rearrange("p (h e) -> p h e", e=HD).unsqueeze(1).broadcast_to([P, TPC, H, HD]), ALU.add).then_inc(v_set, 1)
            dve.wait_ge(mid_set, n + 1)
            nc.vector.tensor_tensor(parts[:, 2, n % 2, cs], rest[:, n % 2, :], parts[:, 1, n % 2, cs], ALU.subtract).then_inc(low_set, 1)
            if n + 1 == 2 * QC:
                left_of_high(n + 1)

        def maximum(u, n):
            h, i = TILES[n]
            k = u * len(TILES) + n
            dve.wait_ge(a_mm, k + 1)
            bank = A_BANKS[k][0]
            nc.vector.tensor_reduce(negmax[:, u % 2, h, i:i + 1], m.psf[:, bank * CH:bank * CH + S - i * P], AX.X, ALU.max,
                                    negate=True).then_inc(max_set, 1)

        def split_maxima(u, _):
            dve.wait_ge(max_set, len(TILES) * (u + 1))
            mine = negmax[:, u % 2, :, :]
            part = lambda p: nparts[:, u % 2, :, :].rearrange("q i (h p) -> q h i p", p=3)[:, :, :, p]
            if u >= 2:
                dve.wait_ge(n_turned, u - 1)
            nc.vector.tensor_copy(part(0), mine).then_inc(nsplit, 1)
            dve.wait_ge(nsplit, 3 * u + 1)
            nc.vector.tensor_tensor(nrest[:, :, :], mine, part(0), ALU.subtract).then_inc(nsplit, 1)
            dve.wait_ge(nsplit, 3 * u + 2)
            nc.vector.tensor_copy(part(1), nrest[:, :, :]).then_inc(nsplit, 1)
            dve.wait_ge(nsplit, 3 * u + 3)
            nc.vector.tensor_tensor(part(2), nrest[:, :, :], part(1), ALU.subtract).then_inc(nparts_set, 1)

        def divide(u, qc):
            k = u * QC + qc
            b, g = divmod(u, G)
            dve.wait_ge(num_turned, k + 1)
            turned = m.ps[:, 7, :].rearrange("p (t h e) -> p t h e", h=GH, e=PAD)
            r = rec[:, k % 2, :].rearrange("p (t h) -> p t h", h=GH)
            nc.vector.reciprocal(r, turned[:, :, :, HD]).then_inc(rec_set, 1)
            dve.wait_ge(rec_set, k + 1)
            t0 = b * TB + qc * TPC
            nc.vector.tensor_tensor(o[:, t0:t0 + TPC, g * GH * HD:(g + 1) * GH * HD].rearrange("p t (h e) -> p t h e", e=HD),
                                    turned[:, :, :, 0:HD], r.unsqueeze(3).broadcast_to([P, TPC, GH, HD]), ALU.mult).then_inc(o_set, 1)

        def weigh_mine(u, n):
            if not by_pool(n):
                weigh(dve, nc.vector, u, n, weighed_v)

        do = {"max": maximum, "split": split_maxima, "weigh": weigh_mine, "divide": divide}
        for what, u, n in schedule():
            if what in do:
                do[what](u, n)
        for c in range(NC):
            dve.wait_ge(y_mm, c + 1)
            dve.wait_ge(m.biased, norm.biased_value(c))
            xs = m.x[:, c * TPC:(c + 1) * TPC, :]
            nc.vector.tensor_tensor(xs, m.ps[:, c, :].rearrange("p (j d) -> p j d", d=D), xs, ALU.add).then_inc(x_done, 1)
            after(dve, c)

    return Part([(x_done, norm.done(c)) for c in range(NC)], tensor=tensor, vector=vector, scalar=scalar, gpsimd=gpsimd, sync=sync,
                before_norm={"scalar": clear, "gpsimd": clear_v}, bias="L0_attn_b_proj")


def l0_ffn(nc, m, A, sem, sb, norm):
    F = 384
    FT = F // P
    SCALE = 1.0 / 127.0
    wi = sb("l0f_wi", [P, 3, F], I32)
    w = sb("l0f_w", [P, 3, F])
    sg = sb("l0f_sg", [P, 2, CH])
    hT = sb("l0f_hT", [P, 2, FT, CH])
    w_in, w_all = norm.loads(1)
    w_scaled = sem("l0f_w_scaled")
    up_done = sem("l0f_up_done")
    sg_done, h_done = sem("l0f_sg_done"), sem("l0f_h_done")
    down_done, x_done = sem("l0f_down_done"), m.x_done

    def sync(sp):
        sp.dma_start(wi[:, :, :], A["L0_ffn_w"]).then_inc(w_in, 16)

    def dequantise(dve):
        dve.wait_ge(w_in, w_all)
        nc.vector.tensor_scalar(w[:, :, :], wi[:, :, :], SCALE, None, ALU.mult).then_inc(w_scaled, 1)

    def tensor(pe):
        def gates(c):
            norm.wait_xnT(pe, c)
            for f in range(FT):
                s = c * FT + f
                if s >= 2:
                    pe.wait_ge(h_done, s - 1)
                for half in range(2):
                    nc.tensor.matmul(m.ps[:, 2 * (s % 2) + half, :], w[:, half, f * P:(f + 1) * P], m.xnT[:, c * CH:(c + 1) * CH],
                                     start=True, stop=True).then_inc(up_done, 1)

        def down(c):
            if c >= 2:
                pe.wait_ge(x_done, norm.done(c - 2))
            for f in range(FT):
                pe.wait_ge(h_done, c * FT + f + 1)
                for j in range(TPC):
                    mm = nc.tensor.matmul(m.ps[:, 4 + c % 2, j * P:(j + 1) * P], hT[:, c % 2, f, j * P:(j + 1) * P],
                                          w[:, 2, f * P:(f + 1) * P], start=(f == 0 and j == 0), stop=(f == FT - 1), skip_group_check=True)
            mm.then_inc(down_done, 1)

        pe.wait_ge(w_scaled, 1)
        for c in range(NC):
            gates(c)
            if c:
                down(c - 1)
        down(NC - 1)

    def scalar(act):
        for s in range(NC * FT):
            norm.copy_xnT(act, s // FT + 1)
            act.wait_ge(up_done, 2 * s + 1)
            nc.scalar.activation(sg[:, s % 2, :], m.ps[:, 2 * (s % 2), :], ACT.Silu).then_inc(sg_done, 1)

    def vector(dve, after):
        def add(c):
            dve.wait_ge(down_done, c + 1)
            xs = m.x[:, c * TPC:(c + 1) * TPC, :]
            nc.vector.tensor_tensor(xs, m.ps[:, 4 + c % 2, :].rearrange("p (j d) -> p j d", d=D), xs, ALU.add).then_inc(x_done, 1)
            after(dve, c)

        for c in range(NC):
            for f in range(FT):
                s = c * FT + f
                dve.wait_ge(up_done, 2 * s + 2)
                dve.wait_ge(sg_done, s + 1)
                nc.vector.tensor_tensor(hT[:, c % 2, f, :], m.ps[:, 2 * (s % 2) + 1, :], sg[:, s % 2, :], ALU.mult).then_inc(h_done, 1)
            if c:
                add(c - 1)
        add(NC - 1)

    return Part([(x_done, norm.done(c)) for c in range(NC)], tensor=tensor, vector=vector, scalar=scalar, sync=sync,
                before_norm={"vector": dequantise})


def l1_attn(nc, m, A, sem, sb, norm):
    H, HD = 16, 8
    HB = NT // 2
    SCALE = HD ** -0.5
    wqk = sb("l1a_wqk", [P, 2, D])
    rope = sb("l1a_rope", [P, P])
    w = sb("l1a_w", [P, 5, D])
    bcol = sb("l1a_bcol", [P, 2])
    bwide = sb("l1a_bwide", [P, 2, P])
    bias = sb("l1a_bias", [P, 5, D])
    kv0 = sb("l1a_kv0", [P, HB, 2, D])
    qkv1 = sb("l1a_qkv1", [P, HB, 3, D])
    prod = sb("l1a_prod", [P, 2, TPC * D])
    sc = sb("l1a_sc", [P, 2, TPC * H])
    mx, tot = sb("l1a_mx", [P, TPC * H]), sb("l1a_tot", [P, TPC * H])
    ex = sb("l1a_ex", [P, 2, TPC * H])

    w_in, w_all = norm.loads(8)
    widened, rot_mm, rot_set = sem("l1a_widened"), sem("l1a_rot_mm"), sem("l1a_rot_set")
    mm_done = sem("l1a_mm_done")
    taken = sem("l1a_taken")
    step, exps, x_done = sem("l1a_step"), sem("l1a_exps"), sem("l1a_x_done")

    ORDER = [t for half in range(2) for pos in range(2) for t in range(pos * HB + half * TPC, pos * HB + half * TPC + TPC)]

    def sync(sp):
        sp.dma_start(wqk[:, :, :], A["L1_attn_wqk"]).then_inc(w_in, 16)
        sp.dma_start(rope[:, :], A["L1_attn_rope"]).then_inc(w_in, 16)
        sp.dma_start(w[:, 0:2, :], A["L1_attn_wkvT"]).then_inc(w_in, 16)
        sp.dma_start(w[:, 4, :], A["L1_attn_wkvT"][:, 1, :]).then_inc(w_in, 16)
        sp.dma_start(bcol[:, :], A["L1_attn_bcol"]).then_inc(w_in, 16)
        sp.dma_start(bias[:, 0, :], A["L1_attn_bkv"][0:1, :].broadcast_to([P, D])).then_inc(w_in, 16)
        sp.dma_start(bias[:, 1, :], A["L1_attn_bkv"][1:2, :].broadcast_to([P, D])).then_inc(w_in, 16)
        sp.dma_start(bias[:, 4, :], A["L1_attn_bkv"][1:2, :].broadcast_to([P, D])).then_inc(w_in, 16)

    def widen(dve):
        dve.wait_ge(w_in, w_all)
        for j in range(2):
            ins = nc.vector.tensor_copy(bwide[:, j, :], bcol[:, j:j + 1].broadcast_to([P, P]))
        ins.then_inc(widened, 1)

    def rotate(pe):
        pe.wait_ge(w_in, w_all)
        pe.wait_ge(widened, 1)
        for j in range(2):
            nc.tensor.matmul(m.ps[:, 0, j * P:(j + 1) * P], wqk[:, j, :], rope[:, :], start=True, stop=True)
            mm = nc.tensor.matmul(m.ps[:, 0, (2 + j) * P:(3 + j) * P], bwide[:, j, :], rope[:, :], start=True, stop=True)
        mm.then_inc(rot_mm, 1)

    def take_rotated(act):
        act.wait_ge(rot_mm, 1)
        nc.scalar.activation(w[:, 2:4, :].rearrange("p a b -> p (a b)"), m.ps[:, 0, 0:2 * P], ACT.Copy)
        nc.scalar.activation(bias[:, 2:4, :].rearrange("p a b -> p (a b)"), m.ps[:, 0, 2 * P:4 * P], ACT.Copy).then_inc(rot_set, 1)

    def tensor(pe):
        pe.wait_ge(rot_set, 1)
        for n, t in enumerate(ORDER):
            norm.wait_xnT(pe, t // TPC)
            if n >= 4:
                pe.wait_ge(taken, n - 3)
            cols = w[:, 0:2, :] if t < HB else w[:, 2:5, :]
            width = 2 * D if t < HB else 3 * D
            nc.tensor.matmul(m.ps[:, n % 4, 0:width], m.xnT[:, t * P:(t + 1) * P], cols, start=True, stop=True).then_inc(mm_done, 1)

    def scalar(act):
        norm.copy_xnT(act, NC - 1)
        for half in range(2):
            act.wait_ge(step, STEPS * half + 4)
            nc.scalar.activation(ex[:, :, :], sc[:, :, :], ACT.Exp, scale=SCALE).then_inc(exps, 1)

    STEPS = 11

    def vector(dve, after):
        count = [0]

        def then(ins):
            ins.then_inc(step, 1)
            count[0] += 1
            dve.wait_ge(step, count[0])

        for n, t in enumerate(ORDER):
            dve.wait_ge(mm_done, n + 1)
            dst, k, b0 = (kv0[:, t, :, :], 2, 0) if t < HB else (qkv1[:, t - HB, :, :], 3, 2)
            nc.vector.tensor_tensor(dst, m.ps[:, n % 4, 0:k * D].rearrange("p (a d) -> p a d", d=D), bias[:, b0:b0 + k, :],
                                    ALU.add).then_inc(taken, 1)
        for half in range(2):
            dve.wait_ge(taken, 8 * half + 8)
            hs = slice(half * TPC, (half + 1) * TPC)
            q1, k1, v1 = (qkv1[:, hs, j, :] for j in range(3))
            k0, v0 = (kv0[:, hs, j, :] for j in range(2))
            tile = lambda a: a.rearrange("p (t d) -> p t d", d=D)
            heads = lambda a: a.rearrange("p (g e) -> p g e", e=HD)
            nc.vector.tensor_tensor(tile(prod[:, 0, :]), q1, k0, ALU.mult)
            then(nc.vector.tensor_tensor(tile(prod[:, 1, :]), q1, k1, ALU.mult))
            then(nc.vector.tensor_reduce(sc[:, :, :].rearrange("p a b -> p (a b)"),
                                         prod[:, :, :].rearrange("p a (g e) -> p (a g) e", e=HD), AX.X, ALU.add))
            then(nc.vector.tensor_tensor(mx[:, :], sc[:, 0, :], sc[:, 1, :], ALU.max))
            then(nc.vector.tensor_tensor(sc[:, :, :], sc[:, :, :], mx[:, :].unsqueeze(1).broadcast_to([P, 2, TPC * H]), ALU.subtract))
            x0 = m.x[:, hs, :]
            x1 = m.x[:, HB + half * TPC:HB + (half + 1) * TPC, :]
            nc.vector.scalar_tensor_tensor(out=x0, in0=v0, scalar=0.5, in1=x0, op0=ALU.mult, op1=ALU.add).then_inc(x_done, 1)
            after(dve, half)
            dve.wait_ge(exps, half + 1)
            then(nc.vector.scalar_tensor_tensor(out=tot[:, :], in0=ex[:, 0, :], scalar=1.0, in1=ex[:, 1, :], op0=ALU.add, op1=ALU.add))
            then(nc.vector.reciprocal(tot[:, :], tot[:, :]))
            then(nc.vector.tensor_tensor(ex[:, :, :], ex[:, :, :], tot[:, :].unsqueeze(1).broadcast_to([P, 2, TPC * H]), ALU.mult))
            weight = lambda j: ex[:, j, :].rearrange("p (t h) -> p t h", h=H).unsqueeze(3).broadcast_to([P, TPC, H, HD])
            split = lambda a: a.rearrange("p t (h e) -> p t h e", e=HD)
            part = lambda j: prod[:, j, :].rearrange("p (t h e) -> p t h e", h=H, e=HD)
            then(nc.vector.tensor_tensor(part(0), split(v0), weight(0), ALU.mult))
            then(nc.vector.tensor_tensor(part(1), split(v1), weight(1), ALU.mult))
            then(nc.vector.tensor_tensor(prod[:, 0, :], prod[:, 0, :], prod[:, 1, :], ALU.add))
            then(nc.vector.tensor_tensor(x1, x1, tile(prod[:, 0, :]), ALU.add))
            assert count[0] == STEPS * (half + 1)
        after(dve, 2)
        after(dve, 3)

    return Part([(x_done, 1), (x_done, 2), (step, STEPS), (step, 2 * STEPS)], tensor=tensor, vector=vector, scalar=scalar, sync=sync,
                before_norm={"vector": widen, "tensor": rotate, "scalar": take_rotated})


def l1_ffn(nc, m, A, sem, sb, norm):
    E, R = 6, 16
    EP = 8
    HID = (E + 1) * R
    W = HID + E
    wa = sb("l1f_wa", [P, W])
    wb = sb("l1f_wb", [HID, D])
    base = sb("l1f_base", [P, D])
    rb = sb("l1f_rb", [P, E])
    r = router_buffers(sb, "l1f", EP)
    e_, sel_, wte = (sb(f"l1f_{n}", [P, NT, EP]) for n in ("e", "sel", "wte"))
    z, tot, f1 = (sb(f"l1f_{n}", [P, NT]) for n in ("z", "tot", "f1"))
    h = sb("l1f_h", [P, NT, HID])
    hT = sb("l1f_hT", [HID, 2, CH])

    w_in, w_all = norm.loads(4)
    filled = sem("l1f_filled")
    h_mm, step, exps = sem("l1f_h_mm"), sem("l1f_step"), sem("l1f_exps")
    h_set, turned, hT_set = sem("l1f_h_set"), sem("l1f_turned"), sem("l1f_hT_set")
    y_mm, x_done = sem("l1f_y_mm"), m.x_done

    def sync(sp):
        for dst, name in ((wa, "L1_ffn_wa"), (wb, "L1_ffn_wb"), (base, "L1_ffn_base")):
            sp.dma_start(dst[:, :], A[name]).then_inc(w_in, 16)
        sp.dma_start(rb[:, :], A["L1_ffn_rb"].broadcast_to([P, E])).then_inc(w_in, 16)

    def tensor(pe):
        pe.wait_ge(w_in, w_all)
        for c in range(NC):
            norm.wait_xnT(pe, c)
            for j in range(TPC):
                t = c * TPC + j
                mm = nc.tensor.matmul(m.ps[:, c, j * W:(j + 1) * W], m.xnT[:, t * P:(t + 1) * P], wa[:, :], start=True, stop=True)
            mm.then_inc(h_mm, 1)
        norm.wait_xnT(pe, NC - 1)
        for c in range(NC + 1):
            if c < NC:
                pe.wait_ge(h_set, c + 1)
                if c >= 2:
                    pe.wait_ge(hT_set, c - 1)
                for j in range(TPC):
                    mm = nc.tensor.transpose(m.ps[0:HID, 4 + c % 2, j * P:(j + 1) * P], h[:, c * TPC + j, :], m.ident[:, :])
                mm.then_inc(turned, 1)
            if c:
                b = c - 1
                pe.wait_ge(hT_set, b + 1)
                if b >= 2:
                    pe.wait_ge(x_done, norm.done(b - 2))
                for j in range(TPC):
                    t = b * TPC + j
                    y = m.ps[:, 6 + b % 2, j * P:(j + 1) * P]
                    nc.tensor.matmul(y, m.xnT[:, t * P:(t + 1) * P], base[:, :], start=(j == 0), stop=False, skip_group_check=True)
                    mm = nc.tensor.matmul(y, hT[:, b % 2, j * P:(j + 1) * P], wb[:, :], start=False, stop=True, skip_group_check=True)
                mm.then_inc(y_mm, 1)

    def scalar(act):
        norm.copy_xnT(act, NC - 1)
        act.wait_ge(step, STEP_D)
        nc.scalar.activation(e_[:, :, :], e_[:, :, :], ACT.Exp).then_inc(exps, 1)
        for c in range(NC):
            act.wait_ge(turned, c + 1)
            if c >= 2:
                act.wait_ge(y_mm, c - 1)
            nc.scalar.activation(hT[:, c % 2, :], m.ps[0:HID, 4 + c % 2, :], ACT.Copy).then_inc(hT_set, 1)

    STEP_D = 3 + RANK_STEPS

    def vector(dve, after):
        count = [0]

        def then(ins):
            ins.then_inc(step, 1)
            count[0] += 1
            dve.wait_ge(step, count[0])

        L = r.logits
        then(nc.vector.memset(L[:, :, E:EP], -3e38))
        dve.wait_ge(w_in, w_all)
        hview = lambda c: m.ps[:, c, 0:TPC * W].rearrange("p (j w) -> p j w", w=W)
        for c in range(NC):
            dve.wait_ge(h_mm, c + 1)
            ts = slice(c * TPC, (c + 1) * TPC)
            nc.vector.tensor_copy(h[:, ts, E * R:HID], hview(c)[:, :, E * R:HID])
            ins = nc.vector.tensor_tensor(L[:, ts, 0:E], hview(c)[:, :, HID:W], rb[:, :].unsqueeze(1).broadcast_to([P, TPC, E]), ALU.add)
            if c == NC - 1:
                then(ins)
        ranks(nc, then, m, r, EP)
        bc = lambda a: a.unsqueeze(2).broadcast_to([P, NT, EP])
        then(nc.vector.tensor_tensor(e_[:, :, :], L[:, :, :], bc(r.first[:, :]), ALU.subtract))
        then(nc.vector.tensor_tensor(sel_[:, :, :], r.is_first[:, :, :], r.is_second[:, :, :], ALU.add))
        assert STEP_D <= count[0], count[0]
        dve.wait_ge(exps, 1)
        then(nc.vector.tensor_reduce(z[:, :], e_[:, :, :], AX.X, ALU.add))
        then(nc.vector.reciprocal(z[:, :], z[:, :]))
        then(nc.vector.tensor_tensor(sel_[:, :, :], sel_[:, :, :], e_[:, :, :], ALU.mult))
        then(nc.vector.tensor_tensor(sel_[:, :, :], sel_[:, :, :], bc(z[:, :]), ALU.mult))
        then(nc.vector.tensor_reduce(tot[:, :], sel_[:, :, :], AX.X, ALU.add))
        then(nc.vector.tensor_scalar(tot[:, :], tot[:, :], 1e-6, None, ALU.add))
        then(nc.vector.reciprocal(tot[:, :], tot[:, :]))
        then(nc.vector.tensor_tensor(wte[:, :, :], sel_[:, :, :], bc(tot[:, :]), ALU.mult))
        for c in range(NC):
            ts = slice(c * TPC, (c + 1) * TPC)
            for j in range(TPC):
                t = c * TPC + j
                ins = nc.vector.tensor_tensor(h[:, t, 0:E * R].rearrange("p (e r) -> p e r", r=R),
                                              hview(c)[:, j, 0:E * R].rearrange("p (e r) -> p e r", r=R),
                                              wte[:, t, 0:E].unsqueeze(2).broadcast_to([P, E, R]), ALU.mult)
            ins.then_inc(h_set, 1)
        for c in range(NC):
            dve.wait_ge(y_mm, c + 1)
            dve.wait_ge(m.biased, norm.biased_value(c))
            xs = m.x[:, c * TPC:(c + 1) * TPC, :]
            nc.vector.tensor_tensor(xs, m.ps[:, 6 + c % 2, :].rearrange("p (j d) -> p j d", d=D), xs, ALU.add).then_inc(x_done, 1)
            after(dve, c)

    return Part([(x_done, norm.done(c)) for c in range(NC)], tensor=tensor, vector=vector, scalar=scalar, sync=sync, bias="L1_ffn_base_b")


def l2_attn(nc, m, A, sem, sb, norm):
    H, HD = 16, 8
    G = H // 4
    PAD = 32
    TB = S // P
    VW = HD + 1
    w = sb("l2a_w", [P, 3, D])
    wo = sb("l2a_wo", [P, D])
    bqk = sb("l2a_bqk", [P, 2])
    bv = sb("l2a_bv", [P, D])
    causal = sb("l2a_causal", [P, P])
    hmask = sb("l2a_hmask", [P, H])
    early = sb("l2a_early", [P, NT * D])
    low, expd = (early[:, n * 2 * CH:(n + 1) * 2 * CH].rearrange("p (a b) -> p a b", a=2) for n in range(2))
    pos = sb("l2a_pos", [P, 2, CH])
    phi = sb("l2a_phi", [P, 2, T])
    ktok = sb("l2a_ktok", [P, NT, D])
    vpad = sb("l2a_vpad", [P, NT, H, PAD])
    qm = sb("l2a_qm", [P, 2, H, P])
    at = sb("l2a_at", [P, 2, G, 4 * P])
    state = sb("l2a_state", [P, 2, H, PAD])
    numT = sb("l2a_numT", [P, 2, G * P])
    den, rec = sb("l2a_den", [P, 2, H]), sb("l2a_rec", [P, 2, H])
    o = early.rearrange("p (t d) -> p t d", d=D)
    oT = sb("l2a_oT", [P, CH])

    norm.bias_late = True
    w_in, w_all = norm.loads(6)
    zeroed = sem("l2a_zeroed")
    p_mm, lowered, expd_set, elu_set, phi_set = (sem(f"l2a_{n}") for n in ("p_mm", "lowered", "expd_set", "elu_set", "phi_set"))
    v_mm, v_set, k_turned, ktok_set = (sem(f"l2a_{n}") for n in ("v_mm", "v_set", "k_turned", "ktok_set"))
    qm_set, a_mm, a_set, s_mm, s_set = (sem(f"l2a_{n}") for n in ("qm_set", "a_mm", "a_set", "s_mm", "s_set"))
    n_mm, n_out, n_turned, den_set, rec_set, o_set = (sem(f"l2a_{n}") for n in ("n_mm", "n_out", "n_turned", "den_set", "rec_set", "o_set"))
    o_turned, oT_set, y_mm = (sem(f"l2a_{n}") for n in ("o_turned", "oT_set", "y_mm"))
    x_done = m.x_done

    def sync(sp):
        sp.dma_start(w[:, :, :], A["L2_attn_w"]).then_inc(w_in, 16)
        sp.dma_start(wo[:, :], A["L2_attn_wo"]).then_inc(w_in, 16)
        sp.dma_start(bqk[:, :], A["L2_attn_bqk"]).then_inc(w_in, 16)
        sp.dma_start(bv[:, :], A["L2_attn_bv"].broadcast_to([P, D])).then_inc(w_in, 16)
        sp.dma_start(causal[:, :], A["causal"]).then_inc(w_in, 16)
        sp.dma_start(hmask[:, :], A["hmask"]).then_inc(w_in, 16)

    def clear(pool):
        pool.wait_ge(w_in, w_all)
        nc.gpsimd.memset(vpad[:, :, :, :], 0.0).then_inc(zeroed, 1)
        nc.gpsimd.memset(state[:, :, :, :], 0.0).then_inc(zeroed, 1)
        pool.wait_ge(zeroed, 2)
        nc.gpsimd.memset(vpad[:, :, :, HD:VW], 1.0).then_inc(zeroed, 1)

    def gpsimd(pool):
        for t in range(NT):
            c = t // TPC
            pool.wait_ge(phi_set, 2 * c + 1)
            if t >= 2:
                pool.wait_ge(a_mm, G * (t - 1))
            nc.gpsimd.tensor_tensor(qm[:, t % 2, :, :], phi[:, 0, t * P:(t + 1) * P].unsqueeze(1).broadcast_to([P, H, P]),
                                    hmask[:, :].unsqueeze(2).broadcast_to([P, H, P]), ALU.mult).then_inc(qm_set, 1)
            if 1 <= t <= NC:
                norm.add_bias(pool, m.bias_of["L2_attn_bo"], t - 1)

    def tensor(pe):
        pe.wait_ge(w_in, w_all)
        for c in range(NC):
            norm.wait_xnT(pe, c)
            cs = slice(c * CH, (c + 1) * CH)
            for j in range(2):
                n = 2 * c + j
                if n >= 4:
                    pe.wait_ge(phi_set, n - 3)
                nc.tensor.matmul(m.ps[:, n % 4, :], w[:, j, :], m.xnT[:, cs], start=True, stop=True).then_inc(p_mm, 1)
            if c:
                pe.wait_ge(v_set, c)
            for t in range(c * TPC, (c + 1) * TPC):
                mm = nc.tensor.matmul(m.ps[:, 4, t % TPC * P:(t % TPC + 1) * P], m.xnT[:, t * P:(t + 1) * P], w[:, 2, :], start=True, stop=True)
            mm.then_inc(v_mm, 1)
        for c in range(NC):
            pe.wait_ge(phi_set, 2 * c + 2)
            if c:
                pe.wait_ge(ktok_set, c)
            for t in range(c * TPC, (c + 1) * TPC):
                mm = nc.tensor.transpose(m.ps[:, 5, t % TPC * P:(t % TPC + 1) * P], phi[:, 1, t * P:(t + 1) * P], m.ident[:, :])
            mm.then_inc(k_turned, 1)
        pe.wait_ge(zeroed, 3)
        pe.wait_ge(v_set, NC)
        pe.wait_ge(ktok_set, NC)

        def scores(t):
            pe.wait_ge(qm_set, t + 1)
            for g in range(G):
                if t:
                    pe.wait_ge(a_set, G * (t - 1) + g + 1)
                nc.tensor.matmul(m.ps[:, g, :], phi[:, 1, t * P:(t + 1) * P], qm[:, t % 2, 4 * g:4 * g + 4, :], start=True, stop=True).then_inc(a_mm, 1)

        def add_state(t):
            if t:
                pe.wait_ge(s_set, t)
            nc.tensor.matmul(m.ps[:, 7, 0:H * VW], ktok[:, t, :], vpad[:, t, :, 0:VW], start=(t % TB == 0), stop=True,
                             skip_group_check=True).then_inc(s_mm, 1)

        def numerators(t):
            if t:
                pe.wait_ge(n_out, t)
            if t % TB:
                pe.wait_ge(s_set, t)
                for g in range(G):
                    nc.tensor.matmul(m.ps[:, 4, g * P:(g + 1) * P], state[:, t % 2, 4 * g:4 * g + 4, :], phi[:, 0, t * P:(t + 1) * P],
                                     start=(g == 0), stop=False, skip_group_check=True)
            for g in range(G):
                pe.wait_ge(a_set, G * t + g + 1)
                for j in range(4):
                    mm = nc.tensor.matmul(m.ps[PAD * j:PAD * (j + 1), 4, g * P:(g + 1) * P], vpad[:, t, 4 * g + j, :],
                                          at[:, t % 2, g, j * P:(j + 1) * P], start=(t % TB == 0 and g == 0), stop=(g == G - 1),
                                          skip_group_check=True)
            mm.then_inc(n_mm, 1)

        def turn_numerators(t):
            pe.wait_ge(n_out, t + 1)
            if t:
                pe.wait_ge(o_set, t)
            for g in range(G):
                mm = nc.tensor.transpose(m.ps[:, 5, g * P:(g + 1) * P], numT[:, t % 2, g * P:(g + 1) * P], m.ident[:, :])
            mm.then_inc(n_turned, 1)

        def project(c):
            pe.wait_ge(o_set, (c + 1) * TPC)
            if c:
                pe.wait_ge(x_done, norm.done(c - 1))
            for j in range(TPC):
                mm = nc.tensor.transpose(m.ps[:, 6, j * P:(j + 1) * P], o[:, c * TPC + j, :], m.ident[:, :])
            mm.then_inc(o_turned, 1)
            pe.wait_ge(oT_set, c + 1)
            for j in range(TPC):
                mm = nc.tensor.matmul(m.ps[:, 6, j * P:(j + 1) * P], oT[:, j * P:(j + 1) * P], wo[:, :], start=True, stop=True)
            mm.then_inc(y_mm, 1)

        for t in range(NT + 2):
            if t < NT:
                scores(t)
            if 1 <= t <= NT:
                numerators(t - 1)
            if t < NT:
                add_state(t)
            if t >= 2:
                turn_numerators(t - 2)
            if t >= 3 and (t - 3) % TPC == TPC - 1:
                project((t - 3) // TPC)
        project(NC - 1)

    def scalar(act):
        for n in range(2 * NC):
            norm.copy_xnT(act, n // 2 + 1)
            act.wait_ge(lowered, n + 1)
            if n >= 2:
                act.wait_ge(phi_set, n - 1)
            nc.scalar.activation(expd[:, n % 2, :], low[:, n % 2, :], ACT.Exp)
            nc.scalar.activation(pos[:, n % 2, :], m.ps[:, n % 4, :], ACT.Relu, bias=bqk[:, n % 2:n % 2 + 1]).then_inc(expd_set, 1)
        for c in range(NC):
            act.wait_ge(k_turned, c + 1)
            nc.scalar.activation(ktok[:, c * TPC:(c + 1) * TPC, :].rearrange("p t d -> p (t d)"), m.ps[:, 5, :], ACT.Copy).then_inc(ktok_set, 1)

        def oT_copy(c):
            act.wait_ge(o_turned, c + 1)
            nc.scalar.activation(oT[:, :], m.ps[:, 6, :], ACT.Copy).then_inc(oT_set, 1)

        for t in range(NT):
            act.wait_ge(n_mm, t + 1)
            if t >= 2:
                act.wait_ge(n_turned, t - 1)
            nc.scalar.activation(numT[:, t % 2, :], m.ps[:, 4, :], ACT.Copy).then_inc(n_out, 1)
            if t >= TPC + 1 and (t - 1) % TPC == 0:
                oT_copy((t - 1) // TPC - 1)
        oT_copy(NC - 1)

    def vector(dve, after):
        def lower(n):
            dve.wait_ge(p_mm, n + 1)
            if n >= 2:
                dve.wait_ge(expd_set, n - 1)
            nc.vector.tensor_scalar(low[:, n % 2, :], m.ps[:, n % 4, :], bqk[:, n % 2:n % 2 + 1], 0.0, ALU.add, ALU.min).then_inc(lowered, 1)

        lower(0)
        for n in range(2 * NC):
            if n + 1 < 2 * NC:
                lower(n + 1)
            if n % 2:
                c = n // 2
                dve.wait_ge(v_mm, c + 1)
                dve.wait_ge(zeroed, 3)
                ts = slice(c * TPC, (c + 1) * TPC)
                nc.vector.tensor_tensor(vpad[:, ts, :, 0:HD], m.ps[:, 4, :].rearrange("p (t h e) -> p t h e", h=H, e=HD),
                                        bv[:, :].rearrange("p (h e) -> p h e", e=HD).unsqueeze(1).broadcast_to([P, TPC, H, HD]), ALU.add).then_inc(v_set, 1)
            dve.wait_ge(expd_set, n + 1)
            c = n // 2
            ph = phi[:, n % 2, c * CH:(c + 1) * CH]
            nc.vector.scalar_tensor_tensor(out=ph, in0=expd[:, n % 2, :], scalar=-1.0, in1=pos[:, n % 2, :],
                                           op0=ALU.add, op1=ALU.add).then_inc(elu_set, 1)
            dve.wait_ge(elu_set, n + 1)
            nc.vector.tensor_scalar(ph, ph, 1.0, None, ALU.add).then_inc(phi_set, 1)

        def mask_scores(t):
            if t >= 2:
                dve.wait_ge(n_mm, t - 1)
            for g in range(G):
                dve.wait_ge(a_mm, G * t + g + 1)
                nc.vector.tensor_tensor(at[:, t % 2, g, :].rearrange("p (j q) -> p j q", q=P), m.ps[:, g, :].rearrange("p (j q) -> p j q", q=P),
                                        causal[:, :].unsqueeze(1).broadcast_to([P, 4, P]), ALU.mult).then_inc(a_set, 1)

        def mask_state(t):
            dve.wait_ge(s_mm, t + 1)
            nc.vector.tensor_tensor(state[:, (t + 1) % 2, :, 0:VW], m.ps[:, 7, 0:H * VW].rearrange("p (h e) -> p h e", e=VW),
                                    hmask[:, :].unsqueeze(2).broadcast_to([P, H, VW]), ALU.mult).then_inc(s_set, 1)

        def divide(t):
            dve.wait_ge(n_turned, t + 1)
            turned = m.ps[:, 5, :].rearrange("p (h e) -> p h e", e=PAD)
            nc.vector.tensor_scalar(den[:, t % 2, :], turned[:, :, HD], 1e-6, None, ALU.add).then_inc(den_set, 1)
            dve.wait_ge(den_set, t + 1)
            nc.vector.reciprocal(rec[:, t % 2, :], den[:, t % 2, :]).then_inc(rec_set, 1)
            dve.wait_ge(rec_set, t + 1)
            nc.vector.tensor_tensor(o[:, t, :].rearrange("p (h e) -> p h e", e=HD), turned[:, :, 0:HD],
                                    rec[:, t % 2, :].unsqueeze(2).broadcast_to([P, H, HD]), ALU.mult).then_inc(o_set, 1)

        def add(c):
            dve.wait_ge(y_mm, c + 1)
            dve.wait_ge(m.biased, norm.biased_value(c))
            xs = m.x[:, c * TPC:(c + 1) * TPC, :]
            nc.vector.tensor_tensor(xs, m.ps[:, 6, :].rearrange("p (j d) -> p j d", d=D), xs, ALU.add).then_inc(x_done, 1)
            after(dve, c)

        for t in range(NT + 2):
            if t < NT:
                mask_scores(t)
            if t < NT:
                mask_state(t)
            if t >= 2:
                divide(t - 2)
            if t >= TPC + 3 and (t - 3) % TPC == 0:
                add((t - 3) // TPC - 1)
        add(NC - 1)

    return Part([(x_done, norm.done(c)) for c in range(NC)], tensor=tensor, vector=vector, scalar=scalar, gpsimd=gpsimd, sync=sync,
                before_norm={"gpsimd": clear}, bias="L2_attn_bo", early=False)


def l2_ffn(nc, m, A, sem, sb, norm):
    E, F = 8, 256
    FT = F // P
    W1, W2, B1, WN = 0, F, 2 * F, 2 * F + 2
    EPS = 1e-6
    UNROLL = 2 * NC
    w = sb("l2f_w", [P, 2, WN])
    gate = sb("l2f_gate", [P, E])
    lnb = sb("l2f_lnb", [E, D])
    b2 = sb("l2f_b2", [P, E, D])
    lng = sb("l2f_lng", [P, E, D])
    hT = sb("l2f_hT", [P, 2, FT, CH])
    xb = sb("l2f_xb", [P, 4, TPC, D])
    z = sb("l2f_z", [P, 4, TPC, D])
    st, mv = sb("l2f_st", [P, 4, TPC, 6]), sb("l2f_mv", [P, 4, TPC, 2])
    ve, rs, nb = (sb(f"l2f_{n}", [P, 4, TPC]) for n in ("ve", "rs", "nb"))
    r = router_buffers(sb, "l2f", E)
    wte, w2nd = sb("l2f_wte", [P, NT, E]), sb("l2f_w2nd", [P, NT, E])
    wteT = sb("l2f_wteT", [E, T])
    gap, z12 = sb("l2f_gap", [P, NT]), sb("l2f_z12", [P, NT])

    small_in, small_all = norm.loads(4)
    w_in = [sem(f"l2f_w_in{u}") for u in range(2)]
    logits, step, exps = sem("l2f_logits"), sem("l2f_step"), sem("l2f_exps")
    wte_set, turned, wteT_set, lnb_mm, lnb_added = (sem(f"l2f_{n}") for n in ("wte_set", "turned", "wteT_set", "lnb_mm", "lnb_added"))
    up_done, h_done, o_done = sem("l2f_up_done"), sem("l2f_h_done"), sem("l2f_o_done")
    xb_done, z_done, stats, var, vareps = (sem(f"l2f_{n}") for n in ("xb_done", "z_done", "stats", "var", "vareps"))
    rstd, nb_done, zn_done, zg_done, y_done = (sem(f"l2f_{n}") for n in ("rstd", "nb_done", "zn_done", "zg_done", "y_done"))

    def load(sp, slot, e):
        return sp.dma_start(w[:, slot, :], A["L2_ffn_w"][bass.ds(e, 1), :, :].rearrange("e p n -> p (e n)")).then_inc(w_in[slot], 16)

    def sync(sp):
        sp.dma_start(gate[:, :], A["L2_ffn_gate_w"]).then_inc(small_in, 16)
        sp.dma_start(lnb[:, :], A["L2_ffn_ln_b"]).then_inc(small_in, 16)
        sp.dma_start(b2[:, :, :].rearrange("p e d -> p (e d)"), A["L2_ffn_b2"].broadcast_to([P, E * D])).then_inc(small_in, 16)
        sp.dma_start(lng[:, :, :].rearrange("p e d -> p (e d)"), A["L2_ffn_ln_g"].broadcast_to([P, E * D])).then_inc(small_in, 16)
        load(sp, 0, 0)
        load(sp, 1, 1)
        with sp.Fori(1, E // 2) as i:
            for u in range(2):
                sp.wait_ge(o_done, i * UNROLL + NC * (u - 1))
                load(sp, u, i * 2 + u)

    def pipelined(eng, body, tail):
        for k in range(UNROLL):
            body(0, k, k)
        with eng.Fori(1, E // 2) as i:
            for k in range(UNROLL):
                body(i, k, None)
        tail()

    def tensor(pe):
        pe.wait_ge(small_in, small_all)
        for t in range(NT):
            if t % TPC == 0:
                norm.wait_xnT(pe, t // TPC)
            mm = nc.tensor.matmul(m.ps[:, 5, t * E:(t + 1) * E], m.xnT[:, t * P:(t + 1) * P], gate[:, :], start=True, stop=True)
        mm.then_inc(logits, 1)

        def up(i, k, n):
            u, c = k // NC % 2, k % NC
            if c == 0:
                pe.wait_ge(w_in[u], (i + 1) * 16)
            if n is None or n >= 2:
                pe.wait_ge(h_done, i * (FT * UNROLL) + FT * (k - 1))
            for f in range(FT):
                mm = nc.tensor.matmul(m.ps[:, 2 * (k % 2) + f, :], w[:, u, W1 + f * P:W1 + (f + 1) * P], m.xnT[:, c * CH:(c + 1) * CH],
                                      start=True, stop=True)
                mm.then_inc(up_done, 1)

        def down(i, k, n):
            u = k // NC % 2
            if n is None or n >= 2:
                pe.wait_ge(z_done, i * UNROLL + (k - 1))
            pe.wait_ge(h_done, i * (FT * UNROLL) + FT * (k + 1))
            for f in range(FT):
                for j in range(TPC):
                    mm = nc.tensor.matmul(m.ps[:, 4 + k % 2, j * P:(j + 1) * P], hT[:, k % 2, f, j * P:(j + 1) * P],
                                          w[:, u, W2 + f * P:W2 + (f + 1) * P], start=(f == 0 and j == 0),
                                          stop=(f == FT - 1), skip_group_check=True)
            mm.then_inc(o_done, 1)

        def norm_biases():
            pe.wait_ge(wte_set, 1)
            for c in range(NC):
                if c >= 2:
                    pe.wait_ge(wteT_set, c - 1)
                for j in range(TPC):
                    mm = nc.tensor.transpose(m.ps[0:E, 6 + c % 2, j * P:(j + 1) * P], wte[:, c * TPC + j, :], m.ident[:, :])
                mm.then_inc(turned, 1)
            for c in range(NC):
                pe.wait_ge(wteT_set, NC)
                if c >= 2:
                    pe.wait_ge(lnb_added, c - 1)
                for j in range(TPC):
                    t = c * TPC + j
                    mm = nc.tensor.matmul(m.ps[:, 6 + c % 2, j * P:(j + 1) * P], wteT[:, t * P:(t + 1) * P], lnb[:, :], start=True, stop=True)
                mm.then_inc(lnb_mm, 1)

        pe.wait_ge(step, 1)

        def body(i, k, n):
            up(i, k, n)
            if n is None or n >= 1:
                down(i, k - 1, None if n is None else n - 1)
            if n == 1:
                norm_biases()

        pipelined(pe, body, lambda: down(E // 2 - 1, UNROLL - 1, None))

    def scalar(act):
        norm.copy_xnT(act, NC - 1)
        act.wait_ge(step, 2 + RANK_STEPS)
        nc.scalar.activation(gap[:, :], gap[:, :], ACT.Exp).then_inc(exps, 1)
        def turn(c):
            act.wait_ge(turned, c + 1)
            nc.scalar.activation(wteT[:, c * CH:(c + 1) * CH], m.ps[0:E, 6 + c % 2, :], ACT.Copy).then_inc(wteT_set, 1)

        def zn(i, k):
            act.wait_ge(nb_done, i * UNROLL + (k + 1))
            for j in range(TPC):
                ins = nc.scalar.activation(z[:, k % 4, j, :], z[:, k % 4, j, :], ACT.Identity, bias=nb[:, k % 4, j:j + 1],
                                           scale=rs[:, k % 4, j:j + 1])
            ins.then_inc(zn_done, 1)

        def body(i, k, n):
            u = k // NC % 2
            for f in range(FT):
                act.wait_ge(up_done, i * (FT * UNROLL) + (FT * k + f + 1))
                nc.scalar.activation(hT[:, k % 2, f, :], m.ps[:, 2 * (k % 2) + f, :], ACT.Gelu,
                                     bias=w[:, u, B1 + f:B1 + f + 1]).then_inc(h_done, 1)
            if n == 1:
                for c in range(NC):
                    turn(c)
            if n is None or n >= 3:
                zn(i, k - 3)

        def tail():
            for k in range(UNROLL - 3, UNROLL):
                zn(E // 2 - 1, k)

        pipelined(act, body, tail)

    def gpsimd(pool):
        pool.wait_ge(small_in, small_all)

        def expert(i, k):
            return bass.ds(i * 2 + k // NC, 1)

        def add_b2(i, k):
            c = k % NC
            nc.gpsimd.tensor_tensor(xb[:, k % 4, :, :], m.xn[:, c * TPC:(c + 1) * TPC, :],
                                    b2[:, expert(i, k), :].broadcast_to([P, TPC, D]), ALU.add).then_inc(xb_done, 1)

        def times_g(i, k):
            nc.gpsimd.tensor_tensor(z[:, k % 4, :, :], z[:, k % 4, :, :], lng[:, expert(i, k), :].broadcast_to([P, TPC, D]),
                                    ALU.mult).then_inc(zg_done, 1)

        def body(i, k, n, last=False):
            if n is None or n >= 2:
                pool.wait_ge(zn_done, i * UNROLL + (k - 1))
            pool.wait_ge(vareps, i * UNROLL + (k + 1))
            nc.gpsimd.tensor_tensor(rs[:, k % 4, :], ve[:, k % 4, :], m.power[:, 0:TPC], ALU.pow).then_inc(rstd, 1)
            if not last:
                add_b2(i, k + 2)
            if n is None or n >= 2:
                times_g(i, k - 2)

        pool.wait_ge(m.ln_xn, norm.value(NC - 1))
        add_b2(0, 0)
        add_b2(0, 1)
        for k in range(UNROLL):
            body(0, k, k)
        with pool.Fori(1, E // 2 - 1) as i:
            for k in range(UNROLL):
                body(i, k, None)
        last = E // 2 - 1
        for k in range(UNROLL):
            body(last, k, None, last=(k >= UNROLL - 2))
        for k in (UNROLL - 2, UNROLL - 1):
            pool.wait_ge(zn_done, last * UNROLL + (k + 1))
            times_g(last, k)

    def vector(dve, after):
        count = [0]

        def then(ins):
            ins.then_inc(step, 1)
            count[0] += 1
            dve.wait_ge(step, count[0])

        L = r.logits
        dve.wait_ge(logits, 1)
        then(nc.vector.tensor_copy(L[:, :, :].rearrange("p t e -> p (t e)"), m.ps[:, 5, 0:NT * E]))
        ranks(nc, then, m, r, E)
        bc = lambda a: a.unsqueeze(2).broadcast_to([P, NT, E])
        then(nc.vector.tensor_tensor(gap[:, :], r.second[:, :], r.first[:, :], ALU.subtract))
        assert count[0] == 2 + RANK_STEPS
        dve.wait_ge(exps, 1)
        then(nc.vector.tensor_scalar(z12[:, :], gap[:, :], 1.0, None, ALU.add))
        then(nc.vector.reciprocal(z12[:, :], z12[:, :]))
        then(nc.vector.tensor_tensor(gap[:, :], gap[:, :], z12[:, :], ALU.mult))
        then(nc.vector.tensor_tensor(w2nd[:, :, :], r.is_second[:, :, :], bc(gap[:, :]), ALU.mult))
        then(nc.vector.tensor_tensor(wte[:, :, :], r.is_first[:, :, :], bc(z12[:, :]), ALU.mult))
        nc.vector.tensor_tensor(wte[:, :, :], wte[:, :, :], w2nd[:, :, :], ALU.add).then_inc(wte_set, 1)
        dve.wait_ge(wte_set, 1)

        def sums(i, k, n):
            if n is None or n >= 4:
                dve.wait_ge(y_done, i * UNROLL + (k - 3))
            dve.wait_ge(o_done, i * UNROLL + (k + 1))
            dve.wait_ge(xb_done, i * UNROLL + (k + 1))
            nc.vector.tensor_tensor(z[:, k % 4, :, :], m.ps[:, 4 + k % 2, :].rearrange("p (j d) -> p j d", d=D), xb[:, k % 4, :, :],
                                    ALU.add).then_inc(z_done, 1)
            dve.wait_ge(z_done, i * UNROLL + (k + 1))
            for j in range(TPC):
                ins = nc.vector.bn_stats(st[:, k % 4, j, :], z[:, k % 4, j, :])
            ins.then_inc(stats, 1)

        def variance(i, k):
            if isinstance(i, int) and i * UNROLL + k == 0:
                dve.wait_ge(stats, 1)
            for j in range(TPC):
                ins = nc.vector.bn_aggr(mv[:, k % 4, j, :], st[:, k % 4, j, :])
            ins.then_inc(var, 1)
            dve.wait_ge(var, i * UNROLL + (k + 1))
            nc.vector.tensor_scalar(ve[:, k % 4, :], mv[:, k % 4, :, 1], EPS, None, ALU.add).then_inc(vareps, 1)

        def shift(i, k, last=False):
            if not last:
                dve.wait_ge(stats, i * UNROLL + (k + 2))
            dve.wait_ge(rstd, i * UNROLL + (k + 1))
            nc.vector.scalar_tensor_tensor(out=nb[:, k % 4, :], in0=mv[:, k % 4, :, 0], scalar=-1.0, in1=rs[:, k % 4, :],
                                           op0=ALU.mult, op1=ALU.mult).then_inc(nb_done, 1)

        def add(i, k, n):
            c = k % NC
            dve.wait_ge(zg_done, i * UNROLL + (k + 1))
            if n is None or n >= NC:
                dve.wait_ge(y_done, i * UNROLL + (k - NC + 1))
            for j in range(TPC):
                t = c * TPC + j
                ins = nc.vector.scalar_tensor_tensor(out=m.x[:, t, :], in0=z[:, k % 4, j, :], scalar=wte[:, t, bass.ds(i * 2 + k // NC, 1)],
                                                     in1=m.x[:, t, :], op0=ALU.mult, op1=ALU.add)
            ins.then_inc(y_done, 1)

        def add_biases(c):
            dve.wait_ge(lnb_mm, c + 1)
            xs = m.x[:, c * TPC:(c + 1) * TPC, :]
            nc.vector.tensor_tensor(xs, m.ps[:, 6 + c % 2, :].rearrange("p (j d) -> p j d", d=D), xs, ALU.add).then_inc(lnb_added, 1)

        def body(i, k, n):
            sums(i, k, n)
            if n == 0:
                for c in range(NC):
                    add_biases(c)
                dve.wait_ge(lnb_added, NC)
            if n is None or n >= 1:
                shift(i, k - 1)
            variance(i, k)
            if n is None or n >= 3:
                add(i, k - 3, None if n is None else n - 3)

        def tail():
            shift(E // 2 - 1, UNROLL - 1, last=True)
            after(dve, 0)
            for k in range(UNROLL - 3, UNROLL):
                add(E // 2 - 1, k, None)
                after(dve, k % NC)

        pipelined(dve, body, tail)

    total = E * NC
    return Part([(y_done, total - NC + c + 1) for c in range(NC)], tensor=tensor, vector=vector, scalar=scalar, gpsimd=gpsimd, sync=sync,
                early=False)


def l3_attn(nc, m, A, sem, sb, norm):
    HEADS, DH, R = 16, 64, 64
    RT = HEADS * R // P
    TB = S // P
    SW = D + 1
    sb("rounded", [P, ROUNDED])
    m.rounded.fresh()
    x_high, x_low = norm.split_xnT()
    wrf_high, wrf_low = (m.rounded.take(n, [P, 2 * RT, P], F32R) for n in ("wrf_high", "wrf_low"))
    wqk = sb("l3a_wqk", [P, 2 * RT, D])
    rf = sb("l3a_rf", [P, RT, P])
    wv = sb("l3a_wv", [P, RT, P])
    wout = sb("l3a_wout", [P, RT, D])
    rows = sb("l3a_rows", [P, 2])
    sel = m.rounded.take("l3a_sel", [P, RT, P], F32R)
    rn = m.rounded.take("l3a_rn", [P, 2, CH], F32R)
    kmask = sb("l3a_kmask", [P, RT, 32])
    blocks = sb("l3a_blocks", [P, P])
    phik = sb("l3a_phik", [P, 2, RT * P])
    s_sb = sb("l3a_s", [P, B, RT, SW])
    sT = sb("l3a_sT", [P, RT, P])
    kv = sb("l3a_kv", [P, RT, P])
    mix = sb("l3a_mix", [P, B, RT, D])
    knorm = sb("l3a_knorm", [P, B, RT, 32])
    phiq = sb("l3a_phiq", [P, 2, RT, CH])
    sel_in = phiq[:, 0, 0:2, :].rearrange("p a (b c) -> p (a b) c", c=P)
    recip, high, rest = (phik[:, n // 2, n % 2 * CH:(n % 2 + 1) * CH] for n in range(3))

    norm.banks = (7,)
    w_in, w_all = norm.loads(8)
    prod = sem("l3a_prod")
    prod_high, prod_low = sem("l3a_prod_high"), sem("l3a_prod_low")
    k_mm = sem("l3a_k_mm")
    k_relu = sem("l3a_k_relu")
    s_mm = sem("l3a_s_mm")
    s_out = sem("l3a_s_out")
    knorm_set = sem("l3a_knorm_set")
    sel_set = knorm_set
    tail_mm = sem("l3a_tail_mm")
    tail_act, tail_dve = sem("l3a_tail_act"), sem("l3a_tail_dve")
    q_mm = sem("l3a_q_mm")
    q_relu = sem("l3a_q_relu")
    n_mm = sem("l3a_n_mm")
    n_eps = sem("l3a_n_eps")
    n_rec = sem("l3a_n_rec")
    N_REC = 7
    b_mm = sem("l3a_b_mm")
    scaled = sem("l3a_scaled")
    o_mm = sem("l3a_o_mm")
    x_done = m.x_done

    def sync(sp):
        for dst, name in ((wqk, "L3_attn_wqkT"), (rf, "L3_attn_rf"), (wv, "L3_attn_wv"), (wout, "L3_attn_wout"),
                          (sel_in, "L3_attn_sel"), (kmask, "L3_attn_kmask")):
            sp.dma_start(dst[:, :, :], A[name]).then_inc(w_in, 16)
        sp.dma_start(blocks[:, :], A["L3_attn_blocks"]).then_inc(w_in, 16)
        sp.dma_start(rows[:, :], A["L3_attn_rows"]).then_inc(w_in, 16)

    def before_norm(pe):
        pe.wait_ge(w_in, w_all)
        for t in range(2 * RT):
            mm = nc.tensor.matmul(m.ps[:, t // 4, t % 4 * P:(t % 4 + 1) * P], wqk[:, t, :], rf[:, t % RT, :],
                                  start=True, stop=True)
            if t % 4 == 3:
                mm.then_inc(prod, 1)

    def tensor(pe):
        def product(out, a, b):
            nc.tensor.matmul(out, a[0], b[0], start=True, stop=False)
            nc.tensor.matmul(out, a[0], b[1], start=False, stop=False)
            return nc.tensor.matmul(out, a[1], b[0], start=False, stop=True)

        def phi_k(n):
            b, t = divmod(n, TB)
            norm.wait_xnT(pe, n // TPC)
            pe.wait_ge(prod_low, 4)
            if n >= 2:
                pe.wait_ge(k_relu, n - 1)
            for h in range(2):
                mm = product(m.ps[:, 2 * (n % 2) + h, :], (x_high[:, n * P:(n + 1) * P], x_low[:, n * P:(n + 1) * P]),
                             (wrf_high[:, RT + 4 * h:RT + 4 * h + 4, :], wrf_low[:, RT + 4 * h:RT + 4 * h + 4, :]))
            mm.then_inc(k_mm, 1)

        def phi_k_xn(n):
            b, t = divmod(n, TB)
            pe.wait_ge(k_relu, n + 1)
            if t == 0 and b:
                pe.wait_ge(s_out, b)
            for r in range(RT):
                mm = nc.tensor.matmul(m.ps[:, 4 + r // 3, r % 3 * SW:(r % 3 + 1) * SW], phik[:, n % 2, r * P:(r + 1) * P],
                                      m.xn1[:, n, :], start=(t == 0 and r % 3 == 0), stop=(t == TB - 1), skip_group_check=True)
            if t == TB - 1:
                mm.then_inc(s_mm, 1)

        for n in range(NT):
            phi_k(n)
            if n:
                phi_k_xn(n - 1)
        phi_k_xn(NT - 1)

        def turn_s(b):
            pe.wait_ge(s_out, B)
            if b:
                pe.wait_ge(tail_act, 2 * b)
            for r in range(RT):
                mm = nc.tensor.transpose(m.ps[:, 6 + r // 4, r % 4 * P:(r % 4 + 1) * P], s_sb[:, b, r, 0:D], m.ident[:, :])
            mm.then_inc(tail_mm, 1)

        def s_wv(b):
            pe.wait_ge(tail_act, 2 * b + 1)
            for r in range(RT):
                mm = nc.tensor.matmul(m.ps[:, 6 + r // 4, r % 4 * P:(r % 4 + 1) * P], wv[:, r, :], sT[:, r, :], start=True, stop=True)
            mm.then_inc(tail_mm, 1)

        def kv_wout(b):
            pe.wait_ge(tail_dve, b + 1)
            for r in range(RT):
                mm = nc.tensor.matmul(m.ps[:, 6 + r // 4, r % 4 * P:(r % 4 + 1) * P], kv[:, r, :], wout[:, r, :], start=True, stop=True)
            mm.then_inc(tail_mm, 1)

        def phi_q(c, rs):
            for r in rs:
                n = c * RT + r
                if n >= 2:
                    pe.wait_ge(q_relu, n - 1)
                product(m.ps[:, n % 2, :], (wrf_high[:, r, :], wrf_low[:, r, :]),
                        (x_high[:, c * CH:(c + 1) * CH], x_low[:, c * CH:(c + 1) * CH])).then_inc(q_mm, 1)

        def normaliser(c):
            b = c // (NC // B)
            pe.wait_ge(knorm_set, b + 2)
            pe.wait_ge(q_relu, c * RT + RT)
            if c:
                pe.wait_ge(n_eps, c)
            for r in range(RT):
                g = 32 * (r % 4)
                mm = nc.tensor.matmul(m.ps[g:g + 32, 2, :], knorm[:, b, r, :], phiq[:, c % 2, r, :], start=(r < 4), stop=(r >= 4),
                                      skip_group_check=True)
            mm.then_inc(n_mm, 1)

        def spread(c, r):
            n = c * RT + r
            if n >= 2:
                pe.wait_ge(scaled, n - 1)
            nc.tensor.matmul(m.ps[:, 3 + n % 2, :], sel[:, r, :], rn[:, c % 2, :], start=True, stop=True).then_inc(b_mm, 1)

        def outputs(c, r):
            b = c // (NC // B)
            pe.wait_ge(scaled, c * RT + r + 1)
            for j in range(TPC):
                mm = nc.tensor.matmul(m.ps[:, 5, j * P:(j + 1) * P], phiq[:, c % 2, r, j * P:(j + 1) * P], mix[:, b, r, :],
                                      start=(r == 0 and j == 0), stop=(r == RT - 1), skip_group_check=True)
            if r == RT - 1:
                mm.then_inc(o_mm, 1)

        def finish(c):
            pe.wait_ge(n_rec, N_REC * (c + 1))
            pe.wait_ge(tail_act, 2 * (c // (NC // B)) + 2)
            if c:
                pe.wait_ge(x_done, norm.done(c - 1))
            for r in range(RT + 1):
                if r < RT:
                    spread(c, r)
                if r:
                    outputs(c, r - 1)

        for c in range(NC + 1):
            tail = c < NC and c % (NC // B) == 0
            b = c // (NC // B)
            if c < NC:
                phi_q(c, range(0, 2))
                if c == 0:
                    turn_s(0)
                if tail:
                    s_wv(b)
                phi_q(c, range(2, 4))
                if tail:
                    kv_wout(b)
                phi_q(c, range(4, RT))
                normaliser(c)
            if c == 1:
                turn_s(1)
            if c:
                finish(c - 1)

    def scalar(act):
        for n in range(4):
            act.wait_ge(prod, n + 1)
            nc.scalar.activation(wrf_high[:, 4 * n:4 * n + 4, :].rearrange("p a b -> p (a b)"), m.ps[:, n, :], ACT.Copy).then_inc(prod_high, 1)

    def low_products(dve):
        dve.wait_ge(w_in, w_all)
        nc.vector.tensor_copy(sel[:, :, :], sel_in).then_inc(sel_set, 1)
        for n in range(4):
            dve.wait_ge(prod_high, n + 1)
            flat = lambda a: a[:, 4 * n:4 * n + 4, :].rearrange("p a b -> p (a b)")
            nc.vector.tensor_tensor(flat(wrf_low), m.ps[:, n, :], flat(wrf_high).bitcast(F32), ALU.subtract).then_inc(prod_low, 1)

    def scalar_main(act):
        def s_copy(b):
            act.wait_ge(s_mm, b + 1)
            for q in range(3):
                k = min(3, RT - 3 * q)
                cp = nc.scalar.activation(s_sb[:, b, 3 * q:3 * q + k, :].rearrange("p a b -> p (a b)"), m.ps[:, 4 + q, 0:k * SW], ACT.Copy)
            cp.then_inc(s_out, 1)

        for n in range(NT):
            norm.copy_xnT(act, n // TPC + 1)
            act.wait_ge(k_mm, n + 1)
            nc.scalar.activation(phik[:, n % 2, :].rearrange("p (a b) -> p a b", a=2), m.ps[:, 2 * (n % 2):2 * (n % 2) + 2, :],
                                 ACT.Relu).then_inc(k_relu, 1)
            if n == TB:
                s_copy(0)
        s_copy(1)

        def relu_q(c, rs):
            for r in rs:
                n = c * RT + r
                act.wait_ge(q_mm, n + 1)
                nc.scalar.activation(phiq[:, c % 2, r, :], m.ps[:, n % 2, :], ACT.Relu).then_inc(q_relu, 1)

        def tail_copy(b, dst, n):
            act.wait_ge(tail_mm, n)
            nc.scalar.activation(dst.rearrange("p (a b) c -> p a (b c)", a=2), m.ps[:, 6:8, :], ACT.Copy).then_inc(tail_act, 1)

        act.wait_ge(sel_set, 1)
        for c in range(NC):
            b = c // (NC // B)
            relu_q(c, range(0, 2))
            if c == 0:
                tail_copy(0, sT[:, :, :], 1)
            relu_q(c, range(2, 4))
            relu_q(c, range(4, RT))
            if c % (NC // B) == 0:
                tail_copy(b, mix[:, b, :, :], 3 * b + 3)
            if c == 1:
                tail_copy(1, sT[:, :, :], 4)

    def vector(dve, after):
        def knorms(b):
            dve.wait_ge(s_out, b + 1)
            nc.vector.tensor_tensor(knorm[:, b, :, :], kmask[:, :, :], s_sb[:, b, :, D:SW].broadcast_to([P, RT, 32]), ALU.mult).then_inc(knorm_set, 1)

        def mask_kv(b):
            dve.wait_ge(tail_mm, 3 * b + 2)
            nc.vector.tensor_tensor(kv[:, :, :], m.ps[:, 6:8, :].rearrange("p a (b c) -> p (a b) c", c=P),
                                    blocks[:, :].unsqueeze(1).broadcast_to([P, RT, P]), ALU.mult).then_inc(tail_dve, 1)

        def reciprocals(c, step):
            done = N_REC * c
            if step == 0:
                dve.wait_ge(n_mm, c + 1)
                nc.vector.tensor_scalar(recip, m.ps[:, 2, :], 1e-6, None, ALU.add).then_inc(n_eps, 1)
            elif step <= 4:
                if step == 1:
                    dve.wait_ge(n_eps, c + 1)
                piece = recip[:, (step - 1) * P:step * P]
                nc.vector.reciprocal(piece, piece).then_inc(n_rec, 1)
            elif step == 5:
                dve.wait_ge(n_rec, done + 4)
                nc.vector.tensor_copy(high.bitcast(F32R), recip).then_inc(n_rec, 1)
                nc.vector.tensor_scalar(rest, recip, rows[:, 1:2], None, ALU.mult).then_inc(n_rec, 1)
            elif step == 6:
                if c >= 2:
                    dve.wait_ge(b_mm, (c - 1) * RT)
                dve.wait_ge(n_rec, done + 6)
                nc.vector.scalar_tensor_tensor(out=rn[:, c % 2, :], in0=high, scalar=rows[:, 0:1], in1=rest, op0=ALU.mult, op1=ALU.add).then_inc(n_rec, 1)

        def scale(c, r):
            n = c * RT + r
            dve.wait_ge(b_mm, n + 1)
            nc.vector.tensor_tensor(phiq[:, c % 2, r, :], m.ps[:, 3 + n % 2, :], phiq[:, c % 2, r, :], ALU.mult).then_inc(scaled, 1)

        def add(c):
            dve.wait_ge(o_mm, c + 1)
            dve.wait_ge(m.biased, norm.biased_value(c))
            xs = m.x[:, c * TPC:(c + 1) * TPC, :]
            nc.vector.tensor_tensor(xs, m.ps[:, 5, :].rearrange("p (j d) -> p j d", d=D), xs, ALU.add).then_inc(x_done, 1)
            after(dve, c)

        knorms(0)
        knorms(1)
        for c in range(NC + 1):
            if c < NC and c % (NC // B) == 0:
                mask_kv(c // (NC // B))
            for r in range(RT):
                if c:
                    scale(c - 1, r)
                if c < NC:
                    reciprocals(c, r)
            if c:
                add(c - 1)

    return Part([(x_done, norm.done(c)) for c in range(NC)], tensor=tensor, vector=vector, scalar=scalar_main, sync=sync,
                before_norm={"tensor": before_norm, "scalar": scalar, "vector": low_products}, bias="L3_attn_b_out")


def l3_ffn(nc, m, w_dram, gate_dram, sem, sb, sb_late, norm):
    E, F = 8, 512
    FT = F // P
    W1, W3, W2 = 0, F, 2 * F
    w = sb("l3f_w", [P, 2, 3 * F])
    gate = sb("l3f_gate", [P, E])
    m.rounded.fresh()
    w_high, w_low = m.rounded.take("l3f_w_high", [P, 2, W2], F32R), m.rounded.take("l3f_w_low", [P, 2, W2], F32R)
    sg = sb("l3f_sg", [P, 2, CH])
    hT = sb_late("l3f_hT", [P, 2, FT, CH])
    x_high, x_low = norm.split_xnT()
    r = router_buffers(sb, "l3f", E)
    keep1, keep2, e1, e2, wte = (sb(f"l3f_{n}", [P, NT, E]) for n in ("keep1", "keep2", "e1", "e2", "wte"))
    d1, d2, fac = (sb(f"l3f_{n}", [P, NT, E]) for n in ("d1", "d2", "fac"))
    z1, z2 = sb("l3f_z1", [P, NT]), sb("l3f_z2", [P, NT])

    gate_in, gate_all = norm.loads(1)
    w_in = [sem(f"l3f_w_in{u}") for u in range(2)]
    logits = sem("l3f_logits")
    step = sem("l3f_step")
    shifted = sem("l3f_shifted")
    w_high_set, w_low_set = sem("l3f_w_high_set"), sem("l3f_w_low_set")
    PIECES = 4
    SPLIT_AT = {(1, 2): 0, (2, 0): 1, (2, 2): 2, (3, 0): 3}
    exps = sem("l3f_exps")
    up_done = sem("l3f_up_done")
    sg_done = sem("l3f_sg_done")
    h_done = sem("l3f_h_done")
    down_done = sem("l3f_down_done")
    y_done = sem("l3f_y_done")

    def load(sp, slot, e):
        return sp.dma_start(w[:, slot, :], w_dram[bass.ds(e, 1), :, :].rearrange("e p n -> p (e n)")).then_inc(w_in[slot], 16)

    def sync(sp):
        sp.dma_start(gate[:, :], gate_dram).then_inc(gate_in, 16)
        load(sp, 0, 0)
        load(sp, 1, 1)
        with sp.Fori(1, E // 2) as i:
            for u in range(2):
                sp.wait_ge(down_done, i * (2 * NC) + NC * (u - 1))
                load(sp, u, i * 2 + u)

    def tensor(pe):
        pe.wait_ge(gate_in, gate_all)
        for t in range(NT):
            if t % TPC == 0:
                norm.wait_xnT(pe, t // TPC)
            last = nc.tensor.matmul(m.ps[:, 5, t * E:(t + 1) * E], m.xnT[:, t * P:(t + 1) * P], gate[:, :], start=True, stop=True)
        last.then_inc(logits, 1)

        def product(out, u, col, cs):
            nc.tensor.matmul(out, w_high[:, u, col:col + P], x_high[:, cs], start=True, stop=False)
            nc.tensor.matmul(out, w_high[:, u, col:col + P], x_low[:, cs], start=False, stop=False)
            return nc.tensor.matmul(out, w_low[:, u, col:col + P], x_high[:, cs], start=False, stop=True)

        def gates(i, k):
            u, c = divmod(k, NC)
            if c == 0:
                pe.wait_ge(w_high_set, i * (2 * PIECES) + (u + 1) * PIECES)
                pe.wait_ge(w_low_set, i * (2 * PIECES) + (u + 1) * PIECES)
            for f in range(FT):
                s = k * FT + f
                pair = 2 * (s % 2)
                cs = slice(c * CH, (c + 1) * CH)
                pe.wait_ge(h_done, i * (2 * NC * FT) + (s + 1))
                product(m.ps[:, pair, :], u, W1 + f * P, cs).then_inc(up_done, 1)
                product(m.ps[:, pair + 1, :], u, W3 + f * P, cs).then_inc(up_done, 1)

        def down(i, k):
            u, c = divmod(k, NC)
            pe.wait_ge(y_done, i * (2 * NC) + (k + 1))
            for f in range(FT):
                pe.wait_ge(h_done, i * (2 * NC * FT) + (k * FT + f + 1 + 2))
                for j in range(TPC):
                    last = nc.tensor.matmul(m.ps[:, 4 + k % 2, j * P:(j + 1) * P], hT[:, k % 2, f, j * P:(j + 1) * P],
                                            w[:, u, W2 + f * P:W2 + (f + 1) * P], start=(f == 0 and j == 0),
                                            stop=(f == FT - 1), skip_group_check=True)
            last.then_inc(down_done, 1)

        pe.wait_ge(step, 1)
        with pe.Fori(0, E // 2) as i:
            for k in range(2 * NC):
                gates(i, k)
                if k:
                    down(i, k - 1)
            down(i, 2 * NC - 1)

    def columns(q):
        return slice(q * (W2 // PIECES), (q + 1) * (W2 // PIECES))

    def scalar(act):
        def split_w(u, q):
            nc.scalar.activation(w_high[:, u, columns(q)], w[:, u, columns(q)], ACT.Copy).then_inc(w_high_set, 1)

        norm.copy_xnT(act, NC - 2)
        act.wait_ge(w_in[0], 16)
        act.wait_ge(*norm.before.ready[NC - 1])
        for q in range(PIECES):
            split_w(0, q)
        norm.copy_xnT(act, NC - 1)

        def routing_exps():
            act.wait_ge(shifted, 1)
            nc.scalar.activation(e1[:, :, :], d1[:, :, :], ACT.Exp, scale=-1.0).then_inc(exps, 1)
            act.wait_ge(shifted, 2)
            nc.scalar.activation(e2[:, :, :], d2[:, :, :], ACT.Exp, scale=-1.0).then_inc(exps, 1)

        def body(i, last, first=False):
            for s in range(2 * NC * FT):
                k, f = divmod(s, FT)
                u, c = divmod(k, NC)
                if (c, f) in SPLIT_AT and not (last and u == 1):
                    if SPLIT_AT[c, f] == 0:
                        act.wait_ge(w_in[1 - u], (i + u + 1) * 16)
                    split_w(1 - u, SPLIT_AT[c, f])
                act.wait_ge(up_done, i * (4 * NC * FT) + (2 * s + 1))
                nc.scalar.activation(sg[:, s % 2, :], m.ps[:, 2 * (s % 2), :], ACT.Silu).then_inc(sg_done, 1)
                if first and s == 4:
                    routing_exps()

        body(0, False, first=True)
        with act.Fori(1, E // 2 - 1) as i:
            body(i, False)
        body(E // 2 - 1, True)

    def vector(dve, after):
        dve.sem_inc(h_done, 2)
        dve.sem_inc(y_done, 2)

        def low(out, whole, high, done):
            return nc.vector.tensor_tensor(out, whole, high.bitcast(F32), ALU.subtract).then_inc(done, 1)

        for q in range(PIECES):
            dve.wait_ge(w_high_set, q + 1)
            low(w_low[:, 0, columns(q)], w[:, 0, columns(q)], w_high[:, 0, columns(q)], w_low_set)
        dve.wait_ge(logits, 1)
        n = [0]

        def then(ins):
            ins.then_inc(step, 1)
            n[0] += 1
            dve.wait_ge(step, n[0])

        L = r.logits
        then(nc.vector.tensor_copy(L[:, :, :].rearrange("p t e -> p (t e)"), m.ps[:, 5, 0:NT * E]))
        bc = lambda a: a.unsqueeze(2).broadcast_to([P, NT, E])

        def distances():
            nc.vector.tensor_tensor(d1[:, :, :], bc(r.first[:, :]), L[:, :, :], ALU.subtract).then_inc(shifted, 1)
            then(nc.vector.tensor_tensor(d2[:, :, :], bc(r.second[:, :]), L[:, :, :], ALU.subtract))
            nc.vector.tensor_scalar(d2[:, :, :], d2[:, :, :], 0.0, None, ALU.max).then_inc(shifted, 1)

        def masks():
            then(nc.vector.scalar_tensor_tensor(out=fac[:, :, :], in0=L[:, :, :], scalar=-1.0, in1=L[:, :, :], op0=ALU.mult, op1=ALU.max))
            then(nc.vector.tensor_tensor(keep1[:, :, :], fac[:, :, :], bc(r.first[:, :]), ALU.max))
            then(nc.vector.tensor_tensor(keep2[:, :, :], fac[:, :, :], bc(r.second[:, :]), ALU.max))
            then(nc.vector.scalar_tensor_tensor(out=keep1[:, :, :], in0=keep1[:, :, :], scalar=0.02, in1=d1[:, :, :], op0=ALU.mult, op1=ALU.is_ge))
            then(nc.vector.scalar_tensor_tensor(out=keep2[:, :, :], in0=keep2[:, :, :], scalar=0.02, in1=d2[:, :, :], op0=ALU.mult, op1=ALU.is_ge))
            then(nc.vector.tensor_tensor(keep2[:, :, :], keep2[:, :, :], r.is_first[:, :, :], ALU.is_gt))

        def weights():
            dve.wait_ge(exps, 2)
            then(nc.vector.tensor_tensor(keep1[:, :, :], keep1[:, :, :], e1[:, :, :], ALU.mult))
            then(nc.vector.tensor_tensor(keep2[:, :, :], keep2[:, :, :], e2[:, :, :], ALU.mult))
            then(nc.vector.tensor_reduce(z1[:, :], keep1[:, :, :], AX.X, ALU.add))
            then(nc.vector.tensor_reduce(z2[:, :], keep2[:, :, :], AX.X, ALU.add))
            then(nc.vector.reciprocal(z1[:, :], z1[:, :]))
            then(nc.vector.reciprocal(z2[:, :], z2[:, :]))
            then(nc.vector.tensor_tensor(wte[:, :, :], r.is_first[:, :, :], bc(z1[:, :]), ALU.mult))
            then(nc.vector.tensor_tensor(e2[:, :, :], r.is_second[:, :, :], bc(z2[:, :]), ALU.mult))
            then(nc.vector.tensor_tensor(wte[:, :, :], wte[:, :, :], e2[:, :, :], ALU.add))

        def routing_beside(s):
            if s == 0:
                first_rank(nc, then, m, r, E)
            elif s == 1:
                second_rank(nc, then, m, r, E)
            elif s == 2:
                distances()
            elif s == 3:
                masks()
            elif s == 6:
                weights()

        def outputs(i, k):
            u, c = divmod(k, NC)
            dve.wait_ge(down_done, i * (2 * NC) + (k + 1))
            dve.wait_ge(y_done, i * (2 * NC) + (k + 1))
            for j in range(TPC):
                t = c * TPC + j
                last = nc.vector.scalar_tensor_tensor(out=m.x[:, t, :], in0=m.ps[:, 4 + k % 2, j * P:(j + 1) * P],
                                                      scalar=wte[:, t, bass.ds(i * 2 + u, 1)], in1=m.x[:, t, :],
                                                      op0=ALU.mult, op1=ALU.add)
            last.then_inc(y_done, 1)

        def body(i, last, first=False):
            for k in range(2 * NC):
                u, c = divmod(k, NC)
                for f in range(FT):
                    s = k * FT + f
                    dve.wait_ge(up_done, i * (4 * NC * FT) + (2 * s + 2))
                    dve.wait_ge(sg_done, i * (2 * NC * FT) + (s + 1))
                    nc.vector.tensor_tensor(hT[:, k % 2, f, :], m.ps[:, 2 * (s % 2) + 1, :], sg[:, s % 2, :],
                                            ALU.mult).then_inc(h_done, 1)
                    if first:
                        routing_beside(s)
                    if (c, f) in SPLIT_AT and not (last and u == 1):
                        q = SPLIT_AT[c, f]
                        dve.wait_ge(w_high_set, i * (2 * PIECES) + ((u + 1) * PIECES + q + 1))
                        low(w_low[:, 1 - u, columns(q)], w[:, 1 - u, columns(q)], w_high[:, 1 - u, columns(q)], w_low_set)
                if k:
                    outputs(i, k - 1)
            outputs(i, 2 * NC - 1)

        body(0, False, first=True)
        with dve.Fori(1, E // 2 - 1) as i:
            body(i, False)
        body(E // 2 - 1, True)

    total = E * NC
    return Part([(y_done, total - NC + c + 1 + 2) for c in range(NC)], tensor=tensor, vector=vector, scalar=scalar, sync=sync)


class Router:
    pass


def router_buffers(sb, name, E):
    r = Router()
    r.logits, r.is_first, r.is_second, r.tmp, r.rest = (
        sb(f"{name}_{n}", [P, NT, E]) for n in ("logits", "is_first", "is_second", "tmp", "rest"))
    r.first, r.second, r.place = (sb(f"{name}_{n}", [P, NT]) for n in ("first", "second", "place"))
    return r


RANK_STEPS = 11


def largest(nc, then, m, r, E, values, value, chosen):
    bc = lambda a: a[:, :].unsqueeze(2).broadcast_to([P, NT, E])
    early_wins = m.descending[:, 0:E].unsqueeze(1).broadcast_to([P, NT, E])
    then(nc.vector.tensor_reduce(value[:, :], values[:, :, :], AX.X, ALU.max))
    then(nc.vector.tensor_tensor(r.tmp[:, :, :], values[:, :, :], bc(value), ALU.is_equal))
    then(nc.vector.tensor_tensor(r.tmp[:, :, :], r.tmp[:, :, :], early_wins, ALU.mult))
    then(nc.vector.tensor_reduce(r.place[:, :], r.tmp[:, :, :], AX.X, ALU.max))
    then(nc.vector.tensor_tensor(chosen[:, :, :], r.tmp[:, :, :], bc(r.place), ALU.is_equal))


def first_rank(nc, then, m, r, E):
    largest(nc, then, m, r, E, r.logits, r.first, r.is_first)
    then(nc.vector.scalar_tensor_tensor(out=r.rest[:, :, :], in0=r.is_first[:, :, :], scalar=-3e38, in1=r.logits[:, :, :], op0=ALU.mult, op1=ALU.add))


def second_rank(nc, then, m, r, E):
    largest(nc, then, m, r, E, r.rest, r.second, r.is_second)


def ranks(nc, then, m, r, E):
    first_rank(nc, then, m, r, E)
    second_rank(nc, then, m, r, E)


BIASES = ["L0_attn_b_proj", "L1_ffn_base_b", "L2_attn_bo", "L3_attn_b_out"]


ROUNDED = 10240
ARENAS = [32900, 13200]


class Memory:
    pass


class Arena:

    def __init__(self, area):
        self.area, self.used = area, 0

    def fresh(self):
        self.used = 0
        return self.take

    def take(self, name, shape, dt=F32):
        size = {F32: 4, F32R: 4, I32: 4, BF16: 2}[dt]
        words = (int(np.prod(shape[1:])) * size + 31) // 32 * 8
        assert self.used + words <= self.area.shape[1], (name, self.used, words)
        flat = self.area[0:shape[0], self.used:self.used + words]
        self.used += words
        flat = (flat if dt in (F32, F32R) else flat.bitcast(dt))[:, 0:int(np.prod(shape[1:]))]
        if len(shape) == 2:
            return flat
        names = "abcd"[:len(shape) - 1]
        return flat.rearrange(f"p ({' '.join(names)}) -> p {' '.join(names)}", **{n: k for n, k in zip(names[1:], shape[2:])})


def program(nc, A, out, parts):
    with ExitStack() as ctx:
        def sb(name, shape, dt=F32):
            return ctx.enter_context(nc.sbuf_tensor(name, shape, dt))

        def sem(name):
            return ctx.enter_context(nc.semaphore(name))

        m = Memory()
        m.ps = ctx.enter_context(nc.psum_tensor("ps", [P, 8, 512], F32))
        m.psf = m.ps[:, :, :].rearrange("p b n -> p (b n)")
        m.ps7b = m.ps[:, 7, :].bitcast(BF16)
        m.x = sb("x", [P, NT, D])
        m.xn1 = sb("xn1", [P, NT, D + 1])
        m.xn = m.xn1[:, :, 0:D]
        m.xnT = sb("xnT", [P, T])
        m.ident = sb("ident", [P, P])
        m.descending = sb("descending", [P, 8])
        m.stats = sb("stats", [P, NT, 6])
        m.meanvar = sb("meanvar", [P, NT, 2])
        m.vareps = sb("vareps", [P, NT])
        m.rstd = sb("rstd", [P, NT])
        m.power = sb("power", [P, NT])
        m.bias = sb("bias", [P, len(BIASES), D])
        m.consts_in, m.x_in, m.set_up, m.out_written = sem("consts_in"), [sem(f"x_in{c}") for c in range(NC)], sem("set_up"), sem("out_written")
        m.ln_var, m.ln_rstd = sem("ln_var"), sem("ln_rstd")
        m.loaded, m.loads = [sem("loaded0"), sem("loaded1")], [0, 0]
        m.splits, m.x_high_set, m.x_low_set = 0, sem("x_high_set"), sem("x_low_set")
        m.biased, m.x_done = sem("biased"), sem("x_done")
        m.ln_xn, m.ln_turned, m.ln_xnT = sem("ln_xn"), sem("ln_turned"), sem("ln_xnT")

        m.bias_of = {name: m.bias[:, n, :] for n, name in enumerate(BIASES)}
        arenas = [None, Arena(sb("arena1", [P, ARENAS[1]]))]
        with nc.sbuf_tensor("arena0", [P, ARENAS[0]], F32) as area0:
            arenas[0] = Arena(area0)
        m.rounded = Arena(sb("rounded", [P, ROUNDED], F32R))
        start = Part([(m.x_in[c], 16) for c in range(NC)])
        built = []
        for k, name in enumerate(parts):
            sb = arenas[k % 2].fresh()
            norm = Norm(nc, m, k, built[-1][1] if built else start, sum(p.bias is not None for _, p in built),
                        sum(p.ready[0][0] is m.x_done for _, p in built))
            if name == "l0_attn":
                part = l0_attn(nc, m, A, sem, sb, norm)
            if name == "l0_ffn":
                part = l0_ffn(nc, m, A, sem, sb, norm)
            if name == "l1_attn":
                part = l1_attn(nc, m, A, sem, sb, norm)
            if name == "l1_ffn":
                part = l1_ffn(nc, m, A, sem, sb, norm)
            if name == "l2_attn":
                part = l2_attn(nc, m, A, sem, sb, norm)
            if name == "l2_ffn":
                part = l2_ffn(nc, m, A, sem, sb, norm)
            if name == "l3_attn":
                part = l3_attn(nc, m, A, sem, sb, norm)
            if name == "l3_ffn":
                late = arenas[0].fresh()
                late("rounded", [P, ROUNDED])
                part = l3_ffn(nc, m, A["L3_ffn_w"], A["L3_ffn_gate_w"], sem, sb, late, norm)
            built.append((norm, part))
        last = built[-1][1]
        following = {id(a): b for (a, _), (b, _) in zip(built, built[1:])}

        def after(norm):
            return following[id(norm)].after if id(norm) in following else lambda dve, c: None

        block = ctx.enter_context(nc.Block())

        @block.sync
        def _(sp):
            x_view = A["x"].rearrange("(t p) d -> p t d", p=P)
            for c in range(NC):
                sp.dma_start(m.x[:, c * TPC:(c + 1) * TPC, :], x_view[:, c * TPC:(c + 1) * TPC, :]).then_inc(m.x_in[c], 16)
            sp.dma_start(m.ident[:, :], A["ident"]).then_inc(m.consts_in, 16)
            sp.dma_start(m.descending[:, :], A["descending"]).then_inc(m.consts_in, 16)
            for n, name in enumerate(BIASES):
                m_bias = m.bias[:, n, :]
                sp.dma_start(m_bias, A[name].broadcast_to([P, D])).then_inc(m.consts_in, 16)
            for k, (norm, part) in enumerate(built):
                if k >= 2:
                    for c in range(NC):
                        sp.wait_ge(*built[k - 2][1].ready[c])
                if part.sync:
                    part.sync(sp)
            out_view = out.rearrange("(t p) d -> p t d", p=P)
            for c in range(NC):
                sp.wait_ge(*last.ready[c])
                sp.dma_start(out_view[:, c * TPC:(c + 1) * TPC, :], m.x[:, c * TPC:(c + 1) * TPC, :]).then_inc(m.out_written, 16)
            sp.wait_ge(m.out_written, 16 * NC)

        @block.tensor
        def _(pe):
            for norm, part in built:
                if "tensor" in part.before_norm:
                    part.before_norm["tensor"](pe)
                if part.tensor:
                    part.tensor(pe)

        @block.vector
        def _(dve):
            for norm, part in built:
                if "vector" in part.before_norm:
                    part.before_norm["vector"](dve)
                norm.vector(dve)
                part.vector(dve, after(norm))

        @block.scalar
        def _(act):
            for norm, part in built:
                if "scalar" in part.before_norm:
                    part.before_norm["scalar"](act)
                part.scalar(act)

        @block.gpsimd
        def _(pool):
            nc.gpsimd.memset(m.xn1[:, :, D:D + 1], 1.0).then_inc(m.set_up, 1)
            nc.gpsimd.memset(m.power[:, :], -0.5).then_inc(m.set_up, 1)
            for norm, part in built:
                if "gpsimd" in part.before_norm:
                    part.before_norm["gpsimd"](pool)
                norm.gpsimd(pool, m.bias_of.get(part.bias))
                if part.gpsimd:
                    part.gpsimd(pool)


ALL_PARTS = ["l0_attn", "l0_ffn", "l1_attn", "l1_ffn", "l2_attn", "l2_ffn", "l3_attn", "l3_ffn"]


def layouts(a):
    c = np.ascontiguousarray
    f = {}
    f["x"] = c(a["L0_attn_hidden_states"]).reshape(T, D)
    f["ident"] = np.eye(P, dtype=np.float32)
    f["descending"] = c(np.broadcast_to(np.arange(8, 0, -1, dtype=np.float32), (P, 8)))
    up = lambda w: np.asarray(w).transpose(0, 2, 1)
    down = lambda w: np.asarray(w).transpose(0, 2, 1).reshape(w.shape[0], -1, P, D).transpose(0, 2, 1, 3).reshape(w.shape[0], P, -1)
    f["L3_ffn_w"] = c(np.concatenate([up(a["L3_ffn_w1"]), up(a["L3_ffn_w3"]), down(a["L3_ffn_w2"])], axis=2))
    f["L3_ffn_gate_w"] = c(np.asarray(a["L3_ffn_gate_w"]).T)
    w = np.asarray(a["L0_attn_w_attn"])
    mix = lambda a: a.reshape(*a.shape[:-1], 16, 8).swapaxes(-1, -2).reshape(a.shape)
    w = w.reshape(D, 3, D)
    f["L0_attn_w"] = c(np.concatenate([mix(w[:, :2]), w[:, 2:]], axis=1))
    f["L0_attn_wo"] = c(a["L0_attn_w_proj"])
    f["L0_attn_bqk"] = c(mix(np.asarray(a["L0_attn_b_attn"])[:256].reshape(2, D)).T)
    f["L0_attn_bv"] = c(np.asarray(a["L0_attn_b_attn"])[256:]).reshape(1, D)
    away = np.arange(P)[:, None] - np.arange(S)[None, :] + S - P
    f["L0_attn_weight"] = np.where(away >= 0, 1 / (np.maximum(away, 0) + 1.0), 0).astype(np.float32)
    bf16 = np.dtype("bfloat16")
    f["L0_attn_ident"] = np.eye(P).astype(bf16)
    before = np.where(np.tril(np.ones((P, P)), -1) > 0, -1e30, 0)
    f["L0_attn_before"] = c(np.stack([before, before.T], axis=1)).astype(bf16)
    tail = np.zeros((P - 48, S))
    tail[48:51] = 1
    f["L0_attn_tail"] = tail.astype(bf16)
    f["L0_ffn_w"] = c(np.stack([np.asarray(a["L0_ffn_w_gate"]).T, np.asarray(a["L0_ffn_w_up"]).T,
                                np.asarray(a["L0_ffn_w_down"]).T.reshape(3, P, D).transpose(1, 0, 2).reshape(P, 384)], axis=1))
    f["L1_attn_wqk"] = c(np.stack([a["L1_attn_Wq"], a["L1_attn_Wk"]], axis=1))
    f["L1_attn_wkvT"] = c(np.stack([np.asarray(a["L1_attn_Wk"]).T, np.asarray(a["L1_attn_Wv"]).T], axis=1))
    f["L1_attn_bcol"] = c(np.stack([a["L1_attn_bq"], a["L1_attn_bk"]], axis=1))
    f["L1_attn_bkv"] = c(np.stack([a["L1_attn_bk"], a["L1_attn_bv"]], axis=0))
    theta = (np.float32(1) / (np.power(np.float32(10000.0), np.arange(0, 8, 2, dtype=np.float32)) / np.float32(8))).astype(np.float32)
    theta = np.concatenate([theta, theta])
    turn = np.zeros((8, 8), np.float32)
    for j in range(8):
        turn[j, j] += np.cos(theta[j])
        turn[(j + 4) % 8, j] += np.sin(theta[j]) * (-1 if j < 4 else 1)
    f["L1_attn_rope"] = np.kron(np.eye(16, dtype=np.float32), turn)
    ra, rbm = np.asarray(a["L1_ffn_routed_A"]), np.asarray(a["L1_ffn_routed_B"])
    f["L1_ffn_wa"] = c(np.concatenate([ra.reshape(96, D), a["L1_ffn_shared_A"], a["L1_ffn_router_W"]], axis=0).T)
    f["L1_ffn_wb"] = c(np.concatenate([rbm.transpose(0, 2, 1).reshape(96, D), np.asarray(a["L1_ffn_shared_B"]).T], axis=0))
    f["L1_ffn_base"] = c(np.asarray(a["L1_ffn_base_W"]).T)
    f["L1_ffn_rb"] = c(a["L1_ffn_router_b"]).reshape(1, 6)
    f["causal"] = np.triu(np.ones((P, P), np.float32))
    f["hmask"] = np.kron(np.eye(16, dtype=np.float32), np.ones((8, 1), np.float32))
    f["L2_attn_w"] = c(np.stack([np.asarray(a[f"L2_attn_W{n}"]).T for n in "qkv"], axis=1))
    f["L2_attn_wo"] = c(np.asarray(a["L2_attn_Wo"]).T)
    f["L2_attn_bqk"] = c(np.stack([a["L2_attn_bq"], a["L2_attn_bk"]], axis=1))
    f["L2_attn_bv"] = c(a["L2_attn_bv"]).reshape(1, D)
    b1 = np.asarray(a["L2_ffn_b1"]).reshape(8, 2, P).transpose(0, 2, 1)
    f["L2_ffn_w"] = c(np.concatenate([np.asarray(a["L2_ffn_w1"]), down(np.asarray(a["L2_ffn_w2"]).transpose(0, 2, 1)), b1], axis=2))
    f["L2_ffn_gate_w"] = c(a["L2_ffn_gate_w"])
    f["L2_ffn_ln_b"] = c(a["L2_ffn_ln_b"])
    f["L2_ffn_b2"] = c(a["L2_ffn_b2"]).reshape(1, -1)
    f["L2_ffn_ln_g"] = c(a["L2_ffn_ln_g"]).reshape(1, -1)
    w = np.asarray(a["L3_attn_W_qkv"])
    f["L3_attn_wqkT"] = c(w[:, :2048].T.reshape(16, P, D).transpose(1, 0, 2))
    rf = np.zeros((8, 2, 64, 2, 64), np.float32)
    for h in range(2):
        rf[:, h, :, h, :] = np.asarray(a["L3_attn_RF"])[h::2]
    f["L3_attn_rf"] = c(rf.reshape(8, P, P).transpose(1, 0, 2))
    f["L3_attn_wv"] = c(w[:, 2048:].reshape(D, 8, P))
    f["L3_attn_wout"] = c(np.asarray(a["L3_attn_W_out"]).reshape(8, P, D).transpose(1, 0, 2))
    sel, kmask = np.zeros((P, 8, P), np.float32), np.zeros((P, 8, 32), np.float32)
    for r in range(8):
        for h in range(2):
            row = 2 * (r // 4) + h
            sel[[32 * (r % 4) + row, 32 * (r % 4) + row + 4], r, 64 * h:64 * h + 64] = 1
            kmask[64 * h:64 * h + 64, r, [row, row + 4]] = 1
    rows = np.zeros((4, 32, 2), np.float32)
    rows[:, 0:4, 0], rows[:, 4:8, 0], rows[:, 4:8, 1] = 1, -1, 1
    f["L3_attn_rows"] = c(rows.reshape(P, 2))
    f["L3_attn_sel"], f["L3_attn_kmask"] = sel, kmask
    f["L3_attn_blocks"] = np.kron(np.eye(2, dtype=np.float32), np.ones((64, 64), np.float32))
    for name in BIASES:
        f[name] = c(a[name]).reshape(1, D)
    return f


def kernel(**inputs):
    import concourse.bacc as bacc
    from concourse.bass_utils import run_bass_kernel_spmd

    nc = bacc.Bacc("TRN2", target_bir_lowering=False, num_devices=1)
    arrays = {f"in_{k}": v for k, v in layouts(inputs).items()}
    A = {k[3:]: nc.dram_tensor(k, v.shape, mybir.dt.from_np(v.dtype), kind="ExternalInput").ap() for k, v in arrays.items()}
    A["scratch"] = nc.dram_tensor("scratch", (2, 6, P, T), BF16, kind="Internal").ap()
    out = nc.dram_tensor("out", (T, D), F32, kind="ExternalOutput").ap()
    program(nc, A, out, ALL_PARTS)
    r = run_bass_kernel_spmd(nc, [arrays], core_ids=[0])
    return r.results[0]["out"].reshape(B, S, D)
```
